# Optimizing a Trainium2 kernel written in Bass

```python
import numpy as np
import jax
import jax.numpy as jnp

def _softmax(x, axis=-1):
    return jax.nn.softmax(x, axis=axis)

def _gelu(x):
    return jax.nn.gelu(x, approximate=True)

def _silu(x):
    return jax.nn.silu(x)

def _sigmoid(x):
    return jax.nn.sigmoid(x)

def _layernorm(x, axis=-1, eps=1e-05):
    m = jnp.mean(x, axis=axis, keepdims=True)
    v = jnp.var(x, axis=axis, keepdims=True)
    return (x - m) / jnp.sqrt(v + eps)

def _scatter_add(tgt, idx, src, axis=0):
    return tgt.at[idx].add(src)

def _segment_sum(src, seg, n):
    return jax.ops.segment_sum(src, seg, n)
kernel_name = 'mk_hybrid_d1_jaxref_r4_1cff83'

def setup_inputs(seed: int=0):
    np.random.seed(seed)
    _w = jnp.asarray

    def _L0_attn_a_setup():
        import jax, jax.numpy as jnp
        import numpy as np
        N_HEADS = 16
        EPS = 1e-06

        def _phi(x):
            return jax.nn.softplus(x) + EPS

        def _reference_tuple_inner(x, Wq, Wk, Wv, Wo):
            B, T, D = x.shape
            H = N_HEADS
            dh = D // H

            def proj(W):
                y = jnp.einsum('btd,ed->bte', x, W)
                return y.reshape(B, T, H, dh).transpose(1, 0, 2, 3)
            q = proj(Wq)
            k = proj(Wk)
            v = proj(Wv)
            qf = _phi(q)
            kf = _phi(k)
            kv0 = jnp.zeros((B, H, dh, dh), dtype=x.dtype)
            z0 = jnp.zeros((B, H, dh), dtype=x.dtype)

            def step(carry, inp):
                kv, z = carry
                qt, kt, vt = inp
                kv = kv + jnp.einsum('bhd,bhe->bhde', kt, vt)
                z = z + kt
                num = jnp.einsum('bhd,bhde->bhe', qt, kv)
                den = jnp.einsum('bhd,bhd->bh', qt, z) + EPS
                return ((kv, z), num / den[..., None])
            (kv_acc, z_acc), out_t = jax.lax.scan(step, (kv0, z0), (qf, kf, v))
            out = out_t.transpose(1, 0, 2, 3).reshape(B, T, D)
            out = jnp.einsum('btd,ed->bte', out, Wo)
            return (out, kv_acc, z_acc)
        key = jax.random.key(seed)
        ks = jax.random.split(key, 5)
        D = 256
        s = 1.0 / np.sqrt(D)
        x = jax.random.normal(ks[0], (4, 1024, D), dtype=jnp.float32)
        Wq = jax.random.normal(ks[1], (D, D), dtype=jnp.float32) * s
        Wk = jax.random.normal(ks[2], (D, D), dtype=jnp.float32) * s
        Wv = jax.random.normal(ks[3], (D, D), dtype=jnp.float32) * s
        Wo = jax.random.normal(ks[4], (D, D), dtype=jnp.float32) * s
        return {'x': x, 'Wq': Wq, 'Wk': Wk, 'Wv': Wv, 'Wo': Wo}
    _L0_attn_a_in = _L0_attn_a_setup()

    def _L0_attn_b_setup():
        import jax, jax.numpy as jnp
        import numpy as np
        B, S, D, H = (2, 512, 256, 16)
        HD = D // H
        MAX_BIAS = 8.0

        def _alibi_bias(T, Sk, dtype):
            slopes = (2.0 ** (-MAX_BIAS / H)) ** jnp.arange(1, H + 1, dtype=dtype)
            qpos = jnp.arange(T)[:, None]
            kpos = jnp.arange(Sk)[None, :]
            rel = -jnp.abs(kpos - qpos).astype(dtype)
            return slopes[:, None, None] * rel[None]
        key = jax.random.key(seed)
        ks = jax.random.split(key, 5)
        sc = 1.0 / np.sqrt(D)
        return {'x': jax.random.normal(ks[0], (B, S, D), jnp.float32), 'Wq': jax.random.normal(ks[1], (D, D), jnp.float32) * sc, 'bq': jnp.zeros((D,), jnp.float32), 'Wk': jax.random.normal(ks[2], (D, D), jnp.float32) * sc, 'bk': jnp.zeros((D,), jnp.float32), 'Wv': jax.random.normal(ks[3], (D, D), jnp.float32) * sc, 'bv': jnp.zeros((D,), jnp.float32), 'Wo': jax.random.normal(ks[4], (D, D), jnp.float32) * sc, 'bo': jnp.zeros((D,), jnp.float32)}
    _L0_attn_b_in = _L0_attn_b_setup()

    def _L0_ffn_setup():
        import jax, jax.numpy as jnp
        import numpy as np
        from jax import lax
        T, B, I, M, O = (64, 64, 256, 256, 256)

        def _xavier(key, shape):
            fan_out, fan_in = shape
            limit = float(np.sqrt(6.0 / (fan_in + fan_out)))
            return jax.random.uniform(key, shape, jnp.float32, -limit, limit)
        key = jax.random.key(seed)
        ks = jax.random.split(key, 9)
        x = jax.random.normal(ks[0], (T, B, I), jnp.float32)
        return {'x': x, 'wf': _xavier(ks[1], (M, I)), 'uf': _xavier(ks[2], (M, M)), 'bf': jnp.zeros((M,), jnp.float32), 'wi': _xavier(ks[3], (M, I)), 'ui': _xavier(ks[4], (M, M)), 'bi': jnp.zeros((M,), jnp.float32), 'wc': _xavier(ks[5], (M, I)), 'uc': _xavier(ks[6], (M, M)), 'bc': jnp.zeros((M,), jnp.float32), 'wo': _xavier(ks[7], (O, I)), 'uo': _xavier(ks[8], (O, M)), 'bo': jnp.zeros((O,), jnp.float32), 'in_c': jnp.zeros((M,), jnp.float32)}
    _L0_ffn_in = _L0_ffn_setup()
    _d = {'L0_attn_a_x': _L0_attn_a_in['x'], 'L0_attn_a_Wq': _L0_attn_a_in['Wq'], 'L0_attn_a_Wk': _L0_attn_a_in['Wk'], 'L0_attn_a_Wv': _L0_attn_a_in['Wv'], 'L0_attn_a_Wo': _L0_attn_a_in['Wo'], 'L0_attn_b_Wq': _L0_attn_b_in['Wq'], 'L0_attn_b_bq': _L0_attn_b_in['bq'], 'L0_attn_b_Wk': _L0_attn_b_in['Wk'], 'L0_attn_b_bk': _L0_attn_b_in['bk'], 'L0_attn_b_Wv': _L0_attn_b_in['Wv'], 'L0_attn_b_bv': _L0_attn_b_in['bv'], 'L0_attn_b_Wo': _L0_attn_b_in['Wo'], 'L0_attn_b_bo': _L0_attn_b_in['bo'], 'L0_ffn_wf': _L0_ffn_in['wf'], 'L0_ffn_uf': _L0_ffn_in['uf'], 'L0_ffn_bf': _L0_ffn_in['bf'], 'L0_ffn_wi': _L0_ffn_in['wi'], 'L0_ffn_ui': _L0_ffn_in['ui'], 'L0_ffn_bi': _L0_ffn_in['bi'], 'L0_ffn_wc': _L0_ffn_in['wc'], 'L0_ffn_uc': _L0_ffn_in['uc'], 'L0_ffn_bc': _L0_ffn_in['bc'], 'L0_ffn_wo': _L0_ffn_in['wo'], 'L0_ffn_uo': _L0_ffn_in['uo'], 'L0_ffn_bo': _L0_ffn_in['bo'], 'L0_ffn_in_c': _L0_ffn_in['in_c']}
    _x0 = _d['L0_attn_a_x']
    _d['L0_attn_a_x'] = jax.random.normal(jax.random.fold_in(jax.random.key(seed), 1), (8, 1024, 256), dtype=_x0.dtype)
    del _x0
    return _d

def reference(L0_attn_a_x, L0_attn_a_Wq, L0_attn_a_Wk, L0_attn_a_Wv, L0_attn_a_Wo, L0_attn_b_Wq, L0_attn_b_bq, L0_attn_b_Wk, L0_attn_b_bk, L0_attn_b_Wv, L0_attn_b_bv, L0_attn_b_Wo, L0_attn_b_bo, L0_ffn_wf, L0_ffn_uf, L0_ffn_bf, L0_ffn_wi, L0_ffn_ui, L0_ffn_bi, L0_ffn_wc, L0_ffn_uc, L0_ffn_bc, L0_ffn_wo, L0_ffn_uo, L0_ffn_bo, L0_ffn_in_c):

    def _L0_attn_a_ref(x, Wq, Wk, Wv, Wo):
        import jax, jax.numpy as jnp
        import numpy as np
        N_HEADS = 16
        EPS = 1e-06

        def _phi(x):
            return jax.nn.softplus(x) + EPS

        def _reference_tuple_inner(x, Wq, Wk, Wv, Wo):
            B, T, D = x.shape
            H = N_HEADS
            dh = D // H

            def proj(W):
                y = jnp.einsum('btd,ed->bte', x, W)
                return y.reshape(B, T, H, dh).transpose(1, 0, 2, 3)
            q = proj(Wq)
            k = proj(Wk)
            v = proj(Wv)
            qf = _phi(q)
            kf = _phi(k)
            kv0 = jnp.zeros((B, H, dh, dh), dtype=x.dtype)
            z0 = jnp.zeros((B, H, dh), dtype=x.dtype)

            def step(carry, inp):
                kv, z = carry
                qt, kt, vt = inp
                kv = kv + jnp.einsum('bhd,bhe->bhde', kt, vt)
                z = z + kt
                num = jnp.einsum('bhd,bhde->bhe', qt, kv)
                den = jnp.einsum('bhd,bhd->bh', qt, z) + EPS
                return ((kv, z), num / den[..., None])
            (kv_acc, z_acc), out_t = jax.lax.scan(step, (kv0, z0), (qf, kf, v))
            out = out_t.transpose(1, 0, 2, 3).reshape(B, T, D)
            out = jnp.einsum('btd,ed->bte', out, Wo)
            return (out, kv_acc, z_acc)
        return _reference_tuple_inner(x, Wq, Wk, Wv, Wo)[0]

    def _L0_attn_b_ref(x, Wq, bq, Wk, bk, Wv, bv, Wo, bo):
        import jax, jax.numpy as jnp
        import numpy as np
        B, S, D, H = (2, 512, 256, 16)
        HD = D // H
        MAX_BIAS = 8.0

        def _alibi_bias(T, Sk, dtype):
            slopes = (2.0 ** (-MAX_BIAS / H)) ** jnp.arange(1, H + 1, dtype=dtype)
            qpos = jnp.arange(T)[:, None]
            kpos = jnp.arange(Sk)[None, :]
            rel = -jnp.abs(kpos - qpos).astype(dtype)
            return slopes[:, None, None] * rel[None]
        Bb, Ss, Dd = x.shape
        q = (x @ Wq + bq).reshape(Bb, Ss, H, HD)
        k = (x @ Wk + bk).reshape(Bb, Ss, H, HD)
        v = (x @ Wv + bv).reshape(Bb, Ss, H, HD)
        scores = jnp.einsum('bthd,bshd->bhts', q, k) / jnp.sqrt(jnp.asarray(HD, x.dtype))
        alibi = _alibi_bias(Ss, Ss, x.dtype)
        causal = jnp.triu(jnp.ones((Ss, Ss), bool), 1)
        scores = scores + alibi[None]
        scores = jnp.where(causal[None, None], -jnp.inf, scores)
        attn = jax.nn.softmax(scores, axis=-1)
        out = jnp.einsum('bhts,bshd->bthd', attn, v).reshape(Bb, Ss, Dd)
        return out @ Wo + bo

    def _L0_ffn_ref(x, wf, uf, bf, wi, ui, bi, wc, uc, bc, wo, uo, bo, in_c):
        import jax, jax.numpy as jnp
        import numpy as np
        from jax import lax
        T, B, I, M, O = (64, 64, 256, 256, 256)

        def _xavier(key, shape):
            fan_out, fan_in = shape
            limit = float(np.sqrt(6.0 / (fan_in + fan_out)))
            return jax.random.uniform(key, shape, jnp.float32, -limit, limit)
        batch = x.shape[1]
        c0 = jnp.broadcast_to(in_c, (batch, in_c.shape[0]))

        def step(c, xt):
            ft = jax.nn.sigmoid(xt @ wf.T + c @ uf.T + bf)
            it = jax.nn.sigmoid(xt @ wi.T + c @ ui.T + bi)
            gt = jnp.tanh(xt @ wc.T + c @ uc.T + bc)
            c = ft * c + it * gt
            return (c, None)
        c_final, _ = lax.scan(step, c0, x)
        h = jnp.tanh(jnp.einsum('tbi,oi->tbo', x, wo) + c_final @ uo.T + bo)
        return h
    x = L0_attn_a_x
    x = x + _L0_attn_a_ref(_layernorm(x, axis=-1), L0_attn_a_Wq, L0_attn_a_Wk, L0_attn_a_Wv, L0_attn_a_Wo)
    x = x + _L0_ffn_ref(_layernorm(x, axis=-1), L0_ffn_wf, L0_ffn_uf, L0_ffn_bf, L0_ffn_wi, L0_ffn_ui, L0_ffn_bi, L0_ffn_wc, L0_ffn_uc, L0_ffn_bc, L0_ffn_wo, L0_ffn_uo, L0_ffn_bo, L0_ffn_in_c)
    x = x + _L0_attn_b_ref(_layernorm(x, axis=-1), L0_attn_b_Wq, L0_attn_b_bq, L0_attn_b_Wk, L0_attn_b_bk, L0_attn_b_Wv, L0_attn_b_bv, L0_attn_b_Wo, L0_attn_b_bo)
    x = x + _L0_ffn_ref(_layernorm(x, axis=-1), L0_ffn_wf, L0_ffn_uf, L0_ffn_bf, L0_ffn_wi, L0_ffn_ui, L0_ffn_bi, L0_ffn_wc, L0_ffn_uc, L0_ffn_bc, L0_ffn_wo, L0_ffn_uo, L0_ffn_bo, L0_ffn_in_c)
    return x

_drawn_inputs = setup_inputs


def setup_inputs(seed=0):
    import zlib

    import numpy as np

    out = dict(_drawn_inputs(seed))
    spreads = {'L0_attn_b_bq': (0.0, 0.431),
     'L0_attn_b_bk': (0.0, 0.8),
     'L0_attn_b_bv': (0.0, 0.1),
     'L0_attn_b_bo': (0.0, 0.1),
     'L0_ffn_bf': (0.0, 0.541),
     'L0_ffn_bi': (0.0, 0.485),
     'L0_ffn_bc': (0.0, 0.1),
     'L0_ffn_bo': (0.0, 0.1),
     'L0_ffn_in_c': (0.0, 0.748)}
    factors = {'L0_attn_a_Wq': 5.272}
    for name, (base, spread) in spreads.items():
        noise = np.random.default_rng([zlib.crc32(name.encode()), seed]).standard_normal(out[name].shape)
        drawn = base * np.exp(spread * noise) if base else spread * noise
        out[name] = jnp.asarray(drawn.astype(out[name].dtype))
    for name, factor in factors.items():
        out[name] = (out[name] * factor).astype(out[name].dtype)
    return out
```

```python
from contextlib import ExitStack

import concourse.bass as bass
from concourse import mybir

F32 = mybir.dt.float32
BF16 = mybir.dt.bfloat16
I32 = mybir.dt.int32
ALU = mybir.AluOpType
ACT = mybir.ActivationFunctionType
AX = mybir.AxisListType

P = 128
B, T, D = 8, 1024, 256
H = 16
HD = D // H
NT = T // P
KT = D // P
CH = 512
HV = HD + 1
SLOT = 64
ROWS = 3 * HD
QROWS = ROWS + 3
KROWS = ROWS + 6
PAIRS = H // 2
RING = 4
NEG = -1.0e30
LN_EPS, PHI_EPS, DEN_EPS = 1e-5, 1e-6, 1e-6

MAX_UNITS = []
for i in range(NT):
    n = (i + 1) * P
    if n > CH:
        MAX_UNITS.append((i, 0, CH, False))
        MAX_UNITS.append((i, CH, n - CH, True))
    else:
        MAX_UNITS.append((i, 0, n, True))
EXP_UNITS = []
for j in range(NT):
    n = T - j * P
    EXP_UNITS.append((j, j * P, min(n, CH), True))
    if n > CH:
        EXP_UNITS.append((j, j * P + CH, n - CH, False))
P_OFF = [sum(T - j * P for j in range(k)) for k in range(NT)]
P_COLS = sum(T - j * P for j in range(NT))
NU = len(MAX_UNITS)
ND = sum(1 for x in EXP_UNITS if x[3])
assert NU == len(EXP_UNITS)

Q_, K_, V_, O_, WF, UF, WI, UI, WC, UC, WO, UO = range(12)
HALF = (UF, UI, UC, UO)
GATES = ((WF, UF), (WI, UI), (WC, UC))
C_BQ, C_BK, C_BF, C_BI, C_BC, C_IN = (2 * n for n in range(6))
SPLIT = ((0, 0), (0, 1), (1, 0))

PER = {
    1: {"act_step": 8, "dve_step": 69, "g_act": 30, "g_dve": 14, "gate": 12, "gate_used": 4, "head_out": 16, 
        "head_taken": 16, "normed1": 4, "normed2": 4, "pool_step": 14, "qk_raw": 8, "qk_ready": 4, 
        "qkp_ready": 4, "qkp_stored0": 96, "qkp_stored1": 96, "s_full": 128, "s_taken": 128, "sp_log": 4, 
        "split1": 4, "split2": 4, "split_o": 1, "stack0": 128, "stack1": 128, "stack2": 128, "stack3": 128, 
        "state_split": 1, "t_full": 64, "t_taken": 64, "v_in": 4, "x_in": 16, "xr_add": 4, "xr_in": 16, 
        "xr_stored": 16, "xt_act": 6, "xt_dve": 6, "xw_out": 4, "xw_stored0": 32, "xw_stored1": 32},
    2: {"dve_step": 49, "g_act": 30, "g_dve": 14, "gate": 12, "gate_used": 4, "head_out": 16, 
        "head_taken": 16, "max_parts": 16, "max_ready": 16, "max_row": 16, "max_sent0": 128, 
        "max_sent1": 128, "max_turned": 16, "normed1": 4, "normed2": 4, "pool_step": 62, "qk_raw": 8, 
        "qkp_ready": 4, "qkp_stored0": 96, "qkp_stored1": 96, "s_full": 192, "s_taken": 192, "split1": 4, 
        "split2": 4, "split_o": 1, "stack0": 128, "stack1": 128, "stack2": 128, "stack3": 128, 
        "state_split": 1, "t_full": 192, "t_taken": 192, "v_in": 4, "x_in": 16, "xa_stored": 16, 
        "xi_in0": 32, "xi_in1": 32, "xi_sum": 4, "xi_tanh": 4, "xi_used": 4, "xr_add": 4, "xr_bias": 1, 
        "xr_in": 16, "xr_stored": 16, "xt_act": 6, "xt_dve": 6, "xw_out": 4, "xw_stored0": 32, 
        "xw_stored1": 32},
}


class Counts:

    def __init__(self):
        self.seen, self.entry, self.trip, self.per = {}, None, None, None

    def next(self, name, n=1):
        seen = self.seen[name] = self.seen.get(name, 0) + n
        if self.trip is None:
            return seen
        self.used.add(name)
        return self.trip * self.per.get(name, 0) + seen

    def open(self, trip, per):
        self.trip, self.per, self.entry, self.used = trip, per, dict(self.seen), set()

    def close(self, trips):
        for name in sorted(self.used):
            n = self.seen[name] - self.entry.get(name, 0)
            if self.per.get(name) != n:
                print("PER", 1 if self.per is PER[1] else 2, name, n, self.per.get(name))
            self.seen[name] = self.entry.get(name, 0) + trips * n
        self.trip = None


class Ring:

    def __init__(self, depth):
        self.depth, self.ends = depth, []

    def turn(self, name, n=1):
        self.ends.append((name, n))
        return self.ends.pop(0) if len(self.ends) > self.depth else None

    def rest(self):
        ends, self.ends = self.ends, []
        return ends


def mixer_kernel(nc, x, weights, cols, rows, key_rows, masks, out):
    with ExitStack() as ctx:
        def sb(name, shape, dt):
            return ctx.enter_context(nc.sbuf_tensor(name, shape, dt))

        def ps(name, shape, dt):
            return ctx.enter_context(nc.psum_tensor(name, shape, dt))

        sem = {}
        for name in (
            "const_in", "const_ready", "const_stored", "w_in0", "w_in1", "w_split",
            "x_in", "xi_in0", "xi_in1", "xi_sum", "xi_tanh", "xi_used", "xa_stored",
            "normed1", "normed2", "split1", "split2", "split_o",
            "g_act", "g_dve", "xt_act", "xt_dve", "qk_raw", "sp_log", "qk_ready", "v_in",
            "qkp_ready", "qkp_stored0", "qkp_stored1", "stack0", "stack1", "stack2", "stack3",
            "s_full", "s_taken", "t_full", "t_taken", "max_ready", "max_parts", "max_turned",
            "max_row", "max_sent0", "max_sent1", "head_out", "head_taken",
            "xr_in", "xr_bias", "xr_add", "xr_stored", "xw_out", "xw_stored0", "xw_stored1",
            "gate", "gate_used", "state_set", "state_split", "cu",
            "act_step", "dve_step", "pool_step",
            "held_pe", "held_act", "held_dve", "held_pool", "held_sp",
            "fin_in0", "fin_in1", "fin_sum", "fin_tanh", "fin_done", "fin_out0", "fin_out1",
        ):
            sem[name] = ctx.enter_context(nc.semaphore(name))

        q_dram = nc.dram_tensor("q_stack", (H, QROWS, T), BF16, kind="Internal").ap()
        k_dram = nc.dram_tensor("k_stack", (H, KROWS, T), BF16, kind="Internal").ap()
        x1_dram = nc.dram_tensor("x_after_attention", (B, T, D), F32, kind="Internal").ap()
        x2_dram = nc.dram_tensor("x_after_ffn", (B, T, D), F32, kind="Internal").ap()
        xw_dram = nc.dram_tensor("x_times_wo", (B, T, D), F32, kind="Internal").ap()

        W = [sb(f"w_{part}", [P, 12, KT, D], BF16) for part in ("high", "low")]
        XA = sb("x_for_attention", [P, NT, D], F32)
        XR = sb("x_residual", [P, NT, D], F32)
        XN = sb("x_normed", [P, 2, 2 * D], F32)
        XI = sb("ffn_h", [P, 2, 2 * D], F32)
        XW = sb("x_wo_out", [P, 2, 2 * D], F32)
        XS1 = [sb(f"ln1_{part}", [P, NT, D], BF16) for part in ("high", "low")]
        XS2 = [sb(f"o_ln2_{part}", [P, NT, D], BF16) for part in ("high", "low")]
        XT1 = [sb(f"ln1_o_turned_{part}", [P, KT, T], BF16) for part in ("high", "low")]
        XT2 = [sb(f"ln2_turned_{part}", [P, KT, T], BF16) for part in ("high", "low")]
        V = sb("values", [P, NT, H * HV], F32)
        QK = sb("qk_block", [P, 2, T], F32)
        QKP = [sb(f"qk_{part}", [P, 2, T], BF16) for part in ("high", "low")]
        QS = sb("q_stacks", [P, RING, T], BF16)
        KS = sb("k_stacks", [P, RING, T], BF16)
        PR = sb("probs_turned", [P, 2, P_COLS], F32)
        MP = sb("maxima", [P, 2, 2 * NT], F32)
        MD = sb("maxima_rest", [P, NT], F32)
        MB = sb("maxima_parts", [P, 3, NT], BF16)
        MR = sb("maxima_rows", [3 * NT, 2, P], BF16)
        ON = sb("attention_out", [P, NT, D], F32)
        DEN = sb("denominators", [P, NT], F32)
        REC = sb("reciprocals", [P, NT], F32)
        CS = sb("state_doubled", [P, KT, T], F32)
        CP = [sb(f"state_{part}", [P, KT, T], BF16) for part in ("high", "low")]
        TG = sb("gate_tanhs", [P, 3, CH], F32)
        CU = sb("state_part_of_h", [P, NT, D], F32)
        U = CU[:, 0:T // D, :].rearrange("p n d -> p (n d)")
        ST = sb("ln_stats", [P, NT, 6], F32)
        MV = sb("ln_mean_var", [P, NT, 2], F32)
        VE = sb("ln_var_eps", [P, NT], F32)
        NY = sb("ln_newton", [P, NT], F32)
        RS = sb("ln_rstd", [P, NT], F32)
        COL = sb("feature_vectors", [P, 12], F32)
        ROW = sb("row_vectors", [P, 3, D], F32)
        ident = sb("identity", [P, P], BF16)
        mask_t = sb("mask_turned", [P, P], BF16)
        mask_s = sb("mask_scores", [P, CH], F32)
        keep = sb("mask_keep", [P, CH], F32)

        G = [ps(f"general_{n}", [P, CH], F32) for n in range(2)]
        SB = [ps(f"scores_{n}", [P, CH], F32) for n in range(2)]
        TB = [ps(f"turned_scores_{n}", [P, CH], F32) for n in range(2)]
        OB = ps("out_of_head", [P, NT, HV], F32)
        MT = ps("maxima_turned", [P, P], BF16)

        def tokens(t, b):
            return t[b].rearrange("(n p) d -> p n d", p=P)

        def pair(t, c):
            return t[:, 2 * c:2 * c + 2, :].rearrange("p n d -> p (n d)")

        block = ctx.enter_context(nc.Block())

        def run(eng, w, phase, batch):
            batch(0, False)
            with eng.Fori(0, B - 1) as trip:
                w.open(trip, PER[phase])
                batch(trip + 1, True)
                w.close(B - 1)

        @block.sync
        def _(sp):
            held = sem["held_sp"]
            w = Counts()
            xa_used, xr_used, stack_used, xi_used = (Ring(n) for n in (1, 1, RING, 2))
            w_used = Ring(2)

            def load_weights(first, count):
                for r in range(count // 2):
                    old = w_used.turn("w_split")
                    if old:
                        sp.wait_ge(sem[old[0]], w.next(*old))
                        sp.sem_inc(held, 1)
                    for m in range(2):
                        src = weights[first + 2 * r + m].rearrange("(k p) e -> p k e", p=P)
                        dst = QK[:, r % 2, m * KT * D:(m + 1) * KT * D].rearrange("p (k e) -> p k e", k=KT)
                        sp.dma_start(dst, src).then_inc(sem[f"w_in{r % 2}"], 16)

            def load_xa(phase, b):
                old = xa_used.turn("normed1", 4)
                if old:
                    sp.wait_ge(sem[old[0]], w.next(*old))
                    sp.sem_inc(held, 1)
                if phase == 2:
                    old = xa_stored.turn("xa_stored", 16)
                    if old:
                        sp.wait_ge(sem[old[0]], w.next(*old))
                        sp.sem_inc(held, 1)
                sp.dma_start(XA[:, :, :], tokens(x if phase == 1 else x1_dram, b)).then_inc(sem["x_in"], 16)

            def load_xi(b, chunks):
                for c in chunks:
                    old = xi_used.turn("xi_used")
                    if old:
                        sp.wait_ge(sem[old[0]], w.next(*old))
                        sp.sem_inc(held, 1)
                    sp.dma_start(XI[:, c % 2, :].rearrange("p (n d) -> p n d", n=2),
                                 tokens(xw_dram, b)[:, 2 * c:2 * c + 2]).then_inc(sem[f"xi_in{c % 2}"], 16)

            def store_xa(b):
                for old in xi_used.rest():
                    sp.wait_ge(sem[old[0]], w.next(*old))
                    sp.sem_inc(held, 1)
                sp.dma_start(tokens(x2_dram, b), XA[:, :, :]).then_inc(sem["xa_stored"], 16)

            def store_stacks():
                for r in range(4):
                    sp.wait_ge(sem["qkp_ready"], w.next("qkp_ready"))
                    sp.sem_inc(held, 1)
                    dst = (k_dram if r % 2 else q_dram)[8 * (r // 2):8 * (r // 2) + 8]
                    rows_of = ((0, 0), (0, HD), (1, 2 * HD)) if r % 2 else ((0, 0), (1, HD), (0, 2 * HD))
                    for part, at in rows_of:
                        sp.dma_start(dst[:, at:at + HD, :], QKP[part][:, r % 2, :]
                                     ).then_inc(sem[f"qkp_stored{r % 2}"], 16)

            def load_stacks(phase, pairs):
                for r in pairs:
                    if r % 4 == 0:
                        sp.wait_ge(sem["qkp_stored0"], w.next("qkp_stored0", 48))
                        sp.sem_inc(held, 1)
                        sp.wait_ge(sem["qkp_stored1"], w.next("qkp_stored1", 48))
                        sp.sem_inc(held, 1)
                    old = stack_used.turn("head_out", 2)
                    if old:
                        sp.wait_ge(sem[old[0]], w.next(*old))
                        sp.sem_inc(held, 1)
                    nq, nk = (ROWS, ROWS) if phase == 1 else (QROWS, KROWS)
                    for par in range(2):
                        h, at = 2 * r + par, SLOT * par
                        sp.dma_start(QS[at:at + nq, r % RING, :], q_dram[h, 0:nq]
                                     ).then_inc(sem[f"stack{r % RING}"], 16)
                        sp.dma_start(KS[at:at + nk, r % RING, :], k_dram[h, 0:nk]
                                     ).then_inc(sem[f"stack{r % RING}"], 16)

            def store_xw(b):
                for c in range(4):
                    sp.wait_ge(sem["xw_out"], w.next("xw_out"))
                    sp.sem_inc(held, 1)
                    sp.dma_start(tokens(xw_dram, b)[:, 2 * c:2 * c + 2],
                                 XW[:, c % 2, :].rearrange("p (n d) -> p n d", n=2)
                                 ).then_inc(sem[f"xw_stored{c % 2}"], 16)

            def load_xr(phase, b):
                old = xr_used.turn("normed2", 4)
                if old:
                    sp.wait_ge(sem[old[0]], w.next(*old))
                    sp.sem_inc(held, 1)
                old = xr_stored.turn("xr_stored", 16)
                if old:
                    sp.wait_ge(sem[old[0]], w.next(*old))
                    sp.sem_inc(held, 1)
                sp.dma_start(XR[:, :, :], tokens(x if phase == 1 else x2_dram, b)).then_inc(sem["xr_in"], 16)

            def store_xr(b):
                sp.wait_ge(sem["xr_add"], w.next("xr_add", 4))
                sp.sem_inc(held, 1)
                sp.dma_start(tokens(x1_dram, b), XR[:, :, :]).then_inc(sem["xr_stored"], 16)

            xa_stored, xr_stored = Ring(1), Ring(1)

            sp.dma_start(COL[:, :], cols).then_inc(sem["const_in"], 16)
            sp.dma_start(ROW[:, :, :], rows.partition_broadcast(P)).then_inc(sem["const_in"], 16)
            sp.dma_start(mask_s[:, :], masks[:, 0:CH]).then_inc(sem["const_in"], 16)
            sp.dma_start(keep[:, :], masks[:, CH:2 * CH]).then_inc(sem["const_in"], 16)
            sp.dma_start(XN[:, 0, 0:2 * P], masks[:, 2 * CH:2 * CH + 2 * P]).then_inc(sem["const_in"], 16)
            sp.dma_start(U[0:3 * H], key_rows).then_inc(sem["const_in"], 16)
            load_weights(0, 4)
            load_xa(1, 0)
            load_weights(8, 8)
            for old in w_used.rest():
                sp.wait_ge(sem[old[0]], w.next(*old))
                sp.sem_inc(held, 1)
            sp.wait_ge(sem["const_ready"], w.next("const_ready"))
            sp.sem_inc(held, 1)
            sp.dma_start(k_dram[:, ROWS:ROWS + 3, :], QKP[0][0:3 * H, 0, :]).then_inc(sem["const_stored"], 16)
            sp.dma_start(q_dram[:, ROWS:ROWS + 3, :], QKP[1][0:3 * H, 0, :]).then_inc(sem["const_stored"], 16)
            sp.dma_start(k_dram[:, ROWS + 3:ROWS + 6, :], QKP[1][0:3 * H, 1, :]).then_inc(sem["const_stored"], 16)
            sp.wait_ge(sem["const_stored"], w.next("const_stored", 48))
            sp.sem_inc(held, 1)

            for phase in (1, 2):
                if phase == 2:
                    load_weights(4, 4)
                    for old in w_used.rest():
                        sp.wait_ge(sem[old[0]], w.next(*old))
                        sp.sem_inc(held, 1)
                    load_xa(2, 0)
                    load_xi(0, range(4))
                    store_xa(0)

                def batch(b, looped):
                    load_xa(phase, (b + 1) % B)
                    store_stacks()
                    load_stacks(phase, range(4))
                    if looped:
                        store_xw(b - 1)
                    load_xr(phase, b)
                    if phase == 2:
                        load_xi((b + 1) % B, range(2))
                    load_stacks(phase, [4])
                    if phase == 2:
                        load_xi((b + 1) % B, range(2, 4))
                    load_stacks(phase, [5])
                    if phase == 2:
                        store_xa((b + 1) % B)
                    load_stacks(phase, [6, 7])
                    store_xr(b)

                run(sp, w, phase, batch)
                store_xw(B - 1)

            sp.wait_ge(sem["xw_stored0"], w.next("xw_stored0", 16 + 2 * 2 * 16 * B))
            sp.sem_inc(held, 1)
            sp.wait_ge(sem["xw_stored1"], w.next("xw_stored1", 16 + 2 * 2 * 16 * B))
            sp.sem_inc(held, 1)
            for old in xr_stored.rest():
                sp.wait_ge(sem[old[0]], w.next(*old))
                sp.sem_inc(held, 1)
            fin_out = Ring(2)
            for b in range(B):
                old = fin_out.turn(f"fin_out{b % 2}", 16)
                if old:
                    sp.wait_ge(sem[old[0]], w.next(*old))
                    sp.sem_inc(held, 1)
                sp.dma_start(PR[:, b % 2, 0:NT * D].rearrange("p (n d) -> p n d", n=NT), tokens(xw_dram, b)
                             ).then_inc(sem[f"fin_in{b % 2}"], 16)
                sp.dma_start(PR[:, b % 2, NT * D:2 * NT * D].rearrange("p (n d) -> p n d", n=NT),
                             tokens(x1_dram, b)).then_inc(sem[f"fin_in{b % 2}"], 16)
                if b >= 1:
                    sp.wait_ge(sem["fin_done"], w.next("fin_done"))
                    sp.sem_inc(held, 1)
                    sp.dma_start(tokens(out, b - 1),
                                 PR[:, (b - 1) % 2, NT * D:2 * NT * D].rearrange("p (n d) -> p n d", n=NT)
                                 ).then_inc(sem[f"fin_out{(b - 1) % 2}"], 16)
            sp.wait_ge(sem["fin_done"], w.next("fin_done"))
            sp.sem_inc(held, 1)
            sp.dma_start(tokens(out, B - 1),
                         PR[:, (B - 1) % 2, NT * D:2 * NT * D].rearrange("p (n d) -> p n d", n=NT)
                         ).then_inc(sem[f"fin_out{(B - 1) % 2}"], 16)
            for old in fin_out.rest():
                sp.wait_ge(sem[old[0]], w.next(*old))
                sp.sem_inc(held, 1)
            for old in xa_stored.rest():
                sp.wait_ge(sem[old[0]], w.next(*old))
                sp.sem_inc(held, 1)

        @block.tensor
        def _(pe):
            held = sem["held_pe"]
            w = Counts()
            general = Ring(2)
            scores, turned = Ring(2), Ring(2)
            out_bank, mt_bank = Ring(1), Ring(1)
            place = [0, 0, 0]

            def turn(src, engine_sems):
                for part in range(2):
                    for k in range(KT):
                        old = general.turn(("xt_act", "xt_dve")[k])
                        if old:
                            pe.wait_ge(sem[old[0]], w.next(*old))
                        bank = G[place[0] % 2][:, :].bitcast(BF16)
                        place[0] += 1
                        for n in range(NT):
                            mm = pe.transpose(bank[:, n * P:(n + 1) * P], src[part][:, n, k * P:(k + 1) * P],
                                              ident[:, :])
                        mm.then_inc(sem[("g_act", "g_dve")[k]], 1)
                for old in general.rest():
                    pe.wait_ge(sem[old[0]], w.next(*old))
                    pe.sem_inc(held, 1)

            def by_feature(bank, terms, e):
                todo = [(m, k, wp, xp, src, t0) for m, src, t0 in terms for k in range(KT) for wp, xp in SPLIT]
                for n, (m, k, wp, xp, src, t0) in enumerate(todo):
                    mm = pe.matmul(bank[:, :], W[wp][:, m, k, e * P:(e + 1) * P], src[xp][:, k, t0:t0 + CH],
                                   start=(n == 0), stop=(n == len(todo) - 1))
                return mm

            def by_token(bank, m, src, c):
                for n in range(2):
                    t0 = (2 * c + n) * P
                    todo = [(k, xp, wp) for k in range(KT) for xp, wp in SPLIT]
                    for i, (k, xp, wp) in enumerate(todo):
                        mm = pe.matmul(bank[:, n * D:(n + 1) * D], src[xp][:, k, t0:t0 + P], W[wp][:, m, k, :],
                                       start=(i == 0), stop=(i == len(todo) - 1))
                return mm

            def unit(consumer, full, product):
                old = general.turn(consumer)
                if old:
                    pe.wait_ge(sem[old[0]], w.next(*old))
                bank = G[place[0] % 2]
                place[0] += 1
                product(bank).then_inc(sem[full], 1)

            def project():
                for e in range(2):
                    for m in (Q_, K_):
                        for c in range(2):
                            unit("qk_raw", "g_act", lambda bank: by_feature(bank, [(m, XT1, c * CH)], e))
                    for c in (2 * e, 2 * e + 1):
                        unit("v_in", "g_dve", lambda bank: by_token(bank, V_, XT1, c))

            def turn_ln2():
                pe.wait_ge(sem["split2"], w.next("split2", 4))
                pe.sem_inc(held, 1)
                turn(XS2, None)
                for c in range(4):
                    unit("xw_out", "g_act", lambda bank: by_token(bank, WO, XT2, c))

            def gates(group):
                e, c = group % 2, group // 2
                if group == 0:
                    pe.wait_ge(sem["state_split"], w.next("state_split"))
                for wm, um in GATES:
                    unit("gate", "g_act", lambda bank: by_feature(bank, [(wm, XT2, c * CH), (um, CP, c * CH)], e))

            def max_unit(n, u):
                r, par = n // 2, n % 2
                if u == 0 and par == 0:
                    pe.wait_ge(sem[f"stack{r % RING}"], w.next(f"stack{r % RING}", 64))
                old = scores.turn("s_taken")
                if old:
                    pe.wait_ge(sem[old[0]], w.next(*old))
                    pe.sem_inc(held, 1)
                bank = SB[place[1] % 2]
                place[1] += 1
                i, c0, width, diag = MAX_UNITS[u]
                at = SLOT * par
                pe.matmul(bank[:, 0:width], QS[at:at + QROWS, r % RING, i * P:(i + 1) * P],
                          KS[at:at + QROWS, r % RING, c0:c0 + width], start=True, stop=True
                          ).then_inc(sem["s_full"], 1)

            def turn_max(n):
                pe.wait_ge(sem["max_parts"], w.next("max_parts"))
                old = mt_bank.turn("max_row")
                if old:
                    pe.wait_ge(sem[old[0]], w.next(*old))
                    pe.sem_inc(held, 1)
                pe.transpose(MT[0:3 * NT, :], MB[:, :, :].rearrange("p a n -> p (a n)"), ident[:, :]
                             ).then_inc(sem["max_turned"], 1)

            def exp_unit(phase, n, u):
                r, par, at = n // 2, n % 2, SLOT * (n % 2)
                j, c0, width, diag = EXP_UNITS[u]
                rows_used = ROWS if phase == 1 else KROWS
                if u == 0 and phase == 1 and par == 0:
                    pe.wait_ge(sem[f"stack{r % RING}"], w.next(f"stack{r % RING}", 64))
                if u == 0 and phase == 2:
                    pe.wait_ge(sem[f"max_sent{n % 2}"], w.next(f"max_sent{n % 2}", 16))
                if phase == 1 and diag:
                    old = scores.turn("s_taken")
                    if old:
                        pe.wait_ge(sem[old[0]], w.next(*old))
                        pe.sem_inc(held, 1)
                    bank, full = SB[place[1] % 2], "s_full"
                    place[1] += 1
                else:
                    old = turned.turn("t_taken")
                    if old:
                        pe.wait_ge(sem[old[0]], w.next(*old))
                        pe.sem_inc(held, 1)
                    bank, full = TB[place[2] % 2], "t_full"
                    place[2] += 1
                masked = diag and phase == 2
                mm = pe.matmul(bank[:, 0:width], KS[at:at + rows_used, r % RING, j * P:(j + 1) * P],
                               QS[at:at + rows_used, r % RING, c0:c0 + width], start=True, stop=not masked)
                if masked:
                    mm = pe.matmul(bank[:, 0:P], ident[:, :], mask_t[:, :], start=False, stop=True)
                mm.then_inc(sem[full], 1)

            def head_tile(n, i):
                if i == 0:
                    old = out_bank.turn("head_taken")
                    if old:
                        pe.wait_ge(sem[old[0]], w.next(*old))
                for j in range(i + 1):
                    at = P_OFF[j] + (i - j) * P
                    mm = pe.matmul(OB[:, i, :], PR[:, n % 2, at:at + P], V[:, j, HV * n:HV * (n + 1)],
                                   start=(j == 0), stop=(j == i))
                if i == NT - 1:
                    mm.then_inc(sem["head_out"], 1)

            when = {1: {5: (0, 1, 2), 6: (3,), 7: (4,), 8: (5,), 9: (6,), 11: (7,)},
                    2: {2: (0,), 3: (1,), 4: (2,), 5: (3,), 6: (4,), 7: (5,), 9: (6,), 11: (7,)}}

            def attention(phase):
                for n in range(H):
                    for u in range(NU):
                        if phase == 2 and n + 2 < H:
                            max_unit(n + 2, u)
                        exp_unit(phase, n, u)
                        if n >= 1:
                            for i in when[phase].get(u, ()):
                                head_tile(n - 1, i)
                        if phase == 2 and u == 6 and 1 <= n and n + 1 < H:
                            turn_max(n + 1)
                for old in scores.rest():
                    pe.wait_ge(sem[old[0]], w.next(*old))
                    pe.sem_inc(held, 1)
                for old in turned.rest():
                    pe.wait_ge(sem[old[0]], w.next(*old))
                    pe.sem_inc(held, 1)
                for i in range(NT):
                    head_tile(H - 1, i)

            def output():
                pe.wait_ge(sem["split_o"], w.next("split_o"))
                turn(XS2, None)
                for c in range(4):
                    unit("xr_add", "g_dve", lambda bank: by_token(bank, O_, XT1, c))

            pe.wait_ge(sem["const_ready"], w.next("const_ready"))
            pe.wait_ge(sem["w_split"], w.next("w_split", 6))

            for phase in (1, 2):
                if phase == 2:
                    pe.wait_ge(sem["w_split"], w.next("w_split", 2))

                def batch(b, looped):
                    pe.wait_ge(sem["split1"], w.next("split1", 4))
                    turn(XS1, None)
                    project()
                    if looped:
                        turn_ln2()
                        gates(0)
                        gates(1)
                    if phase == 2:
                        for n in range(2):
                            for u in range(NU):
                                max_unit(n, u)
                    if looped:
                        gates(2)
                    if phase == 2:
                        turn_max(0)
                        turn_max(1)
                    if looped:
                        gates(3)
                    attention(phase)
                    output()

                run(pe, w, phase, batch)
                w.next("split1", 4)
                turn_ln2()
                for group in range(4):
                    gates(group)
                pe.wait_ge(sem["state_split"], w.next("state_split"))
                for c in range(4):
                    unit("cu", "g_dve", lambda bank: by_token(bank, UO, CP, c))

        @block.scalar
        def _(act):
            held = sem["held_act"]
            w = Counts()
            qk_free, u_free, xw_free = Ring(2), Ring(1), Ring(2)
            gate_free, probs_free, row_free = Ring(1), Ring(2), Ring(2)
            place = [0, 0]

            def step(instruction):
                instruction.then_inc(sem["act_step"], 1)
                act.wait_ge(sem["act_step"], w.next("act_step"))

            def turned_copy(dst):
                for part in range(2):
                    act.wait_ge(sem["g_act"], w.next("g_act"))
                    nc.scalar.copy(dst[part][:, 0, :], G[place[0] % 2][:, :].bitcast(BF16)
                                   ).then_inc(sem["xt_act"], 1)
                    place[0] += 2

            def project(phase):
                for r in range(4):
                    old = qk_free.turn("qkp_ready")
                    if old:
                        act.wait_ge(sem[old[0]], w.next(*old))
                    for c in range(2):
                        act.wait_ge(sem["g_act"], w.next("g_act"))
                        dst = QK[:, r % 2, c * CH:(c + 1) * CH]
                        src = G[place[0] % 2][:, :]
                        if phase == 1:
                            nc.scalar.copy(dst, src).then_inc(sem["qk_raw"], 1)
                        else:
                            at = (C_BK if r % 2 else C_BQ) + r // 2
                            nc.scalar.activation(dst, src, ACT.Identity, bias=COL[:, at:at + 1]
                                                 ).then_inc(sem["qk_raw"], 1)
                        place[0] += 1
                    if phase == 1:
                        old = u_free.turn("qk_ready")
                        if old:
                            act.wait_ge(sem[old[0]], w.next(*old))
                        act.wait_ge(sem["qk_raw"], w.next("qk_raw", 2))
                        step(nc.scalar.activation(U, QK[:, r % 2, :], ACT.Abs))
                        step(nc.scalar.activation(U, U, ACT.Exp, scale=-1.0))
                        nc.scalar.activation(U, U, ACT.Ln, bias=1.0).then_inc(sem["sp_log"], 1)
                    if r % 2:
                        place[0] += 2

            def turned_ln2():
                turned_copy(XT2)
                for c in range(4):
                    old = xw_free.turn(f"xw_stored{c % 2}", 16)
                    if old:
                        act.wait_ge(sem[old[0]], w.next(*old))
                    act.wait_ge(sem["g_act"], w.next("g_act"))
                    nc.scalar.copy(XW[:, c % 2, :], G[place[0] % 2][:, :]).then_inc(sem["xw_out"], 1)
                    place[0] += 1

            def gates(group):
                e = group % 2
                old = gate_free.turn("gate_used")
                if old:
                    act.wait_ge(sem[old[0]], w.next(*old))
                for g, at in enumerate((C_BF, C_BI, C_BC)):
                    act.wait_ge(sem["g_act"], w.next("g_act"))
                    nc.scalar.activation(TG[:, g, :], G[place[0] % 2][:, :], ACT.Tanh,
                                         bias=COL[:, at + e:at + e + 1], scale=1.0 if g == 2 else 0.5
                                         ).then_inc(sem["gate"], 1)
                    place[0] += 1

            def send_max(n):
                old = row_free.turn(f"max_sent{n % 2}", 16)
                if old:
                    act.wait_ge(sem[old[0]], w.next(*old))
                act.wait_ge(sem["max_turned"], w.next("max_turned"))
                nc.scalar.copy(MR[:, n % 2, :], MT[0:3 * NT, :]).then_inc(sem["max_row"], 1)

            def send_max_rows(n):
                act.wait_ge(sem["max_row"], w.next("max_row"))
                at = SLOT * (n % 2) + QROWS
                act.dma_start(QS[at:at + 3, (n // 2) % RING, :].rearrange("a (b c) -> a b c", c=P), MR[:, n % 2, :]
                              ).then_inc(sem[f"max_sent{n % 2}"], 16)

            def exp_units(phase, n):
                old = probs_free.turn("head_out")
                if old:
                    act.wait_ge(sem[old[0]], w.next(*old))
                for u, (j, c0, width, diag) in enumerate(EXP_UNITS):
                    if phase == 1 and diag:
                        continue
                    act.wait_ge(sem["t_full"], w.next("t_full"))
                    at = P_OFF[j] + c0 - j * P
                    dst, src = PR[:, n % 2, at:at + width], TB[place[1] % 2][:, 0:width]
                    place[1] += 1
                    if phase == 1:
                        nc.scalar.copy(dst, src).then_inc(sem["t_taken"], 1)
                    else:
                        nc.scalar.activation(dst, src, ACT.Exp).then_inc(sem["t_taken"], 1)
                    if phase == 2 and 1 <= n and n + 1 < H:
                        if u == 8:
                            send_max(n + 1)
                        if u == 9:
                            send_max_rows(n + 1)

            def h_tanh(c):
                act.wait_ge(sem["xi_sum"], w.next("xi_sum"))
                nc.scalar.activation(XI[:, c % 2, :], XI[:, c % 2, :], ACT.Tanh).then_inc(sem["xi_tanh"], 1)

            act.sem_inc(sem["gate_used"], 1)
            old = gate_free.turn("gate_used")
            if old:
                act.wait_ge(sem[old[0]], w.next(*old))
            for c in range(2):
                act.sem_inc(sem[f"xw_stored{c}"], 16)
                old = xw_free.turn(f"xw_stored{c}", 16)
                if old:
                    act.wait_ge(sem[old[0]], w.next(*old))
            act.wait_ge(sem["const_ready"], w.next("const_ready"))
            for phase in (1, 2):
                if phase == 2:
                    for c in range(4):
                        h_tanh(c)

                def batch(b, looped):
                    turned_copy(XT1)
                    if phase == 1:
                        act.preload_act_table_set("natural_log_exp_and_others")
                    project(phase)
                    if looped:
                        turned_ln2()
                        for group in range(3):
                            gates(group)
                    if phase == 2:
                        for n in range(2):
                            send_max(n)
                            send_max_rows(n)
                    if looped:
                        gates(3)
                    for n in range(H):
                        if phase == 2 and 2 <= n <= 5:
                            h_tanh(n - 2)
                        exp_units(phase, n)
                    turned_copy(XT1)
                    place[0] += 4

                run(act, w, phase, batch)
                turned_ln2()
                for group in range(4):
                    gates(group)
            for b in range(B):
                act.wait_ge(sem["fin_sum"], w.next("fin_sum"))
                a = PR[:, b % 2, 0:NT * D]
                nc.scalar.activation(a, a, ACT.Tanh).then_inc(sem["fin_tanh"], 1)

        @block.vector
        def _(dve):
            held = sem["held_dve"]
            w = Counts()
            xn_free, mp_free, on_free = Ring(2), Ring(2), Ring(1)
            place = [0, 0]

            def step(instruction):
                instruction.then_inc(sem["dve_step"], 1)
                dve.wait_ge(sem["dve_step"], w.next("dve_step"))
                dve.sem_inc(held, 1)

            def turned_copy(dst):
                for part in range(2):
                    dve.wait_ge(sem["g_dve"], w.next("g_dve"))
                    dve.tensor_copy(dst[part][:, 1, :], G[(place[0] + 1) % 2][:, :].bitcast(BF16)
                                    ).then_inc(sem["xt_dve"], 1)
                    place[0] += 2

            def project(phase):
                for e in range(2):
                    place[0] += 4
                    if phase == 1:
                        for r in (2 * e, 2 * e + 1):
                            dve.wait_ge(sem["sp_log"], w.next("sp_log"))
                            t = QK[:, r % 2, :]
                            step(dve.tensor_scalar(t, t, 0.0, PHI_EPS, ALU.max, ALU.add))
                            dve.tensor_tensor(t, t, U, ALU.add).then_inc(sem["qk_ready"], 1)
                    for c in (2 * e, 2 * e + 1):
                        dve.wait_ge(sem["g_dve"], w.next("g_dve"))
                        src = G[place[0] % 2][:, :].rearrange("p (n h v) -> p n h v", n=2, h=H)
                        dst = V[:, 2 * c:2 * c + 2, :].rearrange("p n (h v) -> p n h v", v=HV)[:, :, :, 0:HD]
                        for n in range(2):
                            if phase == 1:
                                i = dve.tensor_copy(dst[:, n], src[:, n])
                            else:
                                i = dve.tensor_tensor(dst[:, n], src[:, n],
                                                      ROW[:, 0, :].rearrange("p (h v) -> p h v", h=H), ALU.add)
                        i.then_inc(sem["v_in"], 1)
                        place[0] += 1

            def gates(group):
                e, c = group % 2, group // 2
                dve.wait_ge(sem["gate"], w.next("gate", 3))
                cs = CS[:, e, c * CH:(c + 1) * CH]
                dve.scalar_tensor_tensor(out=TG[:, 0, :], in0=TG[:, 0, :], scalar=1.0, in1=cs,
                                         op0=ALU.add, op1=ALU.mult)
                step(dve.scalar_tensor_tensor(out=TG[:, 1, :], in0=TG[:, 1, :], scalar=1.0, in1=TG[:, 2, :],
                                              op0=ALU.add, op1=ALU.mult))
                dve.scalar_tensor_tensor(out=cs, in0=TG[:, 0, :], scalar=0.5, in1=TG[:, 1, :],
                                         op0=ALU.mult, op1=ALU.add).then_inc(sem["gate_used"], 1)

            def max_unit(n, u):
                i, c0, width, diag = MAX_UNITS[u]
                if u == 0:
                    old = mp_free.turn("max_parts")
                    if old:
                        dve.wait_ge(sem[old[0]], w.next(*old))
                        dve.sem_inc(held, 1)
                dve.wait_ge(sem["s_full"], w.next("s_full"))
                if diag:
                    dve.sem_inc(held, 1)
                bank = SB[place[1] % 2][:, 0:width]
                place[1] += 1
                if diag:
                    dve.tensor_tensor_reduce(bank, bank, mask_s[:, CH - width:CH], 1.0, NEG,
                                             ALU.add, ALU.max, MP[:, n % 2, i:i + 1]).then_inc(sem["s_taken"], 1)
                else:
                    dve.tensor_reduce(MP[:, n % 2, NT + i:NT + i + 1], bank, AX.X, ALU.max
                                      ).then_inc(sem["s_taken"], 1)
                if u == NU - 1:
                    dve.wait_ge(sem["s_taken"], w.next("s_taken", NU))
                    m = MP[:, n % 2, :]
                    dve.tensor_tensor(m[:, NT // 2:NT], m[:, NT // 2:NT], m[:, NT + NT // 2:2 * NT], ALU.max
                                      ).then_inc(sem["max_ready"], 1)

            def copy_unit(n, u):
                j, c0, width, diag = EXP_UNITS[u]
                if not diag:
                    return
                dve.wait_ge(sem["s_full"], w.next("s_full"))
                at = P_OFF[j] + c0 - j * P
                dve.tensor_tensor(PR[:, n % 2, at:at + width], SB[place[1] % 2][:, 0:width], keep[:, 0:width],
                                  ALU.mult).then_inc(sem["s_taken"], 1)
                place[1] += 1

            def take_head(phase, n):
                if n == 0:
                    old = on_free.turn("split_o")
                    if old:
                        dve.wait_ge(sem[old[0]], w.next(*old))
                dve.wait_ge(sem["head_out"], w.next("head_out"))
                if phase == 1:
                    step(dve.tensor_scalar(DEN[:, :], OB[:, :, HD], DEN_EPS, None, ALU.add))
                    step(dve.reciprocal(REC[:, :], DEN[:, :]))
                else:
                    step(dve.reciprocal(REC[:, :], OB[:, :, HD]))
                dve.tensor_tensor(ON[:, :, HD * n:HD * (n + 1)], OB[:, :, 0:HD],
                                  REC[:, :].rearrange("p (n a) -> p n a", a=1).broadcast_to([P, NT, HD]), ALU.mult
                                  ).then_inc(sem["head_taken"], 1)

            def stats(src, tiles):
                for n in tiles:
                    i = dve.bn_stats(ST[:, n, :], src[:, n, :])
                step(i)

            def aggregate():
                for n in range(NT):
                    i = dve.bn_aggr(MV[:, n, :], ST[:, n, :])
                step(i)
                step(dve.tensor_scalar(VE[:, :], MV[:, :, 1], LN_EPS, None, ALU.add))
                step(dve.tensor_scalar(RS[:, :].bitcast(I32), VE[:, :].bitcast(I32), 1, None,
                                       ALU.logical_shift_right))
                step(dve.tensor_scalar(RS[:, :].bitcast(I32), RS[:, :].bitcast(I32), -1.0, float(0x5F3759DF),
                                       ALU.mult, ALU.add))
                for _ in range(3):
                    step(dve.tensor_tensor(NY[:, :], RS[:, :], RS[:, :], ALU.mult))
                    step(dve.scalar_tensor_tensor(out=NY[:, :], in0=NY[:, :], scalar=-0.5, in1=VE[:, :],
                                                  op0=ALU.mult, op1=ALU.mult))
                    step(dve.scalar_tensor_tensor(out=RS[:, :], in0=NY[:, :], scalar=1.5, in1=RS[:, :],
                                                  op0=ALU.add, op1=ALU.mult))

            def normalise(src, c, normed, split):
                old = xn_free.turn(split)
                if old:
                    dve.wait_ge(sem[old[0]], w.next(*old))
                for n in range(2):
                    t = 2 * c + n
                    i = dve.tensor_scalar(XN[:, c % 2, n * D:(n + 1) * D], src[:, t, :], MV[:, t, 0:1],
                                          RS[:, t:t + 1], ALU.subtract, ALU.mult)
                i.then_inc(sem[normed], 1)

            def h_sum(c):
                dve.wait_ge(sem[f"xi_in{c % 2}"], w.next(f"xi_in{c % 2}", 16))
                dve.tensor_tensor(XI[:, c % 2, :], XI[:, c % 2, :], pair(CU, c), ALU.add
                                  ).then_inc(sem["xi_sum"], 1)

            def h_add(c):
                if c == 0:
                    dve.wait_ge(sem["x_in"], w.next("x_in", 16))
                dve.wait_ge(sem["xi_tanh"], w.next("xi_tanh"))
                dve.tensor_tensor(pair(XA, c), pair(XA, c), XI[:, c % 2, :], ALU.add).then_inc(sem["xi_used"], 1)

            def front(phase, n):
                if phase == 2:
                    if 1 <= n <= 4:
                        h_sum(n - 1)
                    if 2 <= n <= 5:
                        h_add(n - 2)
                if n == 6:
                    if phase == 1:
                        dve.wait_ge(sem["x_in"], w.next("x_in", 16))
                    else:
                        dve.wait_ge(sem["xi_used"], w.next("xi_used", 4))
                    stats(XA, range(4))
                if n == 7:
                    stats(XA, range(4, NT))
                if n == 8:
                    aggregate()
                if 9 <= n <= 12:
                    normalise(XA, n - 9, "normed1", "split1")

            dve.wait_ge(sem["const_in"], w.next("const_in", 96))
            dve.memset(V[:, :, :], 1.0)
            dve.memset(QKP[1][0:3 * H, 0, :], 1.0)
            dve.memset(QKP[1][0:3 * H, 1, :], -1.0)
            dve.tensor_copy(QKP[0][0:3 * H, 0, :], U[0:3 * H])
            dve.tensor_copy(ident[:, :], XN[:, 0, 0:P])
            dve.tensor_copy(mask_t[:, :], XN[:, 0, P:2 * P])
            dve.tensor_scalar(COL[:, C_BQ:C_BQ + 2], COL[:, C_BQ:C_BQ + 2], HD ** -0.5, None, ALU.mult)
            dve.tensor_scalar(COL[:, C_BF:C_BF + 4], COL[:, C_BF:C_BF + 4], 0.5, None, ALU.mult)
            dve.tensor_scalar(COL[:, C_IN:C_IN + 2], COL[:, C_IN:C_IN + 2], 2.0, None, ALU.mult
                              ).then_inc(sem["const_ready"], 1)
            dve.wait_ge(sem["const_ready"], w.next("const_ready"))

            def split_weights(first, count, slot):
                for r in range(count // 2):
                    dve.wait_ge(sem[f"w_in{r % 2}"], w.next(f"w_in{r % 2}", 32))
                    for m in range(2):
                        s = slot + 2 * r + m
                        stage = QK[:, r % 2, m * KT * D:(m + 1) * KT * D]
                        scale = 0.5 if s in HALF else HD ** -0.5 if first == 4 and s == Q_ else None
                        if scale is not None:
                            step(dve.tensor_scalar(stage, stage, scale, None, ALU.mult))
                    stage = QK[:, r % 2, :]
                    s = slot + 2 * r
                    high = W[0][:, s:s + 2].rearrange("p m k e -> p (m k e)")
                    low = W[1][:, s:s + 2].rearrange("p m k e -> p (m k e)")
                    step(dve.tensor_copy(high, stage))
                    dve.tensor_tensor(low, stage, high, ALU.subtract).then_inc(sem["w_split"], 1)

            def set_state():
                step(dve.memset(CS[:, :, :], 0.0))
                for k in range(KT):
                    i = dve.tensor_scalar(CS[:, k, :], CS[:, k, :], COL[:, C_IN + k:C_IN + k + 1], None, ALU.add)
                i.then_inc(sem["state_set"], 1)

            split_weights(0, 4, 0)
            split_weights(8, 8, 4)
            for phase in (1, 2):
                if phase == 2:
                    w.next("s_taken", ND * H * B)
                    split_weights(4, 4, 0)
                set_state()
                if phase == 2:
                    for n in range(1, 6):
                        front(phase, n)
                for n in range(6, 13):
                    front(phase, n)

                def batch(b, looped):
                    turned_copy(XT1)
                    project(phase)
                    if looped:
                        turned_copy(XT2)
                        place[0] += 16
                        gates(0)
                        gates(1)
                    if phase == 2:
                        for n in range(2):
                            for u in range(NU):
                                max_unit(n, u)
                    if looped:
                        gates(2)
                        gates(3)
                    for n in range(H):
                        for u in range(NU):
                            if phase == 2 and n + 2 < H:
                                max_unit(n + 2, u)
                            if phase == 1:
                                copy_unit(n, u)
                        if n >= 1:
                            take_head(phase, n - 1)
                        front(phase, n)
                    take_head(phase, H - 1)
                    turned_copy(XT1)
                    for c in range(4):
                        if c == 0:
                            if phase == 1:
                                dve.wait_ge(sem["xr_in"], w.next("xr_in", 16))
                            else:
                                dve.wait_ge(sem["xr_bias"], w.next("xr_bias"))
                        dve.wait_ge(sem["g_dve"], w.next("g_dve"))
                        dve.tensor_tensor(pair(XR, c), G[place[0] % 2][:, :], pair(XR, c), ALU.add
                                          ).then_inc(sem["xr_add"], 1)
                        place[0] += 1
                    dve.wait_ge(sem["xr_add"], w.next("xr_add", 4))
                    stats(XR, range(NT))
                    aggregate()
                    for c in range(4):
                        normalise(XR, c, "normed2", "split2")

                run(dve, w, phase, batch)
                turned_copy(XT2)
                place[0] += 16
                for group in range(4):
                    gates(group)
                for c in range(4):
                    dve.wait_ge(sem["g_dve"], w.next("g_dve"))
                    for n in range(2):
                        i = dve.tensor_tensor(CU[:, 2 * c + n, :], G[place[0] % 2][:, n * D:(n + 1) * D],
                                              ROW[:, 2, :], ALU.add)
                    i.then_inc(sem["cu"], 1)
                    place[0] += 1
                dve.wait_ge(sem["cu"], w.next("cu", 4))
            for b in range(B + 1):
                if b < B:
                    dve.wait_ge(sem[f"fin_in{b % 2}"], w.next(f"fin_in{b % 2}", 32))
                    a = PR[:, b % 2, 0:NT * D]
                    dve.tensor_tensor(a, a, CU[:, :, :].rearrange("p n d -> p (n d)"), ALU.add
                                      ).then_inc(sem["fin_sum"], 1)
                if b >= 1:
                    dve.wait_ge(sem["fin_tanh"], w.next("fin_tanh"))
                    s = (b - 1) % 2
                    a = PR[:, s, NT * D:2 * NT * D]
                    dve.tensor_tensor(a, a, PR[:, s, 0:NT * D], ALU.add).then_inc(sem["fin_done"], 1)

        @block.gpsimd
        def _(pool):
            held = sem["held_pool"]
            w = Counts()
            parts_free, mb_free = Ring(2), Ring(1)

            def step(instruction, alone=False):
                instruction.then_inc(sem["pool_step"], 1)
                pool.wait_ge(sem["pool_step"], w.next("pool_step"))
                if alone:
                    pool.sem_inc(held, 1)

            def split(high, low, src, done):
                step(pool.tensor_copy(high, src))
                pool.tensor_tensor(low, src, high, ALU.subtract).then_inc(sem[done], 1)

            def split_norm(parts, normed, done, chunks=range(4)):
                for c in chunks:
                    pool.wait_ge(sem[normed], w.next(normed))
                    pool.sem_inc(held, 1)
                    split(pair(parts[0], c), pair(parts[1], c), XN[:, c % 2, :], done)

            def split_state(source, n):
                pool.wait_ge(sem[source], w.next(source, n))
                pool.sem_inc(held, 1)
                flat = [t[:, :, :].rearrange("p k t -> p (k t)") for t in (CP[0], CP[1], CS)]
                split(*flat, "state_split")

            def split_max(n):
                pool.wait_ge(sem["max_ready"], w.next("max_ready"))
                pool.sem_inc(held, 1)
                old = mb_free.turn("max_turned")
                if old:
                    pool.wait_ge(sem[old[0]], w.next(*old))
                    pool.sem_inc(held, 1)
                m = MP[:, n % 2, 0:NT]
                step(pool.tensor_copy(MB[:, 0, :], m))
                step(pool.tensor_tensor(MD[:, :], m, MB[:, 0, :], ALU.subtract), alone=True)
                step(pool.tensor_copy(MB[:, 1, :], MD[:, :]))
                pool.tensor_tensor(MB[:, 2, :], MD[:, :], MB[:, 1, :], ALU.subtract
                                   ).then_inc(sem["max_parts"], 1)

            w.next("gate_used", 1)
            pool.wait_ge(sem["const_ready"], w.next("const_ready"))
            pool.wait_ge(sem["const_stored"], w.next("const_stored", 48))
            for phase in (1, 2):
                if phase == 2:
                    w.next("qk_raw", 8 * B)
                    w.next("xr_in", 16 * B)
                split_state("state_set", 1)
                split_norm(XS1, "normed1", "split1")

                def batch(b, looped):
                    for r in range(4):
                        if phase == 1:
                            pool.wait_ge(sem["qk_ready"], w.next("qk_ready"))
                            pool.sem_inc(held, 1)
                        else:
                            pool.wait_ge(sem["qk_raw"], w.next("qk_raw", 2))
                            pool.sem_inc(held, 1)
                        old = parts_free.turn(f"qkp_stored{r % 2}", 48)
                        if old:
                            pool.wait_ge(sem[old[0]], w.next(*old))
                            pool.sem_inc(held, 1)
                        split(QKP[0][:, r % 2, :], QKP[1][:, r % 2, :], QK[:, r % 2, :], "qkp_ready")
                    if phase == 2:
                        split_max(0)
                        split_max(1)
                    if looped:
                        split_state("gate_used", 4)
                    if phase == 2:
                        pool.wait_ge(sem["xr_in"], w.next("xr_in", 16))
                        for n in range(NT):
                            i = pool.tensor_tensor(XR[:, n, :], XR[:, n, :], ROW[:, 1, :], ALU.add)
                        i.then_inc(sem["xr_bias"], 1)
                    for n in range(H):
                        if phase == 2 and n + 2 < H:
                            split_max(n + 2)
                        if n == 9:
                            pool.wait_ge(sem["xt_dve"], w.next("xt_dve", 2))
                            pool.sem_inc(held, 1)
                        if 9 <= n <= 12:
                            split_norm(XS1, "normed1", "split1", [n - 9])
                    if looped:
                        pool.wait_ge(sem["xt_dve"], w.next("xt_dve", 2))
                        pool.sem_inc(held, 1)
                    pool.wait_ge(sem["head_taken"], w.next("head_taken", H))
                    pool.sem_inc(held, 1)
                    split(*(t[:, :, :].rearrange("p n d -> p (n d)") for t in (XS2[0], XS2[1], ON)), "split_o")
                    pool.wait_ge(sem["xt_dve"], w.next("xt_dve", 2))
                    pool.sem_inc(held, 1)
                    split_norm(XS2, "normed2", "split2")

                run(pool, w, phase, batch)
                w.next("xt_dve", 2)
                split_state("gate_used", 4)


_INS = ["L0_attn_a_x", "L0_attn_a_Wq", "L0_attn_a_Wk", "L0_attn_a_Wv", "L0_attn_a_Wo",
        "L0_attn_b_Wq", "L0_attn_b_bq", "L0_attn_b_Wk", "L0_attn_b_bk", "L0_attn_b_Wv", "L0_attn_b_bv",
        "L0_attn_b_Wo", "L0_attn_b_bo", "L0_ffn_wf", "L0_ffn_uf", "L0_ffn_bf", "L0_ffn_wi", "L0_ffn_ui",
        "L0_ffn_bi", "L0_ffn_wc", "L0_ffn_uc", "L0_ffn_bc", "L0_ffn_wo", "L0_ffn_uo", "L0_ffn_bo", "L0_ffn_in_c"]


def kernel(**inputs):
    import numpy as np
    import concourse.bacc as bacc
    from concourse.bass_utils import run_bass_kernel_spmd as launch

    a = {n: np.asarray(inputs[n]) for n in _INS}
    turned = [a[f"L0_attn_a_{n}"].T for n in ("Wq", "Wk", "Wv", "Wo")]
    plain = [a[f"L0_attn_b_{n}"] for n in ("Wq", "Wk", "Wv", "Wo")]
    ffn = [a[f"L0_ffn_{n}"].T for n in ("wf", "uf", "wi", "ui", "wc", "uc", "wo", "uo")]
    col = [a[n].reshape(KT, P).T for n in ("L0_attn_b_bq", "L0_attn_b_bk", "L0_ffn_bf", "L0_ffn_bi", "L0_ffn_bc",
                                           "L0_ffn_in_c")]
    row = [a[n] for n in ("L0_attn_b_bv", "L0_attn_b_bo", "L0_ffn_bo")]
    slope = np.float32(2.0 ** (-8.0 / H)) ** np.arange(1, H + 1, dtype=np.float32)
    bias = slope[:, None] * (np.arange(T, dtype=np.float32) - T // 2)
    parts = []
    for _ in range(3):
        top = ((bias.view(np.uint32) + np.uint32(0x8000)) & np.uint32(0xFFFF0000)).view(np.float32)
        parts.append(top)
        bias = bias - top
    key_rows = np.stack(parts, axis=1).reshape(3 * H, T)
    p, c = np.arange(P)[:, None], np.arange(P)[None, :]
    masks = np.zeros((P, 2 * CH + 2 * P), np.float32)
    masks[:, CH - P:CH] = np.where(c > p, NEG, 0.0)
    masks[:, CH:2 * CH] = 1.0
    masks[:, CH:CH + P] = np.where(p <= c, 1.0, 0.0)
    masks[:, 2 * CH:2 * CH + P] = np.where(p == c, 1.0, 0.0)
    masks[:, 2 * CH + P:] = np.where(p > c, NEG, 0.0)
    arrays = {
        "in_x": np.ascontiguousarray(a["L0_attn_a_x"]),
        "in_weights": np.ascontiguousarray(np.stack(turned + plain + ffn)),
        "in_cols": np.ascontiguousarray(np.concatenate(col, axis=1)),
        "in_rows": np.ascontiguousarray(np.stack(row)),
        "in_key_rows": np.ascontiguousarray(key_rows),
        "in_masks": masks,
    }
    nc = bacc.Bacc("TRN2", target_bir_lowering=False, num_devices=1)
    args = [nc.dram_tensor(n, v.shape, mybir.dt.from_np(v.dtype), kind="ExternalInput").ap()
            for n, v in arrays.items()]
    args.append(nc.dram_tensor("out_0", (B, T, D), F32, kind="ExternalOutput").ap())
    mixer_kernel(nc, *args)
    r = launch(nc, [arrays], core_ids=[0])
    return r.results[0]["out_0"]
```

```python
from contextlib import ExitStack

import concourse.bass as bass
from concourse import mybir

F32 = mybir.dt.float32
BF16 = mybir.dt.bfloat16
I32 = mybir.dt.int32
ALU = mybir.AluOpType
ACT = mybir.ActivationFunctionType
AX = mybir.AxisListType

P = 128
B, T, D = 8, 1024, 256
H = 16
HD = D // H
NT = T // P
KT = D // P
CH = 512
HV = HD + 1
SLOT = 64
ROWS = 3 * HD
QROWS = ROWS + 3
KROWS = ROWS + 5
PAIRS = H // 2
RING = 4
GH = 8
SLOTS, SLOTS1 = 12, 4
LAG = 4
NEG = -1.0e30
LN_EPS, PHI_EPS, DEN_EPS = 1e-5, 1e-6, 1e-6

MAX_UNITS = []
for i in range(NT - 1, NT // 2 - 1, -1):
    MAX_UNITS.append([(i, 0, 4, 0)])
    rest, other = i - 3, NT - 1 - i
    MAX_UNITS.append([(i, 4, rest, 0)] + ([(other - 1, 0, other, rest)] if other else []))
MAX_UNITS.append([(3, 0, 4, 0)])
EXP_UNITS = [[(0, 0, 4, 0)], [(1, 1, 3, 0), (3, 3, 1, 3)], [(2, 2, 2, 0), (6, 6, 2, 2)]]
EXP_UNITS += [[(j, 4, 4, 0)] for j in range(5)] + [[(5, 5, 3, 0), (7, 7, 1, 3)]]
NU = len(MAX_UNITS)
assert NU == len(EXP_UNITS)
BY_DVE = (1, 4, 7)

Q_, K_, V_, O_, WF, UF, WI, UI, WC, UC, WO, UO = range(12)
HALF = (UF, UI, UC, UO)
GATES = ((WF, UF), (WI, UI), (WC, UC))
C_BQ, C_BK, C_BF, C_BI, C_BC, C_IN = (2 * n for n in range(6))
SPLIT = ((0, 0), (0, 1), (1, 0))

PER = {
    1: {"act_step": 8, "dve_step": 115, "g_act": 34, "g_dve": 20, "gate": 12, "gate_used": 4, 
        "head_taken": 16, "kt_in": 4, "low_pool": 32, "normed1": 4, "normed2": 4, "pv_done": 32, 
        "qk_high": 4, "qk_raw": 8, "qk_ready": 4, "qkp_ready": 4, "qkp_stored0": 48, "qkp_stored1": 48, 
        "qkp_stored2": 48, "qkp_stored3": 48, "s_full": 32, "s_taken": 32, "sp_log": 4, "split1": 4, 
        "split2": 4, "split_o": 1, "stack0": 128, "stack1": 128, "stack2": 128, "stack3": 128, 
        "state_high": 1, "state_split": 1, "sums_in": 6, "sums_split": 1, "v_in": 4, "x_in": 16, "xr_add": 4, 
        "xr_in": 16, "xr_stored": 16, "xt_act": 6, "xt_dve": 6, "xw_out": 4, "xw_stored0": 32, 
        "xw_stored1": 32},
    2: {"dve_step": 93, "g_act": 30, "g_dve": 14, "gate": 12, "gate_used": 4, "head_taken": 16, 
        "low_dve": 48, "low_pool": 96, "max_parts": 16, "max_ready": 16, "max_row": 16, "max_sent0": 128, 
        "max_sent1": 128, "max_turned": 16, "normed1": 4, "normed2": 4, "pool_step": 16, "pv_done": 144, 
        "qk_raw": 8, "qkp_ready": 4, "qkp_stored0": 48, "qkp_stored1": 48, "qkp_stored2": 48, 
        "qkp_stored3": 48, "s_full": 144, "s_taken": 144, "split1": 4, "split2": 4, "split_o": 1, 
        "stack0": 128, "stack1": 128, "stack2": 128, "stack3": 128, "state_high": 1, "state_split": 1, 
        "t_full": 144, "t_taken": 144, "v_in": 4, "x_in": 16, "xa_stored": 16, "xi_in0": 32, "xi_in1": 32, 
        "xi_sum": 4, "xi_tanh": 4, "xi_used": 4, "xr_add": 4, "xr_bias": 1, "xr_in": 16, "xr_stored": 16, 
        "xt_act": 6, "xt_dve": 6, "xw_out": 4, "xw_stored0": 32, "xw_stored1": 32},
}


class Counts:

    def __init__(self):
        self.seen, self.entry, self.trip, self.per = {}, None, None, None

    def later(self, name, n=1):
        self.seen[name] = self.seen.get(name, 0) + n
        return name, self.seen[name]

    def at(self, end):
        name, seen = end
        if self.trip is None:
            return seen
        assert seen > self.entry.get(name, 0)
        self.used.add(name)
        return self.trip * self.per.get(name, 0) + seen

    def next(self, name, n=1):
        return self.at(self.later(name, n))

    def open(self, trip, per):
        self.trip, self.per, self.entry, self.used = trip, per, dict(self.seen), set()

    def close(self, trips):
        for name in sorted(self.seen):
            n = self.seen[name] - self.entry.get(name, 0)
            if name in self.used and self.per.get(name) != n:
                print("PER", 1 if self.per is PER[1] else 2, name, n, self.per.get(name))
            self.seen[name] = self.entry.get(name, 0) + trips * n
        self.trip = None


class Ring:

    def __init__(self, depth):
        self.depth, self.ends = depth, []

    def turn(self, end):
        self.ends.append(end)
        return self.ends.pop(0) if len(self.ends) > self.depth else None

    def rest(self):
        ends, self.ends = self.ends, []
        return ends


def mixer_kernel(nc, x, weights, cols, rows, key_rows, masks, out):
    with ExitStack() as ctx:
        def sb(name, shape, dt):
            return ctx.enter_context(nc.sbuf_tensor(name, shape, dt))

        def ps(name, shape, dt):
            return ctx.enter_context(nc.psum_tensor(name, shape, dt))

        sem = {}
        for name in (
            "const_in", "const_ready", "const_stored", "w_in0", "w_in1", "w_split",
            "x_in", "xi_in0", "xi_in1", "xi_sum", "xi_tanh", "xi_used", "xa_stored",
            "normed1", "normed2", "split1", "split2", "split_o",
            "g_act", "g_dve", "xt_act", "xt_dve", "qk_raw", "qk_high", "sp_log", "qk_ready", "v_in",
            "qkp_ready", "qkp_stored0", "qkp_stored1", "qkp_stored2", "qkp_stored3",
            "stack0", "stack1", "stack2", "stack3",
            "kt_in", "sums_in", "sums_split",
            "s_full", "s_taken", "t_full", "t_taken", "low_dve", "low_pool", "pv_done", "head_taken",
            "max_ready", "max_parts", "max_turned", "max_row", "max_sent0", "max_sent1",
            "xr_in", "xr_bias", "xr_add", "xr_stored", "xw_out", "xw_stored0", "xw_stored1",
            "gate", "gate_used", "state_high", "state_split", "cu",
            "act_step", "dve_step", "pool_step",
            "held_pe", "held_act", "held_dve", "held_pool", "held_sp",
            "fin_in0", "fin_in1", "fin_sum", "fin_tanh", "fin_done", "fin_out0", "fin_out1",
        ):
            sem[name] = ctx.enter_context(nc.semaphore(name))

        q_dram = nc.dram_tensor("q_stack", (H, QROWS, T), BF16, kind="Internal").ap()
        k_dram = nc.dram_tensor("k_stack", (H, KROWS, T), BF16, kind="Internal").ap()
        x1_dram = nc.dram_tensor("x_after_attention", (B, T, D), F32, kind="Internal").ap()
        x2_dram = nc.dram_tensor("x_after_ffn", (B, T, D), F32, kind="Internal").ap()
        xw_dram = nc.dram_tensor("x_times_wo", (B, T, D), F32, kind="Internal").ap()

        W = [sb(f"w_{part}", [P, 12, KT, D], BF16) for part in ("high", "low")]
        XA = sb("x_for_attention", [P, NT, D], F32)
        XR = sb("x_residual", [P, NT, D], F32)
        XN = sb("ln1", [P, NT, D], F32)
        XL = sb("ln1_low", [P, NT, D], BF16)
        ON = sb("attention_out_or_ln2", [P, NT, D], F32)
        OL = sb("attention_out_or_ln2_low", [P, NT, D], BF16)
        XI = sb("ffn_h", [P, 2, 2 * D], F32)
        XW = sb("x_wo_out", [P, 2, 2 * D], F32)
        XT1 = [sb(f"ln1_o_turned_{part}", [P, KT, T], BF16) for part in ("high", "low")]
        XT2 = [sb(f"ln2_turned_{part}", [P, KT, T], BF16) for part in ("high", "low")]
        V = sb("values", [P, NT, H * 2 * HV], BF16)
        QK = sb("qk_block", [P, 2, T], F32)
        QKP = [sb(f"qk_{part}", [P, 2, T], BF16) for part in ("high", "low")]
        QS = sb("q_stacks", [P, RING, T], BF16)
        KS = sb("k_stacks", [P, RING, T], BF16)
        PR = sb("probs_turned", [P, SLOTS, CH], F32)
        PL = sb("probs_turned_low", [P, SLOTS, CH], BF16)
        MP = sb("maxima", [P, 2, 2 * NT], F32)
        MB = sb("maxima_parts", [P, 2, NT], BF16)
        MR = sb("maxima_rows", [2 * NT, 2, P], BF16)
        NM = sb("numerators", [P, 2, NT, HV], F32)
        REC = sb("reciprocals", [P, 2, NT], F32)
        CS = sb("state_doubled", [P, KT, T], F32)
        CP = [sb(f"state_{part}", [P, KT, T], BF16) for part in ("high", "low")]
        TG = sb("gate_tanhs", [P, 3, CH], F32)
        CU = sb("state_part_of_h", [P, NT, D], F32)
        ST = sb("ln_stats", [P, NT, 6], F32)
        MV = sb("ln_mean_var", [P, NT, 2], F32)
        VE = sb("ln_var_eps", [P, NT], F32)
        NY = sb("ln_newton", [P, NT], F32)
        RS = sb("ln_rstd", [P, NT], F32)
        COL = sb("feature_vectors", [P, 12], F32)
        ROW = sb("row_vectors", [P, 3, D], F32)
        ident = sb("identity", [P, P], BF16)
        mask_t = sb("mask_turned", [P, P], BF16)
        mask_s = sb("mask_scores", [P, P], BF16)
        keep = sb("mask_keep", [P, P], BF16)
        own = sb("mask_own_head", [P, GH * HV], BF16)
        zeros = sb("zeros", [P, GH * 2 * HV], BF16)

        U = CU[:, 0:T // D, :].rearrange("p n d -> p (n d)")
        QF = [PR[:, 4 + 2 * n:6 + 2 * n, :].rearrange("p a b -> p (a b)").bitcast(BF16)
              .rearrange("p (k t) -> p k t", k=KT) for n in range(2)]
        KF = [PR[:, 8 + 2 * n:10 + 2 * n, :].rearrange("p a b -> p (a b)").bitcast(BF16)
              .rearrange("p (n d) -> p n d", n=NT) for n in range(2)]
        SW = GH * HV
        SN = NT - 1
        SF = PL[:, SLOTS1:SLOTS, :].rearrange("p a b -> p (a b)").bitcast(F32)[:, 0:KT * SN * SW].rearrange(
            "p (k c v) -> p k c v", k=KT, c=SN)
        SL = CU[:, T // D:2 * T // D, :].rearrange("p n d -> p (n d)").bitcast(BF16)[:, 0:KT * SN * SW].rearrange(
            "p (k c v) -> p k c v", k=KT, c=SN)

        G = [ps(f"general_{n}", [P, CH], F32) for n in range(2)]
        SB = [ps(f"scores_{n}", [P, CH], F32) for n in range(2)]
        TB = [ps(f"turned_scores_{n}", [P, CH], F32) for n in range(2)]
        OB = [ps(f"out_of_heads_{n}", [P, CH], F32) for n in range(2)]
        STB = SB + TB

        def tokens(t, b):
            return t[b].rearrange("(n p) d -> p n d", p=P)

        def pair(t, c):
            return t[:, 2 * c:2 * c + 2, :].rearrange("p n d -> p (n d)")

        def flat(t):
            return t.rearrange("p a b -> p (a b)")

        def top(columns):
            return columns.bitcast(BF16)[:, 1::2]

        def turned_max(n):
            return (OB[n] if n < 2 else G[n % 2])[0:2 * NT, CH - P // 2:CH].bitcast(BF16)

        def parts_of(phase, r):
            if phase == 1:
                return [t[:, r // 2, :] for t in (QKP if r % 2 else QF)]
            return [t[:, r % 2, :] for t in QKP]

        block = ctx.enter_context(nc.Block())

        def run(eng, w, phase, batch):
            batch(0, False)
            with eng.Fori(0, B - 1) as trip:
                w.open(trip, PER[phase])
                batch(trip + 1, True)
                w.close(B - 1)

        @block.sync
        def _(sp):
            held = sem["held_sp"]
            w = Counts()

            def load_weights(first, rounds, waits_from):
                for r in range(rounds):
                    if r >= waits_from:
                        sp.wait_ge(sem["w_split"], w.next("w_split"))
                    for m in range(2):
                        src = weights[first + 2 * r + m].rearrange("(k p) e -> p k e", p=P)
                        dst = QK[:, r % 2, m * KT * D:(m + 1) * KT * D].rearrange("p (k e) -> p k e", k=KT)
                        sp.dma_start(dst, src).then_inc(sem[f"w_in{r % 2}"], 16)

            def load_xa(phase, b, normed=True, stored=True):
                if normed:
                    sp.wait_ge(sem["normed1"], w.next("normed1", 4))
                    sp.sem_inc(held, 1)
                if phase == 2 and stored:
                    sp.wait_ge(sem["xa_stored"], w.next("xa_stored", 16))
                    sp.sem_inc(held, 1)
                sp.dma_start(XA[:, :, :], tokens(x if phase == 1 else x1_dram, b)).then_inc(sem["x_in"], 16)

            def load_xi(b, chunks):
                for c in chunks:
                    if c >= 2:
                        sp.wait_ge(sem["xi_used"], w.next("xi_used"))
                        sp.sem_inc(held, 1)
                    sp.dma_start(XI[:, c % 2, :].rearrange("p (n d) -> p n d", n=2),
                                 tokens(xw_dram, b)[:, 2 * c:2 * c + 2]).then_inc(sem[f"xi_in{c % 2}"], 16)

            def store_xa(b):
                sp.wait_ge(sem["xi_used"], w.next("xi_used", 2))
                sp.sem_inc(held, 1)
                sp.dma_start(tokens(x2_dram, b), XA[:, :, :]).then_inc(sem["xa_stored"], 16)

            def store_stacks(phase):
                for r in range(4):
                    sp.wait_ge(sem["qkp_ready"], w.next("qkp_ready"))
                    sp.sem_inc(held, 1)
                    dst = (k_dram if r % 2 else q_dram)[8 * (r // 2):8 * (r // 2) + 8]
                    rows_of = ((0, 0), (0, HD), (1, 2 * HD)) if r % 2 else ((0, 0), (1, HD), (0, 2 * HD))
                    for part, at in rows_of:
                        sp.dma_start(dst[:, at:at + HD, :], parts_of(phase, r)[part]
                                     ).then_inc(sem[f"qkp_stored{r}"], 16)

            def load_stacks(phase, pairs):
                for r in pairs:
                    if r % 4 == 0:
                        for n in (r // 2, r // 2 + 1):
                            sp.wait_ge(sem[f"qkp_stored{n}"], w.next(f"qkp_stored{n}", 48))
                            sp.sem_inc(held, 1)
                    if phase == 1 and r == RING:
                        sp.wait_ge(sem["s_taken"], w.next("s_taken", 2 * NT))
                        sp.sem_inc(held, 1)
                    if phase == 2 and r >= RING:
                        sp.wait_ge(sem["t_taken"], w.next("t_taken", 2 * NU))
                        sp.sem_inc(held, 1)
                    nq, nk = (ROWS, ROWS) if phase == 1 else (QROWS, KROWS)
                    for par in range(2):
                        h, at = 2 * r + par, SLOT * par
                        sp.dma_start(QS[at:at + nq, r % RING, :], q_dram[h, 0:nq]
                                     ).then_inc(sem[f"stack{r % RING}"], 16)
                        sp.dma_start(KS[at:at + nk, r % RING, :], k_dram[h, 0:nk]
                                     ).then_inc(sem[f"stack{r % RING}"], 16)

            def store_xw(b):
                for c in range(4):
                    sp.wait_ge(sem["xw_out"], w.next("xw_out"))
                    sp.sem_inc(held, 1)
                    sp.dma_start(tokens(xw_dram, b)[:, 2 * c:2 * c + 2],
                                 XW[:, c % 2, :].rearrange("p (n d) -> p n d", n=2)
                                 ).then_inc(sem[f"xw_stored{c % 2}"], 16)

            def load_xr(phase, b, looped):
                if looped or phase == 2:
                    sp.wait_ge(sem["normed2"], w.next("normed2", 4))
                    sp.sem_inc(held, 1)
                    sp.wait_ge(sem["xr_stored"], w.next("xr_stored", 16))
                    sp.sem_inc(held, 1)
                sp.dma_start(XR[:, :, :], tokens(x if phase == 1 else x2_dram, b)).then_inc(sem["xr_in"], 16)

            def store_xr(b):
                sp.wait_ge(sem["xr_add"], w.next("xr_add", 4))
                sp.sem_inc(held, 1)
                sp.dma_start(tokens(x1_dram, b), XR[:, :, :]).then_inc(sem["xr_stored"], 16)

            sp.dma_start(COL[:, :], cols).then_inc(sem["const_in"], 16)
            sp.dma_start(ROW[:, :, :], rows.partition_broadcast(P)).then_inc(sem["const_in"], 16)
            sp.dma_start(flat(XN[:, 0:3, :])[:, 0:4 * P + SW], masks).then_inc(sem["const_in"], 16)
            sp.dma_start(U[0:3 * H], key_rows).then_inc(sem["const_in"], 16)
            load_weights(0, 2, 2)
            load_xa(1, 0, normed=False)
            load_weights(8, 4, 0)
            sp.wait_ge(sem["w_split"], w.next("w_split", 2))
            sp.wait_ge(sem["const_ready"], w.next("const_ready"))
            sp.dma_start(k_dram[:, ROWS:ROWS + 3, :], QKP[0][0:3 * H, 0, :]).then_inc(sem["const_stored"], 16)
            sp.dma_start(q_dram[:, ROWS:ROWS + 3, :], QKP[1][0:3 * H, 0, :]).then_inc(sem["const_stored"], 16)
            sp.dma_start(k_dram[:, ROWS + 3:ROWS + 5, :], QKP[1][0:2 * H, 1, :]).then_inc(sem["const_stored"], 16)
            sp.wait_ge(sem["const_stored"], w.next("const_stored", 48))

            for phase in (1, 2):
                if phase == 2:
                    load_weights(4, 2, 2)
                    sp.wait_ge(sem["w_split"], w.next("w_split", 2))
                    load_xa(2, 0, stored=False)
                    load_xi(0, range(4))
                    store_xa(0)

                def batch(b, looped):
                    load_xa(phase, (b + 1) % B)
                    store_stacks(phase)
                    load_stacks(phase, range(4))
                    if looped:
                        store_xw(b - 1)
                    load_xr(phase, b, looped)
                    if phase == 2:
                        load_xi((b + 1) % B, range(2))
                    load_stacks(phase, [4])
                    if phase == 2:
                        load_xi((b + 1) % B, range(2, 4))
                    load_stacks(phase, [5])
                    if phase == 2:
                        store_xa((b + 1) % B)
                    load_stacks(phase, [6, 7])
                    store_xr(b)
                    if phase == 1:
                        w.later("s_taken", 2 * NT)
                    else:
                        w.later("t_taken", RING * 2 * NU)

                run(sp, w, phase, batch)
                store_xw(B - 1)

            for n in range(2):
                sp.wait_ge(sem[f"xw_stored{n}"], 16 + 2 * 2 * 16 * B)
            sp.wait_ge(sem["xr_stored"], w.next("xr_stored", 16))
            sp.wait_ge(sem["xa_stored"], w.next("xa_stored", 16))
            sp.wait_ge(sem["split1"], 2 * 4 * (B + 1))
            for b in range(B):
                if b >= 2:
                    sp.wait_ge(sem[f"fin_out{b % 2}"], w.next(f"fin_out{b % 2}", 16))
                sp.dma_start((XN, ON)[b % 2][:, :, :], tokens(xw_dram, b)).then_inc(sem[f"fin_in{b % 2}"], 16)
                sp.dma_start((XA, XR)[b % 2][:, :, :], tokens(x1_dram, b)).then_inc(sem[f"fin_in{b % 2}"], 16)
                if b >= 1:
                    sp.wait_ge(sem["fin_done"], w.next("fin_done"))
                    sp.dma_start(tokens(out, b - 1), (XA, XR)[(b - 1) % 2][:, :, :]
                                 ).then_inc(sem[f"fin_out{(b - 1) % 2}"], 16)
            sp.wait_ge(sem["fin_done"], w.next("fin_done"))
            sp.dma_start(tokens(out, B - 1), (XA, XR)[(B - 1) % 2][:, :, :]
                         ).then_inc(sem[f"fin_out{(B - 1) % 2}"], 16)
            for n in range(2):
                sp.wait_ge(sem[f"fin_out{n}"], w.next(f"fin_out{n}", 16))

        @block.tensor
        def _(pe):
            held = sem["held_pe"]
            w = Counts()
            general, scores, turned, both = Ring(2), Ring(2), Ring(2), Ring(4)
            place = [0, 0, 0, 0]

            def drain_general():
                for end in general.rest():
                    pe.wait_ge(sem[end[0]], w.at(end))
                    pe.sem_inc(held, 1)

            def general_bank(consumer):
                end = general.turn(w.later(consumer))
                if end:
                    pe.wait_ge(sem[end[0]], w.at(end))
                    pe.sem_inc(held, 1)
                place[0] += 1
                return G[(place[0] - 1) % 2]

            def turn(high, low):
                for part in range(2):
                    for k in range(KT):
                        bank = general_bank(("xt_act", "xt_dve")[k])[:, :].bitcast(BF16)
                        for n in range(NT):
                            at = slice(k * P, (k + 1) * P)
                            src = low[:, n, at] if part else top(high[:, n, at])
                            mm = pe.transpose(bank[:, n * P:(n + 1) * P], src, ident[:, :])
                        mm.then_inc(sem[("g_act", "g_dve")[k]], 1)
                drain_general()

            def by_feature(bank, terms, e):
                todo = [(m, k, wp, xp, src, t0) for m, src, t0 in terms for k in range(KT) for wp, xp in SPLIT]
                for n, (m, k, wp, xp, src, t0) in enumerate(todo):
                    mm = pe.matmul(bank[:, :], W[wp][:, m, k, e * P:(e + 1) * P], src[xp][:, k, t0:t0 + CH],
                                   start=(n == 0), stop=(n == len(todo) - 1))
                return mm

            def by_token(bank, m, src, c):
                for n in range(2):
                    t0 = (2 * c + n) * P
                    todo = [(k, xp, wp) for k in range(KT) for xp, wp in SPLIT]
                    for i, (k, xp, wp) in enumerate(todo):
                        mm = pe.matmul(bank[:, n * D:(n + 1) * D], src[xp][:, k, t0:t0 + P], W[wp][:, m, k, :],
                                       start=(i == 0), stop=(i == len(todo) - 1))
                return mm

            def project():
                for e in range(2):
                    for m in (Q_, K_):
                        for c in range(2):
                            by_feature(general_bank("qk_raw"), [(m, XT1, c * CH)], e).then_inc(sem["g_act"], 1)
                    for c in (2 * e, 2 * e + 1):
                        by_token(general_bank("v_in"), V_, XT1, c).then_inc(sem["g_dve"], 1)

            def turn_ln2():
                pe.wait_ge(sem["split2"], w.next("split2", 4))
                pe.sem_inc(held, 1)
                turn(ON, OL)
                for c in range(4):
                    by_token(general_bank("xw_out"), WO, XT2, c).then_inc(sem["g_act"], 1)

            def gates(group):
                e, c = group % 2, group // 2
                if group == 0:
                    pe.wait_ge(sem["state_split"], w.next("state_split"))
                    pe.sem_inc(held, 1)
                for wm, um in GATES:
                    by_feature(general_bank("gate"), [(wm, XT2, c * CH), (um, CP, c * CH)], e
                               ).then_inc(sem["g_act"], 1)

            def sums():
                for n in range(4):
                    pe.wait_ge(sem["qkp_ready"], w.next("qkp_ready"))
                    pe.sem_inc(held, 1)
                for part in range(2):
                    for e in range(KT):
                        bank = general_bank("kt_in")[:, :].bitcast(BF16)
                        for n in range(NT):
                            mm = pe.transpose(bank[:, n * P:(n + 1) * P], QKP[part][:, e, n * P:(n + 1) * P],
                                              ident[:, :])
                        mm.then_inc(sem["g_act"], 1)
                drain_general()
                for e in range(KT):
                    for first in range(0, SN, 3):
                        bank = general_bank("sums_in")
                        for c in range(first, min(first + 3, SN)):
                            dst = bank[:, (c - first) * SW:(c - first + 1) * SW].rearrange("p (h v) -> p h v", v=HV)
                            v = V[:, c, :].rearrange("p (h a v) -> p h a v", a=2, v=HV)[:, GH * e:GH * (e + 1)]
                            for n, (kp, vp) in enumerate(SPLIT):
                                mm = pe.matmul(dst, KF[kp][:, c, e * P:(e + 1) * P], v[:, :, vp, :],
                                               start=(n == 0), stop=(n == 2))
                        mm.then_inc(sem["g_dve"], 1)

            def own_unit(k):
                c, g = k // 2 % NT, k % 2
                if c == 0 and g == 0:
                    for r in range(RING):
                        pe.wait_ge(sem[f"stack{r}"], w.next(f"stack{r}", 64))
                        pe.sem_inc(held, 1)
                end = both.turn(w.later("s_taken"))
                if end:
                    pe.wait_ge(sem[end[0]], w.at(end))
                    pe.sem_inc(held, 1)
                bank = STB[place[3] % 4]
                place[3] += 1
                for i in range(4):
                    at = SLOT * g
                    mm = pe.matmul(bank[:, i * P:(i + 1) * P], KS[at:at + ROWS, i, c * P:(c + 1) * P],
                                   QS[at:at + ROWS, i, c * P:(c + 1) * P], start=True, stop=True)
                mm.then_inc(sem["s_full"], 1)

            def own_out(k):
                e, c, g = k // (2 * NT), k // 2 % NT, k % 2
                bank = OB[c % 2]
                if g == 0:
                    if NT * e + c >= 2:
                        pe.wait_ge(sem["head_taken"], w.next("head_taken"))
                        pe.sem_inc(held, 1)
                    pe.matmul(bank[:, 0:2 * SW], ident[:, :], zeros[:, :], start=True, stop=False)
                    if c:
                        q_out = bank[:, 0:2 * SW].rearrange("p (h a v) -> p h a v", a=2, v=HV)[:, :, 0, :]
                        for qp, sp_ in SPLIT:
                            src = SL[:, e, c - 1, :] if sp_ else top(SF[:, e, c - 1, :])
                            pe.matmul(q_out, QF[qp][:, e, c * P:(c + 1) * P],
                                      src.rearrange("p (h v) -> p h v", v=HV), start=False, stop=False)
                pe.wait_ge(sem["low_pool"], w.next("low_pool"))
                s = k % SLOTS1
                for i in range(4):
                    h = 2 * i + g
                    at, v = 2 * HV * h, 2 * HV * (GH * e + h)
                    pe.matmul(bank[:, at:at + 2 * HV], top(PR[:, s, i * P:(i + 1) * P]), V[:, c, v:v + 2 * HV],
                              start=False, stop=False)
                    mm = pe.matmul(bank[:, at:at + HV], PL[:, s, i * P:(i + 1) * P], V[:, c, v:v + HV],
                                   start=False, stop=(g == 1 and i == 3))
                mm.then_inc(sem["pv_done"], 1)

            def linear_attention(looped):
                units = 2 * NT * KT
                for k in range(units):
                    if k == units // 2:
                        for j in range(k - 2, k):
                            own_out(j)
                        if looped:
                            gates(2)
                            gates(3)
                    own_unit(k)
                    if k == 1:
                        pe.wait_ge(sem["sums_split"], w.next("sums_split"))
                        pe.sem_inc(held, 1)
                    if k >= 2 and not units // 2 <= k < units // 2 + 2:
                        own_out(k - 2)
                for j in range(units - 2, units):
                    own_out(j)
                w.later("head_taken", 2)
                both.rest()
                drain_general()

            def max_unit(n, u):
                r, at = n // 2, SLOT * (n % 2)
                if u == 0 and n % 2 == 0:
                    pe.wait_ge(sem[f"stack{r % RING}"], w.next(f"stack{r % RING}", 64))
                    pe.sem_inc(held, 1)
                end = scores.turn(w.later("s_taken"))
                if end:
                    pe.wait_ge(sem[end[0]], w.at(end))
                    pe.sem_inc(held, 1)
                bank = SB[place[1] % 2]
                place[1] += 1
                for i, k0, tiles, first in MAX_UNITS[u]:
                    diag = k0 + tiles == i + 1
                    mm = pe.matmul(bank[:, first * P:(first + tiles) * P],
                                   QS[at:at + QROWS, r % RING, i * P:(i + 1) * P],
                                   KS[at:at + QROWS, r % RING, k0 * P:(k0 + tiles) * P], start=True, stop=not diag)
                    if diag:
                        mm = pe.matmul(bank[:, (first + tiles - 1) * P:(first + tiles) * P], ident[:, :],
                                       mask_s[:, :], start=False, stop=True)
                mm.then_inc(sem["s_full"], 1)

            def turn_max(n):
                pe.wait_ge(sem["max_parts"], w.next("max_parts"))
                pe.sem_inc(held, 1)
                pe.transpose(turned_max(n), flat(MB[:, :, :]), ident[:, :]).then_inc(sem["max_turned"], 1)

            def exp_unit(n, u):
                r, at = n // 2, SLOT * (n % 2)
                if u == 0:
                    pe.wait_ge(sem[f"max_sent{n % 2}"], w.next(f"max_sent{n % 2}", 16))
                    pe.sem_inc(held, 1)
                end = turned.turn(w.later("t_taken"))
                if end:
                    pe.wait_ge(sem[end[0]], w.at(end))
                    pe.sem_inc(held, 1)
                bank = TB[place[2] % 2]
                place[2] += 1
                for j, i0, tiles, first in EXP_UNITS[u]:
                    diag = i0 == j
                    mm = pe.matmul(bank[:, first * P:(first + tiles) * P],
                                   KS[at:at + KROWS, r % RING, j * P:(j + 1) * P],
                                   QS[at:at + KROWS, r % RING, i0 * P:(i0 + tiles) * P], start=True, stop=not diag)
                    if diag:
                        mm = pe.matmul(bank[:, first * P:(first + 1) * P], ident[:, :], mask_t[:, :],
                                       start=False, stop=True)
                mm.then_inc(sem["t_full"], 1)

            def values_unit(n, u):
                bank = OB[n % 2]
                if u == 0:
                    if n >= 2:
                        pe.wait_ge(sem["head_taken"], w.next("head_taken"))
                        pe.sem_inc(held, 1)
                    pe.matmul(bank[:, 0:2 * SW], ident[:, :], zeros[:, :], start=True, stop=False)
                if u in BY_DVE:
                    pe.wait_ge(sem["low_dve"], w.next("low_dve"))
                else:
                    pe.wait_ge(sem["low_pool"], w.next("low_pool"))
                s = (NU * n + u) % SLOTS
                for j, i0, tiles, first in EXP_UNITS[u]:
                    for i in range(tiles):
                        at, cols_ = 2 * HV * (i0 + i), slice((first + i) * P, (first + i + 1) * P)
                        pe.matmul(bank[:, at:at + 2 * HV], top(PR[:, s, cols_]),
                                  V[:, j, 2 * HV * n:2 * HV * (n + 1)], start=False, stop=False)
                        last = u == NU - 1 and first + i == 3
                        mm = pe.matmul(bank[:, at:at + HV], PL[:, s, cols_],
                                       V[:, j, 2 * HV * n:2 * HV * n + HV], start=False, stop=last)
                mm.then_inc(sem["pv_done"], 1)

            def softmax_attention():
                drain_general()
                for k in range(H * NU + LAG):
                    n, u = k // NU, k % NU
                    if n + 2 < H:
                        max_unit(n + 2, u)
                    if n < H:
                        exp_unit(n, u)
                    if k >= LAG:
                        values_unit((k - LAG) // NU, (k - LAG) % NU)
                    if u == 3 and 1 <= n and n + 1 < H:
                        turn_max(n + 1)
                w.later("head_taken", 2)
                scores.rest()
                turned.rest()

            def output():
                pe.wait_ge(sem["split_o"], w.next("split_o"))
                pe.sem_inc(held, 1)
                turn(ON, OL)
                for c in range(4):
                    by_token(general_bank("xr_add"), O_, XT1, c).then_inc(sem["g_dve"], 1)
                drain_general()

            pe.wait_ge(sem["const_ready"], w.next("const_ready"))
            pe.wait_ge(sem["w_split"], w.next("w_split", 6))

            for phase in (1, 2):
                if phase == 2:
                    pe.wait_ge(sem["w_split"], w.next("w_split", 2))

                def batch(b, looped):
                    pe.wait_ge(sem["split1"], w.next("split1", 4))
                    pe.sem_inc(held, 1)
                    turn(XN, XL)
                    project()
                    if looped:
                        turn_ln2()
                        gates(0)
                        gates(1)
                    if phase == 1:
                        sums()
                        linear_attention(looped)
                    else:
                        for n in range(2):
                            for u in range(NU):
                                max_unit(n, u)
                        if looped:
                            gates(2)
                        turn_max(0)
                        turn_max(1)
                        if looped:
                            gates(3)
                        softmax_attention()
                    output()

                run(pe, w, phase, batch)
                w.later("split1", 4)
                turn_ln2()
                for group in range(4):
                    gates(group)
                pe.wait_ge(sem["state_split"], w.next("state_split"))
                for c in range(4):
                    by_token(general_bank("cu"), UO, CP, c).then_inc(sem["g_dve"], 1)
                drain_general()

        @block.scalar
        def _(act):
            held = sem["held_act"]
            w = Counts()
            place = [0, 0]

            def step(instruction):
                instruction.then_inc(sem["act_step"], 1)
                act.wait_ge(sem["act_step"], w.next("act_step"))

            def taken_bank():
                act.wait_ge(sem["g_act"], w.next("g_act"))
                place[0] += 1
                return G[(place[0] - 1) % 2][:, :]

            def turned_copy(dst):
                for part in range(2):
                    nc.scalar.copy(dst[part][:, 0, :], taken_bank().bitcast(BF16)).then_inc(sem["xt_act"], 1)
                    place[0] += 1

            def project(phase):
                def high(r):
                    act.wait_ge(sem["qk_ready"], w.next("qk_ready"))
                    nc.scalar.copy(parts_of(1, r)[0], QK[:, r % 2, :]).then_inc(sem["qk_high"], 1)

                for r in range(4):
                    if r >= 2:
                        act.wait_ge(sem["qkp_ready"], w.next("qkp_ready"))
                        if phase == 2:
                            act.wait_ge(sem[f"qkp_stored{r - 2}"], w.next(f"qkp_stored{r - 2}", 48))
                            act.sem_inc(held, 1)
                    for c in range(2):
                        at = slice(c * CH, (c + 1) * CH)
                        src = taken_bank()
                        if phase == 1:
                            nc.scalar.copy(QK[:, r % 2, at], src).then_inc(sem["qk_raw"], 1)
                        else:
                            bias = (C_BK if r % 2 else C_BQ) + r // 2
                            nc.scalar.activation(QK[:, r % 2, at], src, ACT.Identity, bias=COL[:, bias:bias + 1])
                            nc.scalar.activation(QKP[0][:, r % 2, at], src, ACT.Identity,
                                                 bias=COL[:, bias:bias + 1]).then_inc(sem["qk_raw"], 1)
                    if phase == 1:
                        if r:
                            high(r - 1)
                        act.wait_ge(sem["qk_raw"], w.next("qk_raw", 2))
                        step(nc.scalar.activation(U, QK[:, r % 2, :], ACT.Abs))
                        step(nc.scalar.activation(U, U, ACT.Exp, scale=-1.0))
                        nc.scalar.activation(U, U, ACT.Ln, bias=1.0).then_inc(sem["sp_log"], 1)
                    if r % 2:
                        place[0] += 2
                if phase == 1:
                    high(3)
                w.later("qkp_ready", 2)
                if phase == 1:
                    for n in range(2):
                        w.later(f"qkp_stored{n}", 48)

            def turned_ln2():
                turned_copy(XT2)
                for c in range(4):
                    act.wait_ge(sem[f"xw_stored{c % 2}"], w.next(f"xw_stored{c % 2}", 16))
                    nc.scalar.copy(XW[:, c % 2, :], taken_bank()).then_inc(sem["xw_out"], 1)

            def gates(group):
                e = group % 2
                if group:
                    act.wait_ge(sem["gate_used"], w.next("gate_used"))
                for g, at in enumerate((C_BF, C_BI, C_BC)):
                    nc.scalar.activation(TG[:, g, :], taken_bank(), ACT.Tanh,
                                         bias=COL[:, at + e:at + e + 1], scale=1.0 if g == 2 else 0.5
                                         ).then_inc(sem["gate"], 1)

            def state_high():
                act.wait_ge(sem["gate_used"], w.next("gate_used"))
                nc.scalar.copy(flat(CP[0][:, :, :]), flat(CS[:, :, :])).then_inc(sem["state_high"], 1)

            def keys_by_token():
                for part in range(2):
                    for e in range(KT):
                        nc.scalar.copy(KF[part][:, :, e * P:(e + 1) * P],
                                       taken_bank().bitcast(BF16).rearrange("p (n d) -> p n d", n=NT)
                                       ).then_inc(sem["kt_in"], 1)
                place[0] += KT * -(-SN // 3)

            def send_max(n):
                act.wait_ge(sem["max_turned"], w.next("max_turned"))
                nc.scalar.copy(MR[:, n % 2, :], turned_max(n)).then_inc(sem["max_row"], 1)

            def send_max_rows(n):
                act.wait_ge(sem["max_row"], w.next("max_row"))
                at = SLOT * (n % 2) + QROWS
                act.dma_start(QS[at:at + 2, (n // 2) % RING, :].rearrange("a (b c) -> a b c", c=P), MR[:, n % 2, :]
                              ).then_inc(sem[f"max_sent{n % 2}"], 16)

            def exp_unit(n, u):
                k = NU * n + u
                if k >= SLOTS:
                    act.wait_ge(sem["pv_done"], w.next("pv_done"))
                act.wait_ge(sem["t_full"], w.next("t_full"))
                nc.scalar.activation(PR[:, k % SLOTS, :], TB[place[1] % 2][:, :], ACT.Exp).then_inc(sem["t_taken"], 1)
                place[1] += 1

            def h_tanh(c):
                act.wait_ge(sem["xi_sum"], w.next("xi_sum"))
                nc.scalar.activation(XI[:, c % 2, :], XI[:, c % 2, :], ACT.Tanh).then_inc(sem["xi_tanh"], 1)

            for c in range(2):
                act.sem_inc(sem[f"xw_stored{c}"], 16)
            act.wait_ge(sem["const_ready"], w.next("const_ready"))
            act.wait_ge(sem["const_stored"], w.next("const_stored", 48))
            for phase in (1, 2):
                if phase == 2:
                    for c in range(4):
                        h_tanh(c)

                def batch(b, looped):
                    turned_copy(XT1)
                    if phase == 1:
                        act.preload_act_table_set("natural_log_exp_and_others")
                    project(phase)
                    if looped:
                        turned_ln2()
                        gates(0)
                        gates(1)
                    if phase == 1:
                        keys_by_token()
                    if looped:
                        gates(2)
                    if phase == 2:
                        for n in range(2):
                            send_max(n)
                            send_max_rows(n)
                    if looped:
                        gates(3)
                    if looped and phase == 1:
                        state_high()
                    if phase == 2:
                        for n in range(H):
                            if 2 <= n <= 5:
                                h_tanh(n - 2)
                            if n == 1 and looped:
                                state_high()
                            for u in range(NU):
                                exp_unit(n, u)
                                if u == 4 and 1 <= n and n + 1 < H:
                                    send_max(n + 1)
                                if u == 5 and 1 <= n and n + 1 < H:
                                    send_max_rows(n + 1)
                        w.later("pv_done", SLOTS)
                    turned_copy(XT1)
                    place[0] += 4

                if phase == 2:
                    w.later("pv_done", 2 * NT * KT * B)
                run(act, w, phase, batch)
                turned_ln2()
                for group in range(4):
                    gates(group)
                state_high()
                place[0] += 4
            for b in range(B):
                act.wait_ge(sem["fin_sum"], w.next("fin_sum"))
                a = flat((XN, ON)[b % 2][:, :, :])
                nc.scalar.activation(a, a, ACT.Tanh).then_inc(sem["fin_tanh"], 1)

        @block.vector
        def _(dve):
            held = sem["held_dve"]
            w = Counts()
            place = [0, 0]

            def step(instruction):
                instruction.then_inc(sem["dve_step"], 1)
                dve.wait_ge(sem["dve_step"], w.next("dve_step"))

            def taken_bank():
                dve.wait_ge(sem["g_dve"], w.next("g_dve"))
                place[0] += 1
                return G[(place[0] - 1) % 2][:, :]

            def turned_copy(dst):
                for part in range(2):
                    place[0] += 1
                    dve.tensor_copy(dst[part][:, 1, :], taken_bank().bitcast(BF16)).then_inc(sem["xt_dve"], 1)

            def project(phase):
                for e in range(2):
                    place[0] += 4
                    if phase == 1:
                        for r in (2 * e, 2 * e + 1):
                            dve.wait_ge(sem["sp_log"], w.next("sp_log"))
                            t = QK[:, r % 2, :]
                            step(dve.tensor_scalar(t, t, 0.0, PHI_EPS, ALU.max, ALU.add))
                            dve.tensor_tensor(t, t, U, ALU.add).then_inc(sem["qk_ready"], 1)
                    for c in (2 * e, 2 * e + 1):
                        bank = taken_bank()
                        if phase == 2:
                            step(dve.tensor_tensor(PR[:, c % 2, :].rearrange("p (n d) -> p n d", n=2),
                                                   bank.rearrange("p (n d) -> p n d", n=2),
                                                   ROW[:, 0:1, :].broadcast_to([P, 2, D]), ALU.add))
                            bank = PR[:, c % 2, :]
                        for n in range(2):
                            src = bank[:, n * D:(n + 1) * D].rearrange("p (h v) -> p h v", h=H)
                            dst = V[:, 2 * c + n, :].rearrange("p (h a v) -> p h a v", a=2, v=HV)[:, :, :, 0:HD]
                            step(dve.tensor_copy(dst[:, :, 0, :], src))
                            i = dve.tensor_tensor(dst[:, :, 1, :], src, dst[:, :, 0, :], ALU.subtract)
                        i.then_inc(sem["v_in"], 1)

            def gates(group):
                e, c = group % 2, group // 2
                dve.wait_ge(sem["gate"], w.next("gate", 3))
                cs = CS[:, e, c * CH:(c + 1) * CH]
                dve.scalar_tensor_tensor(out=TG[:, 0, :], in0=TG[:, 0, :], scalar=1.0, in1=cs,
                                         op0=ALU.add, op1=ALU.mult)
                step(dve.scalar_tensor_tensor(out=TG[:, 1, :], in0=TG[:, 1, :], scalar=1.0, in1=TG[:, 2, :],
                                              op0=ALU.add, op1=ALU.mult))
                dve.scalar_tensor_tensor(out=cs, in0=TG[:, 0, :], scalar=0.5, in1=TG[:, 1, :],
                                         op0=ALU.mult, op1=ALU.add).then_inc(sem["gate_used"], 1)

            def sums():
                place[0] += 4
                for e in range(KT):
                    for first in range(0, SN, 3):
                        n = min(3, SN - first)
                        dve.tensor_tensor(SF[:, e, first:first + n, :],
                                          taken_bank()[:, 0:n * SW].rearrange("p (c v) -> p c v", c=n),
                                          own[:, :].rearrange("p (c v) -> p c v", c=1).broadcast_to([P, n, SW]),
                                          ALU.mult).then_inc(sem["sums_in"], 1)
                dve.wait_ge(sem["sums_in"], w.next("sums_in", KT * -(-SN // 3)))
                for c in range(1, SN):
                    step(dve.tensor_tensor(SF[:, :, c, :], SF[:, :, c, :], SF[:, :, c - 1, :], ALU.add))
                for e in range(KT):
                    src = SF[:, e].rearrange("p c v -> p (c v)")
                    i = dve.tensor_tensor(SL[:, e].rearrange("p c v -> p (c v)"), src, top(src), ALU.subtract)
                i.then_inc(sem["sums_split"], 1)

            def mask_unit(k):
                if k % (2 * NT) >= SLOTS1:
                    dve.wait_ge(sem["pv_done"], w.next("pv_done"))
                    dve.sem_inc(held, 1)
                dve.wait_ge(sem["s_full"], w.next("s_full"))
                dve.tensor_tensor(PR[:, k % SLOTS1, :].rearrange("p (a b) -> p a b", a=4),
                                  STB[place[1] % 4][:, :].rearrange("p (a b) -> p a b", a=4),
                                  keep[:, :].rearrange("p (a b) -> p a b", a=1).broadcast_to([P, 4, P]),
                                  ALU.mult).then_inc(sem["s_taken"], 1)
                place[1] += 1

            def take_chunk(e, c):
                src = OB[c % 2][:, 0:2 * SW].rearrange("p (h a v) -> p h a v", a=2, v=HV)
                num, rec = NM[:, c % 2], REC[:, c % 2, :]
                step(dve.tensor_copy(num, src[:, :, 0, :]))
                step(dve.tensor_tensor(num, num, src[:, :, 1, :], ALU.add))
                step(dve.tensor_scalar(rec, num[:, :, HD], DEN_EPS, None, ALU.add))
                step(dve.reciprocal(rec, rec))
                dve.tensor_tensor(ON[:, c, e * P:(e + 1) * P].rearrange("p (h v) -> p h v", h=GH), num[:, :, 0:HD],
                                  rec.rearrange("p (n a) -> p n a", a=1).broadcast_to([P, GH, HD]), ALU.mult
                                  ).then_inc(sem["head_taken"], 1)

            def max_unit(n, u):
                if u == 0:
                    if n >= 2:
                        dve.wait_ge(sem["max_parts"], w.next("max_parts"))
                        dve.sem_inc(held, 1)
                dve.wait_ge(sem["s_full"], w.next("s_full"))
                bank = SB[place[1] % 2]
                place[1] += 1
                for i, k0, tiles, first in MAX_UNITS[u]:
                    at = i + (NT if k0 else 0)
                    r = dve.tensor_reduce(MP[:, n % 2, at:at + 1], bank[:, first * P:(first + tiles) * P],
                                          AX.X, ALU.max)
                r.then_inc(sem["s_taken"], 1)
                if u == NU - 1:
                    dve.wait_ge(sem["s_taken"], w.next("s_taken", NU))
                    m = MP[:, n % 2, :]
                    dve.tensor_tensor(m[:, NT // 2:NT], m[:, NT // 2:NT], m[:, NT + NT // 2:2 * NT], ALU.max
                                      ).then_inc(sem["max_ready"], 1)

            def low_unit(n, u):
                skipped = u - max([-1] + [d for d in BY_DVE if d < u])
                dve.wait_ge(sem["t_taken"], w.next("t_taken", skipped))
                s = (NU * n + u) % SLOTS
                dve.tensor_tensor(PL[:, s, :], PR[:, s, :], top(PR[:, s, :]), ALU.subtract
                                  ).then_inc(sem["low_dve"], 1)

            def take_head(n):
                dve.wait_ge(sem["pv_done"], w.next("pv_done", NU))
                dve.sem_inc(held, 1)
                src = OB[n % 2][:, 0:2 * SW].rearrange("p (n a v) -> p n a v", a=2, v=HV)
                num, rec = NM[:, n % 2], REC[:, n % 2, :]
                step(dve.tensor_copy(num, src[:, :, 0, :]))
                step(dve.tensor_tensor(num, num, src[:, :, 1, :], ALU.add))
                step(dve.reciprocal(rec, num[:, :, HD]))
                dve.tensor_tensor(ON[:, :, HD * n:HD * (n + 1)], num[:, :, 0:HD],
                                  rec.rearrange("p (n a) -> p n a", a=1).broadcast_to([P, NT, HD]), ALU.mult
                                  ).then_inc(sem["head_taken"], 1)

            def stats(src, tiles):
                for n in tiles:
                    i = dve.bn_stats(ST[:, n, :], src[:, n, :])
                step(i)
                dve.sem_inc(held, 1)

            def aggregate():
                for n in range(NT):
                    i = dve.bn_aggr(MV[:, n, :], ST[:, n, :])
                step(i)
                step(dve.tensor_scalar(VE[:, :], MV[:, :, 1], LN_EPS, None, ALU.add))
                step(dve.tensor_scalar(RS[:, :].bitcast(I32), VE[:, :].bitcast(I32), 1, None,
                                       ALU.logical_shift_right))
                step(dve.tensor_scalar(RS[:, :].bitcast(I32), RS[:, :].bitcast(I32), -1.0, float(0x5F3759DF),
                                       ALU.mult, ALU.add))
                for _ in range(3):
                    step(dve.tensor_tensor(NY[:, :], RS[:, :], RS[:, :], ALU.mult))
                    step(dve.scalar_tensor_tensor(out=NY[:, :], in0=NY[:, :], scalar=-0.5, in1=VE[:, :],
                                                  op0=ALU.mult, op1=ALU.mult))
                    step(dve.scalar_tensor_tensor(out=RS[:, :], in0=NY[:, :], scalar=1.5, in1=RS[:, :],
                                                  op0=ALU.add, op1=ALU.mult))

            def normalise(src, dst, c, normed):
                for t in (2 * c, 2 * c + 1):
                    i = dve.tensor_scalar(dst[:, t, :], src[:, t, :], MV[:, t, 0:1], RS[:, t:t + 1],
                                          ALU.subtract, ALU.mult)
                i.then_inc(sem[normed], 1)

            def h_sum(c):
                dve.wait_ge(sem[f"xi_in{c % 2}"], w.next(f"xi_in{c % 2}", 16))
                dve.tensor_tensor(XI[:, c % 2, :], XI[:, c % 2, :], pair(CU, c), ALU.add
                                  ).then_inc(sem["xi_sum"], 1)

            def h_add(c):
                if c == 0:
                    dve.wait_ge(sem["x_in"], w.next("x_in", 16))
                dve.wait_ge(sem["xi_tanh"], w.next("xi_tanh"))
                dve.tensor_tensor(pair(XA, c), pair(XA, c), XI[:, c % 2, :], ALU.add).then_inc(sem["xi_used"], 1)

            def front(phase, n):
                if phase == 2:
                    if 1 <= n <= 4:
                        h_sum(n - 1)
                    if 2 <= n <= 5:
                        h_add(n - 2)
                if n == 6:
                    if phase == 1:
                        dve.wait_ge(sem["x_in"], w.next("x_in", 16))
                    else:
                        dve.wait_ge(sem["xi_used"], w.next("xi_used", 4))
                    stats(XA, range(4))
                if n == 7:
                    stats(XA, range(4, NT))
                if n == 8:
                    aggregate()
                if 9 <= n <= 12:
                    normalise(XA, XN, n - 9, "normed1")

            dve.wait_ge(sem["const_in"], w.next("const_in", 64))
            dve.memset(V[:, :, :], 0.0).then_inc(sem["dve_step"], 1)
            dve.wait_ge(sem["dve_step"], w.next("dve_step"))
            dve.memset(V[:, :, :].rearrange("p n (h v) -> p (n h) v", v=2 * HV)[:, :, HD:HD + 1], 1.0)
            dve.memset(zeros[:, :], 0.0)
            dve.memset(QKP[1][0:3 * H, 0, :], 1.0)
            dve.memset(QKP[1][0:3 * H, 1, :], -1.0)
            dve.tensor_copy(QKP[0][0:3 * H, 0, :], U[0:3 * H])
            stage = flat(XN[:, 0:3, :])
            for n, t in enumerate((ident, mask_t, mask_s, keep)):
                dve.tensor_copy(t[:, :], stage[:, n * P:(n + 1) * P])
            dve.tensor_copy(own[:, :], stage[:, 4 * P:4 * P + SW])
            dve.tensor_scalar(COL[:, C_BQ:C_BQ + 2], COL[:, C_BQ:C_BQ + 2], HD ** -0.5, None, ALU.mult)
            dve.tensor_scalar(COL[:, C_BF:C_BF + 4], COL[:, C_BF:C_BF + 4], 0.5, None, ALU.mult)
            dve.tensor_scalar(COL[:, C_IN:C_IN + 2], COL[:, C_IN:C_IN + 2], 2.0, None, ALU.mult
                              ).then_inc(sem["const_ready"], 1)
            dve.wait_ge(sem["const_ready"], w.next("const_ready"))

            def split_weights(first, rounds, slot):
                for r in range(rounds):
                    dve.wait_ge(sem[f"w_in{r % 2}"], w.next(f"w_in{r % 2}", 32))
                    for m in range(2):
                        s = slot + 2 * r + m
                        stage = QK[:, r % 2, m * KT * D:(m + 1) * KT * D]
                        scale = 0.5 if s in HALF else HD ** -0.5 if first == 4 and s == Q_ else None
                        if scale is not None:
                            step(dve.tensor_scalar(stage, stage, scale, None, ALU.mult))
                    stage = QK[:, r % 2, :]
                    s = slot + 2 * r
                    high = W[0][:, s:s + 2].rearrange("p m k e -> p (m k e)")
                    low = W[1][:, s:s + 2].rearrange("p m k e -> p (m k e)")
                    step(dve.tensor_copy(high, stage))
                    dve.tensor_tensor(low, stage, high, ALU.subtract).then_inc(sem["w_split"], 1)

            def set_state():
                step(dve.memset(CS[:, :, :], 0.0))
                for k in range(KT):
                    i = dve.tensor_scalar(CS[:, k, :], CS[:, k, :], COL[:, C_IN + k:C_IN + k + 1], None, ALU.add)
                step(i)
                step(dve.tensor_copy(CP[0][:, :, :], CS[:, :, :]))
                dve.tensor_tensor(CP[1][:, :, :], CS[:, :, :], CP[0][:, :, :], ALU.subtract
                                  ).then_inc(sem["state_split"], 1)

            split_weights(0, 2, 0)
            split_weights(8, 4, 4)
            for phase in (1, 2):
                if phase == 2:
                    w.later("s_taken", 2 * NT * KT * B)
                    split_weights(4, 2, 0)
                set_state()
                if phase == 2:
                    for n in range(1, 6):
                        front(phase, n)
                for n in range(6, 13):
                    front(phase, n)

                def batch(b, looped):
                    turned_copy(XT1)
                    project(phase)
                    if looped:
                        turned_copy(XT2)
                        place[0] += 10
                        gates(0)
                        gates(1)
                    if phase == 1:
                        sums()
                        for e in range(KT):
                            for c in range(NT):
                                for g in range(2):
                                    mask_unit(2 * (NT * e + c) + g)
                                if c >= 2:
                                    take_chunk(e, c - 2)
                                front(phase, NT * e + c)
                            for c in (NT - 2, NT - 1):
                                dve.wait_ge(sem["pv_done"], w.next("pv_done", 2))
                                dve.sem_inc(held, 1)
                                take_chunk(e, c)
                            if looped and e == 0:
                                place[0] += 6
                                gates(2)
                                gates(3)
                    else:
                        for n in range(2):
                            for u in range(NU):
                                max_unit(n, u)
                        if looped:
                            place[0] += 6
                            gates(2)
                            gates(3)
                        for n in range(H):
                            for u in range(NU):
                                if n + 2 < H:
                                    max_unit(n + 2, u)
                                if u - 1 in BY_DVE:
                                    low_unit(n, u - 1)
                                if u == LAG + 1 and n >= 1:
                                    take_head(n - 1)
                            w.later("t_taken", NU - 1 - BY_DVE[-1])
                            front(phase, n)
                        take_head(H - 1)
                        w.later("max_parts", 2)
                    turned_copy(XT1)
                    for c in range(4):
                        if c == 0:
                            if phase == 1:
                                dve.wait_ge(sem["xr_in"], w.next("xr_in", 16))
                            else:
                                dve.wait_ge(sem["xr_bias"], w.next("xr_bias"))
                        dve.tensor_tensor(pair(XR, c), taken_bank(), pair(XR, c), ALU.add
                                          ).then_inc(sem["xr_add"], 1)
                    dve.wait_ge(sem["xr_add"], w.next("xr_add", 4))
                    stats(XR, range(NT))
                    aggregate()
                    for c in range(4):
                        normalise(XR, ON, c, "normed2")

                run(dve, w, phase, batch)
                turned_copy(XT2)
                place[0] += 16
                for group in range(4):
                    gates(group)
                for c in range(4):
                    bank = taken_bank()
                    for n in range(2):
                        i = dve.tensor_tensor(CU[:, 2 * c + n, :], bank[:, n * D:(n + 1) * D],
                                              ROW[:, 2, :], ALU.add)
                    i.then_inc(sem["cu"], 1)
                dve.wait_ge(sem["cu"], w.next("cu", 4))
            for b in range(B + 1):
                if b < B:
                    dve.wait_ge(sem[f"fin_in{b % 2}"], w.next(f"fin_in{b % 2}", 32))
                    a = flat((XN, ON)[b % 2][:, :, :])
                    dve.tensor_tensor(a, a, flat(CU[:, :, :]), ALU.add).then_inc(sem["fin_sum"], 1)
                if b >= 1:
                    dve.wait_ge(sem["fin_tanh"], w.next("fin_tanh"))
                    s = (b - 1) % 2
                    a = flat((XA, XR)[s][:, :, :])
                    dve.tensor_tensor(a, a, flat((XN, ON)[s][:, :, :]), ALU.add).then_inc(sem["fin_done"], 1)

        @block.gpsimd
        def _(pool):
            held = sem["held_pool"]
            w = Counts()

            def lows(normed, done, src, dst, chunks=range(4)):
                for c in chunks:
                    pool.wait_ge(sem[normed], w.next(normed))
                    pool.tensor_tensor(pair(dst, c), pair(src, c), top(pair(src, c)), ALU.subtract
                                       ).then_inc(sem[done], 1)

            def state_low():
                pool.wait_ge(sem["state_high"], w.next("state_high"))
                pool.tensor_tensor(flat(CP[1][:, :, :]), flat(CS[:, :, :]), flat(CP[0][:, :, :]), ALU.subtract
                                   ).then_inc(sem["state_split"], 1)

            def split_max(n):
                pool.wait_ge(sem["max_ready"], w.next("max_ready"))
                pool.sem_inc(held, 1)
                if n >= 1:
                    pool.wait_ge(sem["max_turned"], w.next("max_turned"))
                    pool.sem_inc(held, 1)
                m = MP[:, n % 2, 0:NT]
                pool.tensor_copy(MB[:, 0, :], m).then_inc(sem["pool_step"], 1)
                pool.wait_ge(sem["pool_step"], w.next("pool_step"))
                pool.tensor_tensor(MB[:, 1, :], m, MB[:, 0, :], ALU.subtract).then_inc(sem["max_parts"], 1)

            def low_unit(slots, k, taken, events):
                pool.wait_ge(sem[taken], w.next(taken, events))
                s = k % slots
                pool.tensor_tensor(PL[:, s, :], PR[:, s, :], top(PR[:, s, :]), ALU.subtract
                                   ).then_inc(sem["low_pool"], 1)

            pool.wait_ge(sem["const_ready"], w.next("const_ready"))
            pool.wait_ge(sem["const_stored"], w.next("const_stored", 48))
            for phase in (1, 2):
                if phase == 2:
                    w.later("qk_raw", 8 * B)
                    w.later("xr_in", 16 * B)
                lows("normed1", "split1", XN, XL)

                def batch(b, looped):
                    for r in range(4):
                        if phase == 1:
                            pool.wait_ge(sem["qk_high"], w.next("qk_high"))
                        else:
                            pool.wait_ge(sem["qk_raw"], w.next("qk_raw", 2))
                        high, low = parts_of(phase, r)
                        pool.tensor_tensor(low, QK[:, r % 2, :], high, ALU.subtract).then_inc(sem["qkp_ready"], 1)
                    if phase == 1:
                        for k in range(2 * NT * KT):
                            low_unit(SLOTS1, k, "s_taken", 1)
                            if k == 2 * NT + 4 and looped:
                                state_low()
                        lows("normed1", "split1", XN, XL)
                        pool.wait_ge(sem["head_taken"], w.next("head_taken", NT * KT))
                    else:
                        split_max(0)
                        split_max(1)
                        for n in range(H):
                            for u in range(NU):
                                if u not in BY_DVE:
                                    low_unit(SLOTS, NU * n + u, "t_taken", 2 if u - 1 in BY_DVE else 1)
                                if u == 0 and 1 <= n and n + 1 < H:
                                    split_max(n + 1)
                            if n == 1 and looped:
                                state_low()
                            if n == 8:
                                pool.wait_ge(sem["xr_in"], w.next("xr_in", 16))
                                for m in range(NT):
                                    i = pool.tensor_tensor(XR[:, m, :], XR[:, m, :], ROW[:, 1, :], ALU.add)
                                i.then_inc(sem["xr_bias"], 1)
                            if 10 <= n <= 13:
                                lows("normed1", "split1", XN, XL, [n - 10])
                        w.later("max_turned", 1)
                        pool.wait_ge(sem["head_taken"], w.next("head_taken", H))
                    pool.tensor_tensor(flat(OL[:, :, :]), flat(ON[:, :, :]), top(flat(ON[:, :, :])), ALU.subtract
                                       ).then_inc(sem["split_o"], 1)
                    lows("normed2", "split2", ON, OL)

                run(pool, w, phase, batch)
                state_low()


_INS = ["L0_attn_a_x", "L0_attn_a_Wq", "L0_attn_a_Wk", "L0_attn_a_Wv", "L0_attn_a_Wo",
        "L0_attn_b_Wq", "L0_attn_b_bq", "L0_attn_b_Wk", "L0_attn_b_bk", "L0_attn_b_Wv", "L0_attn_b_bv",
        "L0_attn_b_Wo", "L0_attn_b_bo", "L0_ffn_wf", "L0_ffn_uf", "L0_ffn_bf", "L0_ffn_wi", "L0_ffn_ui",
        "L0_ffn_bi", "L0_ffn_wc", "L0_ffn_uc", "L0_ffn_bc", "L0_ffn_wo", "L0_ffn_uo", "L0_ffn_bo", "L0_ffn_in_c"]


def kernel(**inputs):
    import numpy as np
    import concourse.bacc as bacc
    from concourse.bass_utils import run_bass_kernel_spmd as launch

    a = {n: np.asarray(inputs[n]) for n in _INS}
    turned = [a[f"L0_attn_a_{n}"].T for n in ("Wq", "Wk", "Wv", "Wo")]
    plain = [a[f"L0_attn_b_{n}"] for n in ("Wq", "Wk", "Wv", "Wo")]
    ffn = [a[f"L0_ffn_{n}"].T for n in ("wf", "uf", "wi", "ui", "wc", "uc", "wo", "uo")]
    col = [a[n].reshape(KT, P).T for n in ("L0_attn_b_bq", "L0_attn_b_bk", "L0_ffn_bf", "L0_ffn_bi", "L0_ffn_bc",
                                           "L0_ffn_in_c")]
    row = [a[n] for n in ("L0_attn_b_bv", "L0_attn_b_bo", "L0_ffn_bo")]
    slope = np.float32(2.0 ** (-8.0 / H)) ** np.arange(1, H + 1, dtype=np.float32)
    bias = slope[:, None] * (np.arange(T, dtype=np.float32) - T // 2)
    parts = []
    for _ in range(3):
        top = ((bias.view(np.uint32) + np.uint32(0x8000)) & np.uint32(0xFFFF0000)).view(np.float32)
        parts.append(top)
        bias = bias - top
    key_rows = np.stack(parts, axis=1).reshape(3 * H, T)
    p, c = np.arange(P)[:, None], np.arange(P)[None, :]
    masks = np.zeros((P, 4 * P + GH * HV), np.float32)
    masks[:, 0:P] = np.where(p == c, 1.0, 0.0)
    masks[:, P:2 * P] = np.where(p > c, NEG, 0.0)
    masks[:, 2 * P:3 * P] = np.where(c > p, NEG, 0.0)
    masks[:, 3 * P:4 * P] = np.where(p <= c, 1.0, 0.0)
    masks[:, 4 * P:] = np.where(p // HD == np.arange(GH * HV)[None, :] // HV, 1.0, 0.0)
    arrays = {
        "in_x": np.ascontiguousarray(a["L0_attn_a_x"]),
        "in_weights": np.ascontiguousarray(np.stack(turned + plain + ffn)),
        "in_cols": np.ascontiguousarray(np.concatenate(col, axis=1)),
        "in_rows": np.ascontiguousarray(np.stack(row)),
        "in_key_rows": np.ascontiguousarray(key_rows),
        "in_masks": masks,
    }
    nc = bacc.Bacc("TRN2", target_bir_lowering=False, num_devices=1)
    args = [nc.dram_tensor(n, v.shape, mybir.dt.from_np(v.dtype), kind="ExternalInput").ap()
            for n, v in arrays.items()]
    args.append(nc.dram_tensor("out_0", (B, T, D), F32, kind="ExternalOutput").ap())
    mixer_kernel(nc, *args)
    r = launch(nc, [arrays], core_ids=[0])
    return r.results[0]["out_0"]
```

```python
from contextlib import ExitStack

import concourse.bass as bass
from concourse import mybir

F32 = mybir.dt.float32
BF16 = mybir.dt.bfloat16
I32 = mybir.dt.int32
ALU = mybir.AluOpType
ACT = mybir.ActivationFunctionType
AX = mybir.AxisListType

P = 128
B, T, D = 8, 1024, 256
H = 16
HD = D // H
NT = T // P
KT = D // P
CH = 512
HV = HD + 1
SLOT = 64
ROWS = 3 * HD
QROWS = ROWS + 3
KROWS = ROWS + 5
PAIRS = H // 2
RING = 4
GH = 8
SLOTS, SLOTS1 = 12, 4
LAG = 4
NEG = -1.0e30
LN_EPS, PHI_EPS, DEN_EPS = 1e-5, 1e-6, 1e-6

MAX_UNITS = []
for i in range(NT - 1, NT // 2 - 1, -1):
    MAX_UNITS.append([(i, 0, 4, 0)])
    rest, other = i - 3, NT - 1 - i
    MAX_UNITS.append([(i, 4, rest, 0)] + ([(other - 1, 0, other, rest)] if other else []))
MAX_UNITS.append([(3, 0, 4, 0)])
EXP_UNITS = [[(0, 0, 4, 0)], [(1, 1, 3, 0), (3, 3, 1, 3)], [(2, 2, 2, 0), (6, 6, 2, 2)]]
EXP_UNITS += [[(j, 4, 4, 0)] for j in range(5)] + [[(5, 5, 3, 0), (7, 7, 1, 3)]]
NU = len(MAX_UNITS)
assert NU == len(EXP_UNITS)


def by_dve(n):
    return (1, 4, 7) if n + 2 < H else (1, 3, 5, 7)

Q_, K_, V_, O_, WF, UF, WI, UI, WC, UC, WO, UO = range(12)
HALF = (UF, UI, UC, UO)
GATES = ((WF, UF), (WI, UI), (WC, UC))
C_BQ, C_BK, C_BF, C_BI, C_BC, C_IN = (2 * n for n in range(6))
SPLIT = ((0, 0), (0, 1), (1, 0))

PER = {
    1: {"act_step": 8, "dve_step": 115, "g_act": 34, "g_dve": 20, "gate": 12, "gate_used": 4, 
        "head_taken": 16, "kt_in": 4, "low_pool": 32, "normed1": 4, "normed2": 4, "pv_done": 32, 
        "qk_high": 4, "qk_raw": 8, "qk_ready": 4, "qkp_ready": 4, "qkp_stored0": 48, "qkp_stored1": 48, 
        "qkp_stored2": 48, "qkp_stored3": 48, "s_full": 32, "s_taken": 32, "sp_log": 4, "split1": 4, 
        "split2": 4, "split_o": 1, "split_o_upper": 1, "stack0": 128, "state_high": 1, "state_split": 1, 
        "sums_in": 6, "sums_split": 1, "v_in": 4, "x_in": 16, "xr_add": 4, "xr_in": 16, "xr_stored": 16, 
        "xt_act": 6, "xt_dve": 6, "xw_out": 4, "xw_stored0": 32, "xw_stored1": 32},
    2: {"dve_step": 93, "g_act": 30, "g_dve": 14, "gate": 12, "gate_used": 4, "head_taken": 16, 
        "low_dve": 50, "low_pool": 94, "max_parts": 16, "max_ready": 16, "max_row": 16, "max_sent0": 128, 
        "max_sent1": 128, "max_turned": 16, "normed1": 4, "normed2": 4, "pool_step": 16, "pv_done": 144, 
        "qk_raw": 8, "qkp_ready": 4, "qkp_stored0": 48, "qkp_stored1": 48, "qkp_stored2": 48, 
        "qkp_stored3": 48, "s_full": 144, "s_taken": 144, "split1": 4, "split2": 4, "split_o": 1, 
        "split_o_upper": 1, "stack0": 128, "stack1": 96, "stack2": 128, "stack3": 96, "state_high": 1, 
        "state_split": 1, "t_full": 144, "t_taken": 144, "v_in": 4, "x_in": 16, "xa_stored": 16, 
        "xi_in0": 32, "xi_in1": 32, "xi_sum": 4, "xi_tanh": 4, "xi_used": 4, "xr_add": 4, "xr_bias": 1, 
        "xr_in": 16, "xr_stored": 16, "xt_act": 6, "xt_dve": 6, "xw_out": 4, "xw_stored0": 32, 
        "xw_stored1": 32},
}


class Counts:

    def __init__(self):
        self.seen, self.entry, self.trip, self.per = {}, None, None, None

    def later(self, name, n=1):
        self.seen[name] = self.seen.get(name, 0) + n
        return name, self.seen[name]

    def at(self, end):
        name, seen = end
        if self.trip is None:
            return seen
        assert seen > self.entry.get(name, 0)
        self.used.add(name)
        return self.trip * self.per.get(name, 0) + seen

    def next(self, name, n=1):
        return self.at(self.later(name, n))

    def open(self, trip, per):
        self.trip, self.per, self.entry, self.used = trip, per, dict(self.seen), set()

    def close(self, trips):
        for name in sorted(self.seen):
            n = self.seen[name] - self.entry.get(name, 0)
            if name in self.used and self.per.get(name) != n:
                print("PER", 1 if self.per is PER[1] else 2, name, n, self.per.get(name))
            self.seen[name] = self.entry.get(name, 0) + trips * n
        self.trip = None


class Ring:

    def __init__(self, depth):
        self.depth, self.ends = depth, []

    def turn(self, end):
        self.ends.append(end)
        return self.ends.pop(0) if len(self.ends) > self.depth else None

    def rest(self):
        ends, self.ends = self.ends, []
        return ends


def mixer_kernel(nc, x, weights, cols, rows, key_rows, masks, out):
    with ExitStack() as ctx:
        def sb(name, shape, dt):
            return ctx.enter_context(nc.sbuf_tensor(name, shape, dt))

        def ps(name, shape, dt):
            return ctx.enter_context(nc.psum_tensor(name, shape, dt))

        sem = {}
        for name in (
            "const_in", "const_ready", "const_stored", "w_in0", "w_in1", "w_split",
            "x_in", "xi_in0", "xi_in1", "xi_sum", "xi_tanh", "xi_used", "xa_stored",
            "normed1", "normed2", "split1", "split2", "split_o", "split_o_upper",
            "g_act", "g_dve", "xt_act", "xt_dve", "qk_raw", "qk_high", "sp_log", "qk_ready", "v_in",
            "qkp_ready", "qkp_stored0", "qkp_stored1", "qkp_stored2", "qkp_stored3",
            "stack0", "stack1", "stack2", "stack3",
            "kt_in", "sums_in", "sums_split",
            "s_full", "s_taken", "t_full", "t_taken", "low_dve", "low_pool", "pv_done", "head_taken",
            "max_ready", "max_parts", "max_turned", "max_row", "max_sent0", "max_sent1",
            "xr_in", "xr_bias", "xr_add", "xr_stored", "xw_out", "xw_stored0", "xw_stored1",
            "gate", "gate_used", "state_high", "state_split", "cu",
            "act_step", "dve_step", "pool_step",
            "held_pe", "held_act", "held_dve", "held_pool", "held_sp",
            "fin_in0", "fin_in1", "fin_sum", "fin_tanh", "fin_done", "fin_out0", "fin_out1",
        ):
            sem[name] = ctx.enter_context(nc.semaphore(name))

        q_dram = nc.dram_tensor("q_stack", (H, KROWS, T), BF16, kind="Internal").ap()
        k_dram = nc.dram_tensor("k_stack", (H, KROWS, T), BF16, kind="Internal").ap()
        x1_dram = nc.dram_tensor("x_after_attention", (B, T, D), F32, kind="Internal").ap()
        x2_dram = nc.dram_tensor("x_after_ffn", (B, T, D), F32, kind="Internal").ap()
        xw_dram = nc.dram_tensor("x_times_wo", (B, T, D), F32, kind="Internal").ap()

        W = [sb(f"w_{part}", [P, 12, KT, D], BF16) for part in ("high", "low")]
        XA = sb("x_for_attention", [P, NT, D], F32)
        XR = sb("x_residual", [P, NT, D], F32)
        XN = sb("ln1", [P, NT, D], F32)
        XL = sb("ln1_low", [P, NT, D], BF16)
        ON = sb("attention_out_or_ln2", [P, NT, D], F32)
        OL = sb("attention_out_or_ln2_low", [P, NT, D], BF16)
        XI = sb("ffn_h", [P, 2, 2 * D], F32)
        XW = sb("x_wo_out", [P, 2, 2 * D], F32)
        XT1 = [sb(f"ln1_o_turned_{part}", [P, KT, T], BF16) for part in ("high", "low")]
        XT2 = [sb(f"ln2_turned_{part}", [P, KT, T], BF16) for part in ("high", "low")]
        V = sb("values", [P, NT, H * 2 * HV], BF16)
        QK = sb("qk_block", [P, 2, T], F32)
        QKP = [sb(f"qk_{part}", [P, 2, T], BF16) for part in ("high", "low")]
        QS = sb("q_stacks", [P, RING, T], BF16)
        KS = sb("k_stacks", [P, RING, T], BF16)
        PR = sb("probs_turned", [P, SLOTS, CH], F32)
        PL = sb("probs_turned_low", [P, SLOTS, CH], BF16)
        MP = sb("maxima", [P, 2, 2 * NT], F32)
        MB = sb("maxima_parts", [P, 2, NT], BF16)
        MR = sb("maxima_rows", [2 * NT, 2, P], BF16)
        NM = sb("numerators", [P, 2, NT, HV], F32)
        REC = sb("reciprocals", [P, 2, NT], F32)
        CS = sb("state_doubled", [P, KT, T], F32)
        CP = [sb(f"state_{part}", [P, KT, T], BF16) for part in ("high", "low")]
        TG = sb("gate_tanhs", [P, 3, CH], F32)
        CU = sb("state_part_of_h", [P, NT, D], F32)
        ST = sb("ln_stats", [P, NT, 6], F32)
        MV = sb("ln_mean_var", [P, NT, 2], F32)
        VE = sb("ln_var_eps", [P, NT], F32)
        NY = sb("ln_newton", [P, NT], F32)
        RS = sb("ln_rstd", [P, NT], F32)
        COL = sb("feature_vectors", [P, 12], F32)
        ROW = sb("row_vectors", [P, 3, D], F32)
        ident = sb("identity", [P, P], BF16)
        mask_t = sb("mask_turned", [P, P], BF16)
        mask_s = sb("mask_scores", [P, P], BF16)
        keep = sb("mask_keep", [P, P], BF16)
        own = sb("mask_own_head", [P, GH * HV], BF16)
        zeros = sb("zeros", [P, GH * 2 * HV], BF16)

        U = CU[:, 0:T // D, :].rearrange("p n d -> p (n d)")
        QF = [PR[:, 4 + 2 * n:6 + 2 * n, :].rearrange("p a b -> p (a b)").bitcast(BF16)
              .rearrange("p (k t) -> p k t", k=KT) for n in range(2)]
        KF = [PR[:, 8 + 2 * n:10 + 2 * n, :].rearrange("p a b -> p (a b)").bitcast(BF16)
              .rearrange("p (n d) -> p n d", n=NT) for n in range(2)]
        SW = GH * HV
        SN = NT - 1
        SF = PL[:, SLOTS1:SLOTS, :].rearrange("p a b -> p (a b)").bitcast(F32)[:, 0:KT * SN * SW].rearrange(
            "p (k c v) -> p k c v", k=KT, c=SN)
        SL = CU[:, T // D:2 * T // D, :].rearrange("p n d -> p (n d)").bitcast(BF16)[:, 0:KT * SN * SW].rearrange(
            "p (k c v) -> p k c v", k=KT, c=SN)

        G = [ps(f"general_{n}", [P, CH], F32) for n in range(2)]
        SB = [ps(f"scores_{n}", [P, CH], F32) for n in range(2)]
        TB = [ps(f"turned_scores_{n}", [P, CH], F32) for n in range(2)]
        OB = [ps(f"out_of_heads_{n}", [P, CH], F32) for n in range(2)]
        STB = SB + TB

        def tokens(t, b):
            return t[b].rearrange("(n p) d -> p n d", p=P)

        def pair(t, c):
            return t[:, 2 * c:2 * c + 2, :].rearrange("p n d -> p (n d)")

        def flat(t):
            return t.rearrange("p a b -> p (a b)")

        def top(columns):
            return columns.bitcast(BF16)[:, 1::2]

        S3 = SB + [G[1]]

        def parts_of(phase, r):
            if phase == 1:
                return [t[:, r // 2, :] for t in (QKP if r % 2 else QF)]
            return [t[:, r % 2, :] for t in QKP]

        def turn_place(n):
            return 2 * NU + n if n < 2 else NU * (n + 1) + 4 * (n + 1 < H) + n

        def score_place(n, u):
            turns = 0 if n < 2 else 2 if n == 2 else n - 1 + (u > 3)
            return NU * n + u + turns

        block = ctx.enter_context(nc.Block())

        def run(eng, w, phase, batch):
            batch(0, False)
            with eng.Fori(0, B - 1) as trip:
                w.open(trip, PER[phase])
                batch(trip + 1, True)
                w.close(B - 1)

        @block.sync
        def _(sp):
            held = sem["held_sp"]
            w = Counts()

            def load_weights(first, rounds, waits_from):
                for r in range(rounds):
                    if r >= waits_from:
                        sp.wait_ge(sem["w_split"], w.next("w_split"))
                    for m in range(2):
                        src = weights[first + 2 * r + m].rearrange("(k p) e -> p k e", p=P)
                        dst = QK[:, r % 2, m * KT * D:(m + 1) * KT * D].rearrange("p (k e) -> p k e", k=KT)
                        sp.dma_start(dst, src).then_inc(sem[f"w_in{r % 2}"], 16)

            def load_xa(phase, b, normed=True, stored=True):
                if normed:
                    sp.wait_ge(sem["normed1"], w.next("normed1", 4))
                    sp.sem_inc(held, 1)
                if phase == 2 and stored:
                    sp.wait_ge(sem["xa_stored"], w.next("xa_stored", 16))
                    sp.sem_inc(held, 1)
                sp.dma_start(XA[:, :, :], tokens(x if phase == 1 else x1_dram, b)).then_inc(sem["x_in"], 16)

            def load_xi(b, chunks):
                for c in chunks:
                    if c >= 2:
                        sp.wait_ge(sem["xi_used"], w.next("xi_used"))
                        sp.sem_inc(held, 1)
                    sp.dma_start(XI[:, c % 2, :].rearrange("p (n d) -> p n d", n=2),
                                 tokens(xw_dram, b)[:, 2 * c:2 * c + 2]).then_inc(sem[f"xi_in{c % 2}"], 16)

            def store_xa(b):
                sp.wait_ge(sem["xi_used"], w.next("xi_used", 2))
                sp.sem_inc(held, 1)
                sp.dma_start(tokens(x2_dram, b), XA[:, :, :]).then_inc(sem["xa_stored"], 16)

            def store_stacks(phase):
                for r in range(4):
                    sp.wait_ge(sem["qkp_ready"], w.next("qkp_ready"))
                    sp.sem_inc(held, 1)
                    dst = (k_dram if r % 2 else q_dram)[8 * (r // 2):8 * (r // 2) + 8]
                    rows_of = ((0, 0), (0, HD), (1, 2 * HD)) if r % 2 else ((0, 0), (1, HD), (0, 2 * HD))
                    for part, at in rows_of:
                        sp.dma_start(dst[:, at:at + HD, :], parts_of(phase, r)[part]
                                     ).then_inc(sem[f"qkp_stored{r}"], 16)

            def stored(half):
                for n in (2 * half, 2 * half + 1):
                    sp.wait_ge(sem[f"qkp_stored{n}"], w.next(f"qkp_stored{n}", 48))
                    sp.sem_inc(held, 1)

            def load_pairs(half):
                stored(half)
                if half:
                    sp.wait_ge(sem["s_taken"], w.next("s_taken", 2 * NT))
                    sp.sem_inc(held, 1)
                for g in range(2):
                    for stack, dram in ((QS, q_dram), (KS, k_dram)):
                        sp.dma_start(stack[SLOT * g:SLOT * g + ROWS, :, :],
                                     dram[GH * half + g:GH * (half + 1):2, 0:ROWS, :].rearrange("h r t -> r h t")
                                     ).then_inc(sem["stack0"], 16)

            def load_heads(first, last, at_once=1):
                for h in range(first, last, at_once):
                    if h % GH == 0:
                        stored(h // GH)
                    if h >= RING:
                        sp.wait_ge(sem["t_taken"], w.next("t_taken", NU))
                        sp.sem_inc(held, 1)
                    s = h % RING
                    for stack, dram in ((QS, q_dram), (KS, k_dram)):
                        sp.dma_start(stack[0:KROWS, s:s + at_once, :],
                                     dram[h:h + at_once].rearrange("h r t -> r h t")).then_inc(sem[f"stack{s}"], 16)

            def store_xw(b):
                for c in range(4):
                    sp.wait_ge(sem["xw_out"], w.next("xw_out"))
                    sp.sem_inc(held, 1)
                    sp.dma_start(tokens(xw_dram, b)[:, 2 * c:2 * c + 2],
                                 XW[:, c % 2, :].rearrange("p (n d) -> p n d", n=2)
                                 ).then_inc(sem[f"xw_stored{c % 2}"], 16)

            def load_xr(phase, b, looped):
                if looped or phase == 2:
                    sp.wait_ge(sem["normed2"], w.next("normed2", 4))
                    sp.sem_inc(held, 1)
                    sp.wait_ge(sem["xr_stored"], w.next("xr_stored", 16))
                    sp.sem_inc(held, 1)
                sp.dma_start(XR[:, :, :], tokens(x if phase == 1 else x2_dram, b)).then_inc(sem["xr_in"], 16)

            def store_xr(b):
                sp.wait_ge(sem["xr_add"], w.next("xr_add", 4))
                sp.sem_inc(held, 1)
                sp.dma_start(tokens(x1_dram, b), XR[:, :, :]).then_inc(sem["xr_stored"], 16)

            sp.dma_start(COL[:, :], cols).then_inc(sem["const_in"], 16)
            sp.dma_start(ROW[:, :, :], rows.partition_broadcast(P)).then_inc(sem["const_in"], 16)
            sp.dma_start(flat(XN[:, 0:3, :])[:, 0:4 * P + SW], masks).then_inc(sem["const_in"], 16)
            sp.dma_start(U[0:3 * H], key_rows).then_inc(sem["const_in"], 16)
            load_weights(0, 2, 2)
            load_xa(1, 0, normed=False)
            load_weights(8, 4, 0)
            sp.wait_ge(sem["w_split"], w.next("w_split", 2))
            sp.wait_ge(sem["const_ready"], w.next("const_ready"))
            sp.dma_start(k_dram[:, ROWS:ROWS + 3, :], QKP[0][0:3 * H, 0, :]).then_inc(sem["const_stored"], 16)
            sp.dma_start(q_dram[:, ROWS:ROWS + 3, :], QKP[1][0:3 * H, 0, :]).then_inc(sem["const_stored"], 16)
            sp.dma_start(k_dram[:, ROWS + 3:ROWS + 5, :], QKP[1][0:2 * H, 1, :]).then_inc(sem["const_stored"], 16)
            sp.dma_start(q_dram[:, ROWS + 3:ROWS + 5, :], QKP[0][0:2 * H, 1, :]).then_inc(sem["const_stored"], 16)
            sp.wait_ge(sem["const_stored"], w.next("const_stored", 64))

            for phase in (1, 2):
                if phase == 2:
                    load_weights(4, 2, 2)
                    sp.wait_ge(sem["w_split"], w.next("w_split", 2))
                    load_xa(2, 0, stored=False)
                    load_xi(0, range(4))
                    store_xa(0)

                def batch(b, looped):
                    load_xa(phase, (b + 1) % B)
                    store_stacks(phase)
                    if phase == 1:
                        load_pairs(0)
                    else:
                        load_heads(0, 4, 2)
                    if looped:
                        store_xw(b - 1)
                    load_xr(phase, b, looped)
                    if phase == 1:
                        load_pairs(1)
                        w.later("s_taken", 2 * NT)
                    else:
                        load_xi((b + 1) % B, range(2))
                        load_heads(4, 7)
                        load_xi((b + 1) % B, [2])
                        load_heads(7, 8)
                        load_xi((b + 1) % B, [3])
                        load_heads(8, 10)
                        store_xa((b + 1) % B)
                        load_heads(10, H)
                        w.later("t_taken", RING * NU)
                    store_xr(b)

                run(sp, w, phase, batch)
                store_xw(B - 1)

            for n in range(2):
                sp.wait_ge(sem[f"xw_stored{n}"], 16 + 2 * 2 * 16 * B)
            sp.wait_ge(sem["xr_stored"], w.next("xr_stored", 16))
            sp.wait_ge(sem["xa_stored"], w.next("xa_stored", 16))
            sp.wait_ge(sem["split1"], 2 * 4 * (B + 1))
            for b in range(B):
                if b >= 2:
                    sp.wait_ge(sem[f"fin_out{b % 2}"], w.next(f"fin_out{b % 2}", 16))
                sp.dma_start((XN, ON)[b % 2][:, :, :], tokens(xw_dram, b)).then_inc(sem[f"fin_in{b % 2}"], 16)
                sp.dma_start((XA, XR)[b % 2][:, :, :], tokens(x1_dram, b)).then_inc(sem[f"fin_in{b % 2}"], 16)
                if b >= 1:
                    sp.wait_ge(sem["fin_done"], w.next("fin_done"))
                    sp.dma_start(tokens(out, b - 1), (XA, XR)[(b - 1) % 2][:, :, :]
                                 ).then_inc(sem[f"fin_out{(b - 1) % 2}"], 16)
            sp.wait_ge(sem["fin_done"], w.next("fin_done"))
            sp.dma_start(tokens(out, B - 1), (XA, XR)[(B - 1) % 2][:, :, :]
                         ).then_inc(sem[f"fin_out{(B - 1) % 2}"], 16)
            for n in range(2):
                sp.wait_ge(sem[f"fin_out{n}"], w.next(f"fin_out{n}", 16))

        @block.tensor
        def _(pe):
            held = sem["held_pe"]
            w = Counts()
            general, scores, turned, both = Ring(2), Ring(3), Ring(2), Ring(4)
            gate_ring = Ring(2)
            place = [0, 0, 0, 0]

            def drain_general():
                for end in general.rest():
                    pe.wait_ge(sem[end[0]], w.at(end))
                    pe.sem_inc(held, 1)

            def general_bank(consumer):
                end = general.turn(w.later(consumer))
                if end:
                    pe.wait_ge(sem[end[0]], w.at(end))
                    pe.sem_inc(held, 1)
                place[0] += 1
                return G[(place[0] - 1) % 2]

            def turn(high, low):
                for part in range(2):
                    for k in range(KT):
                        bank = general_bank(("xt_act", "xt_dve")[k])[:, :].bitcast(BF16)
                        for n in range(NT):
                            at = slice(k * P, (k + 1) * P)
                            src = low[:, n, at] if part else top(high[:, n, at])
                            mm = pe.transpose(bank[:, n * P:(n + 1) * P], src, ident[:, :])
                        mm.then_inc(sem[("g_act", "g_dve")[k]], 1)
                drain_general()

            def by_feature(bank, terms, e):
                todo = [(m, k, wp, xp, src, t0) for m, src, t0 in terms for k in range(KT) for wp, xp in SPLIT]
                for n, (m, k, wp, xp, src, t0) in enumerate(todo):
                    mm = pe.matmul(bank[:, :], W[wp][:, m, k, e * P:(e + 1) * P], src[xp][:, k, t0:t0 + CH],
                                   start=(n == 0), stop=(n == len(todo) - 1))
                return mm

            def by_token(bank, m, src, c):
                for n in range(2):
                    t0 = (2 * c + n) * P
                    todo = [(k, xp, wp) for k in range(KT) for xp, wp in SPLIT]
                    for i, (k, xp, wp) in enumerate(todo):
                        mm = pe.matmul(bank[:, n * D:(n + 1) * D], src[xp][:, k, t0:t0 + P], W[wp][:, m, k, :],
                                       start=(i == 0), stop=(i == len(todo) - 1))
                return mm

            def project():
                for e in range(2):
                    for m in (Q_, K_):
                        for c in range(2):
                            by_feature(general_bank("qk_raw"), [(m, XT1, c * CH)], e).then_inc(sem["g_act"], 1)
                    for c in (2 * e, 2 * e + 1):
                        by_token(general_bank("v_in"), V_, XT1, c).then_inc(sem["g_dve"], 1)

            def turn_ln2():
                pe.wait_ge(sem["split2"], w.next("split2", 4))
                pe.sem_inc(held, 1)
                turn(ON, OL)
                for c in range(4):
                    by_token(general_bank("xw_out"), WO, XT2, c).then_inc(sem["g_act"], 1)

            def gate_piece(unit, bank, first, last):
                group, g = unit // 3, unit % 3
                e, c = group % 2, group // 2
                wm, um = GATES[g]
                todo = [(m, k, wp, xp, src) for m, src in ((wm, XT2), (um, CP)) for k in range(KT) for wp, xp in SPLIT]
                if unit == 0 and first == 0:
                    pe.wait_ge(sem["state_split"], w.next("state_split"))
                    pe.sem_inc(held, 1)
                for n in range(first, last):
                    m, k, wp, xp, src = todo[n]
                    mm = pe.matmul(bank[:, :], W[wp][:, m, k, e * P:(e + 1) * P], src[xp][:, k, c * CH:(c + 1) * CH],
                                   start=(n == 0), stop=(n == len(todo) - 1))
                if last == len(todo):
                    mm.then_inc(sem["g_act"], 1)

            def gates_between(unit, piece, pieces, banks):
                if piece == 0:
                    gate_ring.depth = banks
                    end = gate_ring.turn(w.later("gate"))
                    if end:
                        pe.wait_ge(sem[end[0]], w.at(end))
                gate_piece(unit, G[unit % banks], 12 * piece // pieces, 12 * (piece + 1) // pieces)

            def sums():
                for n in range(4):
                    pe.wait_ge(sem["qkp_ready"], w.next("qkp_ready"))
                    pe.sem_inc(held, 1)
                for part in range(2):
                    for e in range(KT):
                        bank = general_bank("kt_in")[:, :].bitcast(BF16)
                        for n in range(NT):
                            mm = pe.transpose(bank[:, n * P:(n + 1) * P], QKP[part][:, e, n * P:(n + 1) * P],
                                              ident[:, :])
                        mm.then_inc(sem["g_act"], 1)
                drain_general()
                for e in range(KT):
                    for first in range(0, SN, 3):
                        bank = general_bank("sums_in")
                        for c in range(first, min(first + 3, SN)):
                            dst = bank[:, (c - first) * SW:(c - first + 1) * SW].rearrange("p (h v) -> p h v", v=HV)
                            v = V[:, c, :].rearrange("p (h a v) -> p h a v", a=2, v=HV)[:, GH * e:GH * (e + 1)]
                            for n, (kp, vp) in enumerate(SPLIT):
                                mm = pe.matmul(dst, KF[kp][:, c, e * P:(e + 1) * P], v[:, :, vp, :],
                                               start=(n == 0), stop=(n == 2))
                        mm.then_inc(sem["g_dve"], 1)

            def own_unit(k):
                c, g = k // 2 % NT, k % 2
                if c == 0 and g == 0:
                    pe.wait_ge(sem["stack0"], w.next("stack0", 64))
                    pe.sem_inc(held, 1)
                end = both.turn(w.later("s_taken"))
                if end:
                    pe.wait_ge(sem[end[0]], w.at(end))
                    pe.sem_inc(held, 1)
                bank = STB[place[3] % 4]
                place[3] += 1
                for i in range(4):
                    at = SLOT * g
                    mm = pe.matmul(bank[:, i * P:(i + 1) * P], KS[at:at + ROWS, i, c * P:(c + 1) * P],
                                   QS[at:at + ROWS, i, c * P:(c + 1) * P], start=True, stop=True)
                mm.then_inc(sem["s_full"], 1)

            def own_out(k):
                e, c, g = k // (2 * NT), k // 2 % NT, k % 2
                bank = OB[c % 2]
                if g == 0:
                    if NT * e + c >= 2:
                        pe.wait_ge(sem["head_taken"], w.next("head_taken"))
                        pe.sem_inc(held, 1)
                    pe.matmul(bank[:, 0:2 * SW], ident[:, :], zeros[:, :], start=True, stop=False)
                    if c:
                        q_out = bank[:, 0:2 * SW].rearrange("p (h a v) -> p h a v", a=2, v=HV)[:, :, 0, :]
                        for qp, sp_ in SPLIT:
                            src = SL[:, e, c - 1, :] if sp_ else top(SF[:, e, c - 1, :])
                            pe.matmul(q_out, QF[qp][:, e, c * P:(c + 1) * P],
                                      src.rearrange("p (h v) -> p h v", v=HV), start=False, stop=False)
                pe.wait_ge(sem["low_pool"], w.next("low_pool"))
                s = k % SLOTS1
                for i in range(4):
                    h = 2 * i + g
                    at, v = 2 * HV * h, 2 * HV * (GH * e + h)
                    pe.matmul(bank[:, at:at + 2 * HV], top(PR[:, s, i * P:(i + 1) * P]), V[:, c, v:v + 2 * HV],
                              start=False, stop=False)
                    mm = pe.matmul(bank[:, at:at + HV], PL[:, s, i * P:(i + 1) * P], V[:, c, v:v + HV],
                                   start=False, stop=(g == 1 and i == 3))
                mm.then_inc(sem["pv_done"], 1)

            def linear_attention(looped):
                drain_general()
                units, half = 2 * NT * KT, 2 * NT
                for k in range(units):
                    if k == half:
                        own_out(k - 2)
                        own_out(k - 1)
                    own_unit(k)
                    if k == 1:
                        pe.wait_ge(sem["sums_split"], w.next("sums_split"))
                        pe.sem_inc(held, 1)
                    if k >= 2 and not half <= k < half + 2:
                        own_out(k - 2)
                    if looped and 4 <= k < 28:
                        gates_between((k - 4) // 2, k % 2, 2, 2)
                for j in range(units - 2, units):
                    own_out(j)
                w.later("head_taken", 2)
                both.rest()
                for end in gate_ring.rest():
                    pe.wait_ge(sem[end[0]], w.at(end))
                    pe.sem_inc(held, 1)

            def max_unit(n, u):
                r = n % RING
                if u == 0 and n not in (1, 3):
                    pe.wait_ge(sem[f"stack{r}"], w.next(f"stack{r}", 32))
                end = scores.turn(w.later("s_taken"))
                if end:
                    pe.wait_ge(sem[end[0]], w.at(end))
                bank = S3[place[1] % 3]
                place[1] += 1
                for i, k0, tiles, first in MAX_UNITS[u]:
                    diag = k0 + tiles == i + 1
                    mm = pe.matmul(bank[:, first * P:(first + tiles) * P],
                                   QS[:, r, i * P:(i + 1) * P], KS[:, r, k0 * P:(k0 + tiles) * P],
                                   start=True, stop=not diag)
                    if diag:
                        mm = pe.matmul(bank[:, (first + tiles - 1) * P:(first + tiles) * P], ident[:, :],
                                       mask_s[:, :], start=False, stop=True)
                mm.then_inc(sem["s_full"], 1)

            def turn_max(n):
                pe.wait_ge(sem["max_parts"], w.next("max_parts"))
                pe.sem_inc(held, 1)
                end = scores.turn(w.later("max_row"))
                if end:
                    pe.wait_ge(sem[end[0]], w.at(end))
                    pe.sem_inc(held, 1)
                bank = S3[place[1] % 3]
                place[1] += 1
                pe.transpose(bank[0:2 * NT, 0:P // 2].bitcast(BF16), flat(MB[:, :, :]), ident[:, :]
                             ).then_inc(sem["max_turned"], 1)

            def exp_unit(n, u):
                r = n % RING
                if u == 0:
                    pe.wait_ge(sem[f"max_sent{n % 2}"], w.next(f"max_sent{n % 2}", 16))
                end = turned.turn(w.later("t_taken"))
                if end:
                    pe.wait_ge(sem[end[0]], w.at(end))
                bank = TB[place[2] % 2]
                place[2] += 1
                for j, i0, tiles, first in EXP_UNITS[u]:
                    diag = i0 == j
                    mm = pe.matmul(bank[:, first * P:(first + tiles) * P],
                                   KS[:, r, j * P:(j + 1) * P], QS[:, r, i0 * P:(i0 + tiles) * P],
                                   start=True, stop=not diag)
                    if diag:
                        mm = pe.matmul(bank[:, first * P:(first + 1) * P], ident[:, :], mask_t[:, :],
                                       start=False, stop=True)
                mm.then_inc(sem["t_full"], 1)

            def values_unit(n, u):
                bank = OB[n % 2]
                if u == 0:
                    if n >= 2:
                        pe.wait_ge(sem["head_taken"], w.next("head_taken"))
                        pe.sem_inc(held, 1)
                    pe.matmul(bank[:, 0:2 * SW], ident[:, :], zeros[:, :], start=True, stop=False)
                if u in by_dve(n):
                    pe.wait_ge(sem["low_dve"], w.next("low_dve"))
                else:
                    pe.wait_ge(sem["low_pool"], w.next("low_pool"))
                s = (NU * n + u) % SLOTS
                for j, i0, tiles, first in EXP_UNITS[u]:
                    for i in range(tiles):
                        at, cols_ = 2 * HV * (i0 + i), slice((first + i) * P, (first + i + 1) * P)
                        pe.matmul(bank[:, at:at + 2 * HV], top(PR[:, s, cols_]),
                                  V[:, j, 2 * HV * n:2 * HV * (n + 1)], start=False, stop=False)
                        last = u == NU - 1 and first + i == 3
                        mm = pe.matmul(bank[:, at:at + HV], PL[:, s, cols_],
                                       V[:, j, 2 * HV * n:2 * HV * n + HV], start=False, stop=last)
                mm.then_inc(sem["pv_done"], 1)

            def softmax_attention(looped):
                for k in range(H * NU + LAG):
                    n, u = k // NU, k % NU
                    if n + 2 < H:
                        max_unit(n + 2, u)
                    if n < H:
                        exp_unit(n, u)
                    if k >= LAG:
                        values_unit((k - LAG) // NU, (k - LAG) % NU)
                    if u == 3 and 1 <= n and n + 1 < H:
                        turn_max(n + 1)
                    if looped and 1 <= n <= 12 and 1 <= u <= 6:
                        gates_between(n - 1, u - 1, 6, 1)
                w.later("head_taken", 2)
                for end in gate_ring.rest():
                    pe.wait_ge(sem[end[0]], w.at(end))
                    pe.sem_inc(held, 1)
                scores.rest()
                turned.rest()

            def output():
                for half in ("split_o", "split_o_upper"):
                    pe.wait_ge(sem[half], w.next(half))
                    pe.sem_inc(held, 1)
                turn(ON, OL)
                for c in range(4):
                    by_token(general_bank("xr_add"), O_, XT1, c).then_inc(sem["g_dve"], 1)
                drain_general()

            pe.wait_ge(sem["const_ready"], w.next("const_ready"))
            pe.wait_ge(sem["w_split"], w.next("w_split", 6))

            for phase in (1, 2):
                if phase == 2:
                    pe.wait_ge(sem["w_split"], w.next("w_split", 2))

                def batch(b, looped):
                    pe.wait_ge(sem["split1"], w.next("split1", 4))
                    pe.sem_inc(held, 1)
                    turn(XN, XL)
                    project()
                    if looped:
                        turn_ln2()
                    if phase == 1:
                        sums()
                        linear_attention(looped)
                    else:
                        drain_general()
                        place[1] = 0
                        for n in range(2):
                            for u in range(NU):
                                max_unit(n, u)
                        turn_max(0)
                        turn_max(1)
                        softmax_attention(looped)
                    output()

                run(pe, w, phase, batch)
                w.later("split1", 4)
                turn_ln2()
                for unit in range(12):
                    gate_piece(unit, general_bank("gate"), 0, 12)
                pe.wait_ge(sem["state_split"], w.next("state_split"))
                for c in range(4):
                    by_token(general_bank("cu"), UO, CP, c).then_inc(sem["g_dve"], 1)
                drain_general()

        @block.scalar
        def _(act):
            held = sem["held_act"]
            w = Counts()
            place = [0, 0]

            def step(instruction):
                instruction.then_inc(sem["act_step"], 1)
                act.wait_ge(sem["act_step"], w.next("act_step"))

            def taken_bank():
                act.wait_ge(sem["g_act"], w.next("g_act"))
                place[0] += 1
                return G[(place[0] - 1) % 2][:, :]

            def turned_copy(dst):
                for part in range(2):
                    nc.scalar.copy(dst[part][:, 0, :], taken_bank().bitcast(BF16)).then_inc(sem["xt_act"], 1)
                    place[0] += 1

            def project(phase):
                def high(r):
                    act.wait_ge(sem["qk_ready"], w.next("qk_ready"))
                    nc.scalar.copy(parts_of(1, r)[0], QK[:, r % 2, :]).then_inc(sem["qk_high"], 1)

                for r in range(4):
                    if r >= 2:
                        act.wait_ge(sem["qkp_ready"], w.next("qkp_ready"))
                        if phase == 2:
                            act.wait_ge(sem[f"qkp_stored{r - 2}"], w.next(f"qkp_stored{r - 2}", 48))
                            act.sem_inc(held, 1)
                    for c in range(2):
                        at = slice(c * CH, (c + 1) * CH)
                        src = taken_bank()
                        if phase == 1:
                            nc.scalar.copy(QK[:, r % 2, at], src).then_inc(sem["qk_raw"], 1)
                        else:
                            bias = (C_BK if r % 2 else C_BQ) + r // 2
                            nc.scalar.activation(QK[:, r % 2, at], src, ACT.Identity, bias=COL[:, bias:bias + 1])
                            nc.scalar.activation(QKP[0][:, r % 2, at], src, ACT.Identity,
                                                 bias=COL[:, bias:bias + 1]).then_inc(sem["qk_raw"], 1)
                    if phase == 1:
                        if r:
                            high(r - 1)
                        act.wait_ge(sem["qk_raw"], w.next("qk_raw", 2))
                        step(nc.scalar.activation(U, QK[:, r % 2, :], ACT.Abs))
                        step(nc.scalar.activation(U, U, ACT.Exp, scale=-1.0))
                        nc.scalar.activation(U, U, ACT.Ln, bias=1.0).then_inc(sem["sp_log"], 1)
                    if r % 2:
                        place[0] += 2
                if phase == 1:
                    high(3)
                w.later("qkp_ready", 2)
                if phase == 1:
                    for n in range(2):
                        w.later(f"qkp_stored{n}", 48)

            def turned_ln2():
                turned_copy(XT2)
                for c in range(4):
                    act.wait_ge(sem[f"xw_stored{c % 2}"], w.next(f"xw_stored{c % 2}", 16))
                    nc.scalar.copy(XW[:, c % 2, :], taken_bank()).then_inc(sem["xw_out"], 1)

            def gate_tanh(unit, bank=None):
                group, g = unit // 3, unit % 3
                if group and g == 0:
                    act.wait_ge(sem["gate_used"], w.next("gate_used"))
                if bank is None:
                    bank = taken_bank()
                else:
                    act.wait_ge(sem["g_act"], w.next("g_act"))
                at = (C_BF, C_BI, C_BC)[g] + group % 2
                nc.scalar.activation(TG[:, g, :], bank, ACT.Tanh,
                                     bias=COL[:, at:at + 1], scale=1.0 if g == 2 else 0.5
                                     ).then_inc(sem["gate"], 1)

            def state_high():
                act.wait_ge(sem["gate_used"], w.next("gate_used"))
                nc.scalar.copy(flat(CP[0][:, :, :]), flat(CS[:, :, :])).then_inc(sem["state_high"], 1)

            def keys_by_token():
                for part in range(2):
                    for e in range(KT):
                        nc.scalar.copy(KF[part][:, :, e * P:(e + 1) * P],
                                       taken_bank().bitcast(BF16).rearrange("p (n d) -> p n d", n=NT)
                                       ).then_inc(sem["kt_in"], 1)
                place[0] += KT * -(-SN // 3)

            def send_max(n):
                act.wait_ge(sem["max_turned"], w.next("max_turned"))
                bank = S3[turn_place(n) % 3]
                nc.scalar.copy(MR[:, n % 2, :], bank[0:2 * NT, 0:P // 2].bitcast(BF16)).then_inc(sem["max_row"], 1)

            def send_max_rows(n):
                act.wait_ge(sem["max_row"], w.next("max_row"))
                act.dma_start(QS[QROWS:KROWS, n % RING, :].rearrange("a (b c) -> a b c", c=P), MR[:, n % 2, :]
                              ).then_inc(sem[f"max_sent{n % 2}"], 16)

            def exp_unit(n, u):
                k = NU * n + u
                if k >= SLOTS:
                    act.wait_ge(sem["pv_done"], w.next("pv_done"))
                act.wait_ge(sem["t_full"], w.next("t_full"))
                nc.scalar.activation(PR[:, k % SLOTS, :], TB[place[1] % 2][:, :], ACT.Exp).then_inc(sem["t_taken"], 1)
                place[1] += 1

            def h_tanh(c):
                act.wait_ge(sem["xi_sum"], w.next("xi_sum"))
                nc.scalar.activation(XI[:, c % 2, :], XI[:, c % 2, :], ACT.Tanh).then_inc(sem["xi_tanh"], 1)

            for c in range(2):
                act.sem_inc(sem[f"xw_stored{c}"], 16)
            act.wait_ge(sem["const_ready"], w.next("const_ready"))
            act.wait_ge(sem["const_stored"], w.next("const_stored", 64))
            for phase in (1, 2):
                if phase == 2:
                    for c in range(4):
                        h_tanh(c)

                def batch(b, looped):
                    turned_copy(XT1)
                    if phase == 1:
                        act.preload_act_table_set("natural_log_exp_and_others")
                    project(phase)
                    if looped:
                        turned_ln2()
                    if phase == 1:
                        keys_by_token()
                    if looped and phase == 1:
                        for unit in range(12):
                            gate_tanh(unit, G[unit % 2][:, :])
                        state_high()
                    if phase == 2:
                        for n in range(2):
                            send_max(n)
                            send_max_rows(n)
                    if phase == 2:
                        for n in range(H):
                            if 2 <= n <= 5:
                                h_tanh(n - 2)
                            if n == 14 and looped:
                                state_high()
                            for u in range(NU):
                                exp_unit(n, u)
                                if u == 7 and looped and 1 <= n <= 12:
                                    gate_tanh(n - 1, G[0][:, :])
                                if u == 4 and 1 <= n and n + 1 < H:
                                    send_max(n + 1)
                                if u == 5 and 1 <= n and n + 1 < H:
                                    send_max_rows(n + 1)
                        w.later("pv_done", SLOTS)
                    turned_copy(XT1)
                    place[0] += 4

                if phase == 2:
                    w.later("pv_done", 2 * NT * KT * B)
                run(act, w, phase, batch)
                turned_ln2()
                for unit in range(12):
                    gate_tanh(unit)
                state_high()
                place[0] += 4
            for b in range(B):
                act.wait_ge(sem["fin_sum"], w.next("fin_sum"))
                a = flat((XN, ON)[b % 2][:, :, :])
                nc.scalar.activation(a, a, ACT.Tanh).then_inc(sem["fin_tanh"], 1)

        @block.vector
        def _(dve):
            held = sem["held_dve"]
            w = Counts()
            place = [0, 0]

            def step(instruction):
                instruction.then_inc(sem["dve_step"], 1)
                dve.wait_ge(sem["dve_step"], w.next("dve_step"))

            def taken_bank():
                dve.wait_ge(sem["g_dve"], w.next("g_dve"))
                place[0] += 1
                return G[(place[0] - 1) % 2][:, :]

            def turned_copy(dst):
                for part in range(2):
                    place[0] += 1
                    dve.tensor_copy(dst[part][:, 1, :], taken_bank().bitcast(BF16)).then_inc(sem["xt_dve"], 1)

            def second_norm_stats():
                dve.wait_ge(sem["xr_add"], w.next("xr_add", 4))
                stats(XR, range(NT))

            def second_norm():
                aggregate()
                for c in range(4):
                    normalise(XR, ON, c, "normed2")

            def project(phase, looped):
                for e in range(2):
                    place[0] += 4
                    if phase == 1:
                        for r in (2 * e, 2 * e + 1):
                            dve.wait_ge(sem["sp_log"], w.next("sp_log"))
                            t = QK[:, r % 2, :]
                            step(dve.tensor_scalar(t, t, 0.0, PHI_EPS, ALU.max, ALU.add))
                            dve.tensor_tensor(t, t, U, ALU.add).then_inc(sem["qk_ready"], 1)
                    for c in (2 * e, 2 * e + 1):
                        bank = taken_bank()
                        if phase == 2:
                            step(dve.tensor_tensor(PR[:, c % 2, :].rearrange("p (n d) -> p n d", n=2),
                                                   bank.rearrange("p (n d) -> p n d", n=2),
                                                   ROW[:, 0:1, :].broadcast_to([P, 2, D]), ALU.add))
                            bank = PR[:, c % 2, :]
                        for n in range(2):
                            src = bank[:, n * D:(n + 1) * D].rearrange("p (h v) -> p h v", h=H)
                            dst = V[:, 2 * c + n, :].rearrange("p (h a v) -> p h a v", a=2, v=HV)[:, :, :, 0:HD]
                            step(dve.tensor_copy(dst[:, :, 0, :], src))
                            i = dve.tensor_tensor(dst[:, :, 1, :], src, dst[:, :, 0, :], ALU.subtract)
                        i.then_inc(sem["v_in"], 1)
                    if e == 0 and looped:
                        second_norm()

            def gates(group):
                e, c = group % 2, group // 2
                dve.wait_ge(sem["gate"], w.next("gate", 3))
                cs = CS[:, e, c * CH:(c + 1) * CH]
                dve.scalar_tensor_tensor(out=TG[:, 0, :], in0=TG[:, 0, :], scalar=1.0, in1=cs,
                                         op0=ALU.add, op1=ALU.mult)
                step(dve.scalar_tensor_tensor(out=TG[:, 1, :], in0=TG[:, 1, :], scalar=1.0, in1=TG[:, 2, :],
                                              op0=ALU.add, op1=ALU.mult))
                dve.scalar_tensor_tensor(out=cs, in0=TG[:, 0, :], scalar=0.5, in1=TG[:, 1, :],
                                         op0=ALU.mult, op1=ALU.add).then_inc(sem["gate_used"], 1)

            def sums():
                place[0] += 4
                for e in range(KT):
                    for first in range(0, SN, 3):
                        n = min(3, SN - first)
                        dve.tensor_tensor(SF[:, e, first:first + n, :],
                                          taken_bank()[:, 0:n * SW].rearrange("p (c v) -> p c v", c=n),
                                          own[:, :].rearrange("p (c v) -> p c v", c=1).broadcast_to([P, n, SW]),
                                          ALU.mult).then_inc(sem["sums_in"], 1)
                dve.wait_ge(sem["sums_in"], w.next("sums_in", KT * -(-SN // 3)))
                for c in range(1, SN):
                    step(dve.tensor_tensor(SF[:, :, c, :], SF[:, :, c, :], SF[:, :, c - 1, :], ALU.add))
                for e in range(KT):
                    src = SF[:, e].rearrange("p c v -> p (c v)")
                    i = dve.tensor_tensor(SL[:, e].rearrange("p c v -> p (c v)"), src, top(src), ALU.subtract)
                i.then_inc(sem["sums_split"], 1)

            def mask_unit(k):
                if k % (2 * NT) >= SLOTS1:
                    dve.wait_ge(sem["pv_done"], w.next("pv_done"))
                    dve.sem_inc(held, 1)
                dve.wait_ge(sem["s_full"], w.next("s_full"))
                dve.tensor_tensor(PR[:, k % SLOTS1, :].rearrange("p (a b) -> p a b", a=4),
                                  STB[place[1] % 4][:, :].rearrange("p (a b) -> p a b", a=4),
                                  keep[:, :].rearrange("p (a b) -> p a b", a=1).broadcast_to([P, 4, P]),
                                  ALU.mult).then_inc(sem["s_taken"], 1)
                place[1] += 1

            def take_chunk(e, c):
                src = OB[c % 2][:, 0:2 * SW].rearrange("p (h a v) -> p h a v", a=2, v=HV)
                num, rec = NM[:, c % 2], REC[:, c % 2, :]
                step(dve.tensor_copy(num, src[:, :, 0, :]))
                step(dve.tensor_tensor(num, num, src[:, :, 1, :], ALU.add))
                step(dve.tensor_scalar(rec, num[:, :, HD], DEN_EPS, None, ALU.add))
                step(dve.reciprocal(rec, rec))
                dve.tensor_tensor(ON[:, c, e * P:(e + 1) * P].rearrange("p (h v) -> p h v", h=GH), num[:, :, 0:HD],
                                  rec.rearrange("p (n a) -> p n a", a=1).broadcast_to([P, GH, HD]), ALU.mult
                                  ).then_inc(sem["head_taken"], 1)

            def max_unit(n, u):
                if u == 0:
                    if n >= 2:
                        dve.wait_ge(sem["max_parts"], w.next("max_parts"))
                        dve.sem_inc(held, 1)
                dve.wait_ge(sem["s_full"], w.next("s_full"))
                bank = S3[score_place(n, u) % 3]
                for i, k0, tiles, first in MAX_UNITS[u]:
                    at = i + (NT if k0 else 0)
                    r = dve.tensor_reduce(MP[:, n % 2, at:at + 1], bank[:, first * P:(first + tiles) * P],
                                          AX.X, ALU.max)
                r.then_inc(sem["s_taken"], 1)
                if u == NU - 1:
                    dve.wait_ge(sem["s_taken"], w.next("s_taken", NU))
                    m = MP[:, n % 2, :]
                    dve.tensor_tensor(m[:, NT // 2:NT], m[:, NT // 2:NT], m[:, NT + NT // 2:2 * NT], ALU.max
                                      ).then_inc(sem["max_ready"], 1)

            def low_unit(n, u):
                skipped = u - max([-1] + [d for d in by_dve(n) if d < u])
                dve.wait_ge(sem["t_taken"], w.next("t_taken", skipped))
                s = (NU * n + u) % SLOTS
                dve.tensor_tensor(PL[:, s, :], PR[:, s, :], top(PR[:, s, :]), ALU.subtract
                                  ).then_inc(sem["low_dve"], 1)

            def take_head(n):
                dve.wait_ge(sem["pv_done"], w.next("pv_done", NU))
                dve.sem_inc(held, 1)
                src = OB[n % 2][:, 0:2 * SW].rearrange("p (n a v) -> p n a v", a=2, v=HV)
                num, rec = NM[:, n % 2], REC[:, n % 2, :]
                step(dve.tensor_copy(num, src[:, :, 0, :]))
                step(dve.tensor_tensor(num, num, src[:, :, 1, :], ALU.add))
                step(dve.reciprocal(rec, num[:, :, HD]))
                dve.tensor_tensor(ON[:, :, HD * n:HD * (n + 1)], num[:, :, 0:HD],
                                  rec.rearrange("p (n a) -> p n a", a=1).broadcast_to([P, NT, HD]), ALU.mult
                                  ).then_inc(sem["head_taken"], 1)

            def stats(src, tiles):
                for n in tiles:
                    i = dve.bn_stats(ST[:, n, :], src[:, n, :])
                step(i)
                dve.sem_inc(held, 1)

            def aggregate():
                for n in range(NT):
                    i = dve.bn_aggr(MV[:, n, :], ST[:, n, :])
                step(i)
                step(dve.tensor_scalar(VE[:, :], MV[:, :, 1], LN_EPS, None, ALU.add))
                step(dve.tensor_scalar(RS[:, :].bitcast(I32), VE[:, :].bitcast(I32), 1, None,
                                       ALU.logical_shift_right))
                step(dve.tensor_scalar(RS[:, :].bitcast(I32), RS[:, :].bitcast(I32), -1.0, float(0x5F3759DF),
                                       ALU.mult, ALU.add))
                for _ in range(3):
                    step(dve.tensor_tensor(NY[:, :], RS[:, :], RS[:, :], ALU.mult))
                    step(dve.scalar_tensor_tensor(out=NY[:, :], in0=NY[:, :], scalar=-0.5, in1=VE[:, :],
                                                  op0=ALU.mult, op1=ALU.mult))
                    step(dve.scalar_tensor_tensor(out=RS[:, :], in0=NY[:, :], scalar=1.5, in1=RS[:, :],
                                                  op0=ALU.add, op1=ALU.mult))

            def normalise(src, dst, c, normed):
                for t in (2 * c, 2 * c + 1):
                    i = dve.tensor_scalar(dst[:, t, :], src[:, t, :], MV[:, t, 0:1], RS[:, t:t + 1],
                                          ALU.subtract, ALU.mult)
                i.then_inc(sem[normed], 1)

            def h_sum(c):
                dve.wait_ge(sem[f"xi_in{c % 2}"], w.next(f"xi_in{c % 2}", 16))
                dve.tensor_tensor(XI[:, c % 2, :], XI[:, c % 2, :], pair(CU, c), ALU.add
                                  ).then_inc(sem["xi_sum"], 1)

            def h_add(c):
                if c == 0:
                    dve.wait_ge(sem["x_in"], w.next("x_in", 16))
                dve.wait_ge(sem["xi_tanh"], w.next("xi_tanh"))
                dve.tensor_tensor(pair(XA, c), pair(XA, c), XI[:, c % 2, :], ALU.add).then_inc(sem["xi_used"], 1)

            def front(phase, n):
                if phase == 2:
                    if 1 <= n <= 4:
                        h_sum(n - 1)
                    if 2 <= n <= 5:
                        h_add(n - 2)
                if n == 6:
                    if phase == 1:
                        dve.wait_ge(sem["x_in"], w.next("x_in", 16))
                    else:
                        dve.wait_ge(sem["xi_used"], w.next("xi_used", 4))
                    stats(XA, range(4))
                if n == 7:
                    stats(XA, range(4, NT))
                if n == 8:
                    aggregate()
                if 9 <= n <= 12:
                    normalise(XA, XN, n - 9, "normed1")

            dve.wait_ge(sem["const_in"], w.next("const_in", 64))
            dve.memset(V[:, :, :], 0.0).then_inc(sem["dve_step"], 1)
            dve.wait_ge(sem["dve_step"], w.next("dve_step"))
            dve.memset(V[:, :, :].rearrange("p n (h v) -> p (n h) v", v=2 * HV)[:, :, HD:HD + 1], 1.0)
            dve.memset(zeros[:, :], 0.0)
            dve.memset(QKP[1][0:3 * H, 0, :], 1.0)
            dve.memset(QKP[1][0:2 * H, 1, :], -1.0)
            dve.memset(QKP[0][0:2 * H, 1, :], 0.0)
            dve.tensor_copy(QKP[0][0:3 * H, 0, :], U[0:3 * H])
            stage = flat(XN[:, 0:3, :])
            for n, t in enumerate((ident, mask_t, mask_s, keep)):
                dve.tensor_copy(t[:, :], stage[:, n * P:(n + 1) * P])
            dve.tensor_copy(own[:, :], stage[:, 4 * P:4 * P + SW])
            dve.tensor_scalar(COL[:, C_BQ:C_BQ + 2], COL[:, C_BQ:C_BQ + 2], HD ** -0.5, None, ALU.mult)
            dve.tensor_scalar(COL[:, C_BF:C_BF + 4], COL[:, C_BF:C_BF + 4], 0.5, None, ALU.mult)
            dve.tensor_scalar(COL[:, C_IN:C_IN + 2], COL[:, C_IN:C_IN + 2], 2.0, None, ALU.mult
                              ).then_inc(sem["const_ready"], 1)
            dve.wait_ge(sem["const_ready"], w.next("const_ready"))

            def split_weights(first, rounds, slot):
                for r in range(rounds):
                    dve.wait_ge(sem[f"w_in{r % 2}"], w.next(f"w_in{r % 2}", 32))
                    for m in range(2):
                        s = slot + 2 * r + m
                        stage = QK[:, r % 2, m * KT * D:(m + 1) * KT * D]
                        scale = 0.5 if s in HALF else HD ** -0.5 if first == 4 and s == Q_ else None
                        if scale is not None:
                            step(dve.tensor_scalar(stage, stage, scale, None, ALU.mult))
                    stage = QK[:, r % 2, :]
                    s = slot + 2 * r
                    high = W[0][:, s:s + 2].rearrange("p m k e -> p (m k e)")
                    low = W[1][:, s:s + 2].rearrange("p m k e -> p (m k e)")
                    step(dve.tensor_copy(high, stage))
                    dve.tensor_tensor(low, stage, high, ALU.subtract).then_inc(sem["w_split"], 1)

            def set_state():
                step(dve.memset(CS[:, :, :], 0.0))
                for k in range(KT):
                    i = dve.tensor_scalar(CS[:, k, :], CS[:, k, :], COL[:, C_IN + k:C_IN + k + 1], None, ALU.add)
                step(i)
                step(dve.tensor_copy(CP[0][:, :, :], CS[:, :, :]))
                dve.tensor_tensor(CP[1][:, :, :], CS[:, :, :], CP[0][:, :, :], ALU.subtract
                                  ).then_inc(sem["state_split"], 1)

            split_weights(0, 2, 0)
            split_weights(8, 4, 4)
            for phase in (1, 2):
                if phase == 2:
                    w.later("s_taken", 2 * NT * KT * B)
                    split_weights(4, 2, 0)
                    dve.memset(QS[:, :, :], 0.0)
                    dve.memset(KS[:, :, :], 0.0)
                set_state()
                if phase == 2:
                    for n in range(1, 6):
                        front(phase, n)
                for n in range(6, 13):
                    front(phase, n)

                def batch(b, looped):
                    turned_copy(XT1)
                    if looped:
                        second_norm_stats()
                    project(phase, looped)
                    if looped:
                        turned_copy(XT2)
                        place[0] += 4
                    if phase == 1:
                        sums()
                        for e in range(KT):
                            for c in range(NT):
                                for g in range(2):
                                    mask_unit(2 * (NT * e + c) + g)
                                if c >= 2:
                                    take_chunk(e, c - 2)
                                front(phase, NT * e + c)
                                if looped and (NT * e + c) in (5, 8, 11, 14):
                                    gates((NT * e + c - 5) // 3)
                            for c in (NT - 2, NT - 1):
                                dve.wait_ge(sem["pv_done"], w.next("pv_done", 2))
                                dve.sem_inc(held, 1)
                                take_chunk(e, c)
                    else:
                        for n in range(2):
                            for u in range(NU):
                                max_unit(n, u)
                        for n in range(H):
                            for u in range(NU):
                                if n + 2 < H:
                                    max_unit(n + 2, u)
                                if u - 1 in by_dve(n):
                                    low_unit(n, u - 1)
                                if u == LAG + 1 and n >= 1:
                                    take_head(n - 1)
                            w.later("t_taken", NU - 1 - by_dve(n)[-1])
                            front(phase, n)
                            if looped and n in (3, 6, 9, 12):
                                gates(n // 3 - 1)
                        take_head(H - 1)
                        w.later("max_parts", 2)
                    dve.wait_ge(sem["head_taken"], w.next("head_taken", H))
                    dve.tensor_tensor(OL[:, :, P:2 * P], ON[:, :, P:2 * P], flat(ON[:, :, :]).bitcast(BF16).rearrange(
                        "p (n d) -> p n d", n=NT)[:, :, 2 * P + 1:4 * P:2], ALU.subtract
                                      ).then_inc(sem["split_o_upper"], 1)
                    turned_copy(XT1)
                    for c in range(4):
                        if c == 0:
                            if phase == 1:
                                dve.wait_ge(sem["xr_in"], w.next("xr_in", 16))
                            else:
                                dve.wait_ge(sem["xr_bias"], w.next("xr_bias"))
                        dve.tensor_tensor(pair(XR, c), taken_bank(), pair(XR, c), ALU.add
                                          ).then_inc(sem["xr_add"], 1)

                run(dve, w, phase, batch)
                second_norm_stats()
                second_norm()
                turned_copy(XT2)
                place[0] += 16
                for group in range(4):
                    gates(group)
                for c in range(4):
                    bank = taken_bank()
                    for n in range(2):
                        i = dve.tensor_tensor(CU[:, 2 * c + n, :], bank[:, n * D:(n + 1) * D],
                                              ROW[:, 2, :], ALU.add)
                    i.then_inc(sem["cu"], 1)
                dve.wait_ge(sem["cu"], w.next("cu", 4))
            for b in range(B + 1):
                if b < B:
                    dve.wait_ge(sem[f"fin_in{b % 2}"], w.next(f"fin_in{b % 2}", 32))
                    a = flat((XN, ON)[b % 2][:, :, :])
                    dve.tensor_tensor(a, a, flat(CU[:, :, :]), ALU.add).then_inc(sem["fin_sum"], 1)
                if b >= 1:
                    dve.wait_ge(sem["fin_tanh"], w.next("fin_tanh"))
                    s = (b - 1) % 2
                    a = flat((XA, XR)[s][:, :, :])
                    dve.tensor_tensor(a, a, flat((XN, ON)[s][:, :, :]), ALU.add).then_inc(sem["fin_done"], 1)

        @block.gpsimd
        def _(pool):
            held = sem["held_pool"]
            w = Counts()

            def lows(normed, done, src, dst, chunks=range(4)):
                for c in chunks:
                    pool.wait_ge(sem[normed], w.next(normed))
                    pool.tensor_tensor(pair(dst, c), pair(src, c), top(pair(src, c)), ALU.subtract
                                       ).then_inc(sem[done], 1)

            def lower_heads_low():
                pool.wait_ge(sem["head_taken"], w.next("head_taken", GH))
                pool.tensor_tensor(OL[:, :, 0:P], ON[:, :, 0:P], flat(ON[:, :, :]).bitcast(BF16).rearrange(
                    "p (n d) -> p n d", n=NT)[:, :, 1:2 * P:2], ALU.subtract).then_inc(sem["split_o"], 1)
                w.later("head_taken", GH)

            def state_low():
                pool.wait_ge(sem["state_high"], w.next("state_high"))
                pool.tensor_tensor(flat(CP[1][:, :, :]), flat(CS[:, :, :]), flat(CP[0][:, :, :]), ALU.subtract
                                   ).then_inc(sem["state_split"], 1)

            def split_max(n):
                pool.wait_ge(sem["max_ready"], w.next("max_ready"))
                pool.sem_inc(held, 1)
                if n >= 1:
                    pool.wait_ge(sem["max_turned"], w.next("max_turned"))
                    pool.sem_inc(held, 1)
                m = MP[:, n % 2, 0:NT]
                pool.tensor_copy(MB[:, 0, :], m).then_inc(sem["pool_step"], 1)
                pool.wait_ge(sem["pool_step"], w.next("pool_step"))
                pool.tensor_tensor(MB[:, 1, :], m, MB[:, 0, :], ALU.subtract).then_inc(sem["max_parts"], 1)

            def low_unit(slots, k, taken, events):
                pool.wait_ge(sem[taken], w.next(taken, events))
                s = k % slots
                pool.tensor_tensor(PL[:, s, :], PR[:, s, :], top(PR[:, s, :]), ALU.subtract
                                   ).then_inc(sem["low_pool"], 1)

            pool.wait_ge(sem["const_ready"], w.next("const_ready"))
            pool.wait_ge(sem["const_stored"], w.next("const_stored", 64))
            for phase in (1, 2):
                if phase == 2:
                    w.later("qk_raw", 8 * B)
                    w.later("xr_in", 16 * B)
                lows("normed1", "split1", XN, XL)

                def batch(b, looped):
                    for r in range(4):
                        if r == 2 and looped:
                            lows("normed2", "split2", ON, OL)
                        if phase == 1:
                            pool.wait_ge(sem["qk_high"], w.next("qk_high"))
                        else:
                            pool.wait_ge(sem["qk_raw"], w.next("qk_raw", 2))
                        high, low = parts_of(phase, r)
                        pool.tensor_tensor(low, QK[:, r % 2, :], high, ALU.subtract).then_inc(sem["qkp_ready"], 1)
                    if phase == 1:
                        for k in range(2 * NT * KT):
                            low_unit(SLOTS1, k, "s_taken", 1)
                            if k >= 22 and k % 2 == 0 and k < 30:
                                lows("normed1", "split1", XN, XL, [(k - 22) // 2])
                            if k == 20:
                                lower_heads_low()
                        if looped:
                            state_low()
                    else:
                        split_max(0)
                        split_max(1)
                        for n in range(H):
                            for u in range(NU):
                                if u not in by_dve(n):
                                    low_unit(SLOTS, NU * n + u, "t_taken", 2 if u - 1 in by_dve(n) else 1)
                                if u == 0 and 1 <= n and n + 1 < H:
                                    split_max(n + 1)
                            if n == 14 and looped:
                                state_low()
                            if n == 8:
                                pool.wait_ge(sem["xr_in"], w.next("xr_in", 16))
                                for m in range(NT):
                                    i = pool.tensor_tensor(XR[:, m, :], XR[:, m, :], ROW[:, 1, :], ALU.add)
                                i.then_inc(sem["xr_bias"], 1)
                            if n == 9:
                                lower_heads_low()
                            if 10 <= n <= 13:
                                lows("normed1", "split1", XN, XL, [n - 10])
                        w.later("max_turned", 1)

                run(pool, w, phase, batch)
                lows("normed2", "split2", ON, OL)
                state_low()


_INS = ["L0_attn_a_x", "L0_attn_a_Wq", "L0_attn_a_Wk", "L0_attn_a_Wv", "L0_attn_a_Wo",
        "L0_attn_b_Wq", "L0_attn_b_bq", "L0_attn_b_Wk", "L0_attn_b_bk", "L0_attn_b_Wv", "L0_attn_b_bv",
        "L0_attn_b_Wo", "L0_attn_b_bo", "L0_ffn_wf", "L0_ffn_uf", "L0_ffn_bf", "L0_ffn_wi", "L0_ffn_ui",
        "L0_ffn_bi", "L0_ffn_wc", "L0_ffn_uc", "L0_ffn_bc", "L0_ffn_wo", "L0_ffn_uo", "L0_ffn_bo", "L0_ffn_in_c"]


def kernel(**inputs):
    import numpy as np
    import concourse.bacc as bacc
    from concourse.bass_utils import run_bass_kernel_spmd as launch

    a = {n: np.asarray(inputs[n]) for n in _INS}
    turned = [a[f"L0_attn_a_{n}"].T for n in ("Wq", "Wk", "Wv", "Wo")]
    plain = [a[f"L0_attn_b_{n}"] for n in ("Wq", "Wk", "Wv", "Wo")]
    ffn = [a[f"L0_ffn_{n}"].T for n in ("wf", "uf", "wi", "ui", "wc", "uc", "wo", "uo")]
    col = [a[n].reshape(KT, P).T for n in ("L0_attn_b_bq", "L0_attn_b_bk", "L0_ffn_bf", "L0_ffn_bi", "L0_ffn_bc",
                                           "L0_ffn_in_c")]
    row = [a[n] for n in ("L0_attn_b_bv", "L0_attn_b_bo", "L0_ffn_bo")]
    slope = np.float32(2.0 ** (-8.0 / H)) ** np.arange(1, H + 1, dtype=np.float32)
    bias = slope[:, None] * (np.arange(T, dtype=np.float32) - T // 2)
    parts = []
    for _ in range(3):
        top = ((bias.view(np.uint32) + np.uint32(0x8000)) & np.uint32(0xFFFF0000)).view(np.float32)
        parts.append(top)
        bias = bias - top
    key_rows = np.stack(parts, axis=1).reshape(3 * H, T)
    p, c = np.arange(P)[:, None], np.arange(P)[None, :]
    masks = np.zeros((P, 4 * P + GH * HV), np.float32)
    masks[:, 0:P] = np.where(p == c, 1.0, 0.0)
    masks[:, P:2 * P] = np.where(p > c, NEG, 0.0)
    masks[:, 2 * P:3 * P] = np.where(c > p, NEG, 0.0)
    masks[:, 3 * P:4 * P] = np.where(p <= c, 1.0, 0.0)
    masks[:, 4 * P:] = np.where(p // HD == np.arange(GH * HV)[None, :] // HV, 1.0, 0.0)
    arrays = {
        "in_x": np.ascontiguousarray(a["L0_attn_a_x"]),
        "in_weights": np.ascontiguousarray(np.stack(turned + plain + ffn)),
        "in_cols": np.ascontiguousarray(np.concatenate(col, axis=1)),
        "in_rows": np.ascontiguousarray(np.stack(row)),
        "in_key_rows": np.ascontiguousarray(key_rows),
        "in_masks": masks,
    }
    nc = bacc.Bacc("TRN2", target_bir_lowering=False, num_devices=1)
    args = [nc.dram_tensor(n, v.shape, mybir.dt.from_np(v.dtype), kind="ExternalInput").ap()
            for n, v in arrays.items()]
    args.append(nc.dram_tensor("out_0", (B, T, D), F32, kind="ExternalOutput").ap())
    mixer_kernel(nc, *args)
    r = launch(nc, [arrays], core_ids=[0])
    return r.results[0]["out_0"]
```
